# Optimizing a Trainium2 kernel written in Bass

```python
import numpy as np
import jax
import jax.numpy as jnp

def _softmax(x, axis=-1):
    return jax.nn.softmax(x, axis=axis)

def _gelu(x):
    return jax.nn.gelu(x, approximate=True)

def _silu(x):
    return jax.nn.silu(x)

def _sigmoid(x):
    return jax.nn.sigmoid(x)

def _layernorm(x, axis=-1, eps=1e-05):
    m = jnp.mean(x, axis=axis, keepdims=True)
    v = jnp.var(x, axis=axis, keepdims=True)
    return (x - m) / jnp.sqrt(v + eps)

def _scatter_add(tgt, idx, src, axis=0):
    return tgt.at[idx].add(src)

def _segment_sum(src, seg, n):
    return jax.ops.segment_sum(src, seg, n)
kernel_name = 'mk_decoder_preln_d1_seqx_r8_67efe1'

def setup_inputs(seed: int=0):
    np.random.seed(seed)
    _w = jnp.asarray

    def _rec_inputs():
        import jax
        import jax.numpy as jnp
        _rk = jax.random.key(seed)
        x = -0.0002928 + 1 * jax.random.normal(jax.random.fold_in(_rk, 1), (8, 256, 128), jnp.float32)
        _lenS = 256 - jax.random.randint(jax.random.fold_in(_rk, 7), (8,), 0, max(1, 256 // 4) + 1, jnp.int32)
        _lenS2 = 256 - jax.random.randint(jax.random.fold_in(_rk, 8), (8,), 0, max(1, 256 // 4) + 1, jnp.int32)
        _ctx_1024P = jax.random.normal(jax.random.fold_in(_rk, 11), (8, 16, 128), jnp.float32)
        _ctx_1024c = jax.random.dirichlet(jax.random.fold_in(_rk, 511), 0.3 * jnp.ones((16,), jnp.float32), (8, 256))
        _ctx_1024t = jnp.einsum('bsk,bkd->bsd', _ctx_1024c, _ctx_1024P)
        _ctx_1024t = _ctx_1024t * jax.lax.rsqrt(jnp.mean(jnp.square(_ctx_1024t)) + 1e-12) * 0.953939
        ctx_1024 = -1.39393e-06 + 0.999914 * (_ctx_1024t + 0.3 * jax.random.normal(jax.random.fold_in(_rk, 611), (8, 256, 128), jnp.float32))
        _validS = jnp.arange(256)[None, :] < _lenS[:, None]
        _validS2 = jnp.arange(256)[None, :] < _lenS2[:, None]
        _causal = jnp.tril(jnp.ones((256, 256), dtype=bool))
        mask_SxS2_ff0 = jnp.where(jnp.ones((256, 256), dtype=bool), 0.0, -1000000000.0).astype(jnp.float32)
        return (x, ctx_1024, mask_SxS2_ff0)
    x, ctx_1024, mask_SxS2_ff0 = _rec_inputs()

    def _L0_attn_setup():
        import jax, jax.numpy as jnp
        import numpy as np
        B, S, D, H = (2, 256, 128, 16)
        HD = D // H
        key = jax.random.key(seed)
        ks = jax.random.split(key, 5)
        x = jax.random.normal(ks[0], (B, S, D), dtype=jnp.float32)
        qk_w = jax.random.normal(ks[1], (D, 2 * D), dtype=jnp.float32) * 0.02
        qk_b = jnp.zeros((2 * D,), dtype=jnp.float32)
        v_w = jax.random.normal(ks[2], (D, D), dtype=jnp.float32) * 0.02
        cproj_w = jax.random.normal(ks[3], (D, D), dtype=jnp.float32) * 0.02
        resid_gain = jnp.ones((1, H, 1, 1), dtype=jnp.float32)
        skip_gain = jnp.ones((1, H, 1, 1), dtype=jnp.float32)
        centre_gain = jnp.ones((1, H, 1, 1), dtype=jnp.float32)
        return {'x': x, 'qk_w': qk_w, 'qk_b': qk_b, 'v_w': v_w, 'cproj_w': cproj_w, 'resid_gain': resid_gain, 'skip_gain': skip_gain, 'centre_gain': centre_gain}
    _L0_attn_all = _L0_attn_setup()
    _L0_attn_in = {k: v for k, v in _L0_attn_all.items() if k in ('qk_w', 'qk_b', 'v_w', 'cproj_w', 'resid_gain', 'skip_gain', 'centre_gain')}
    del _L0_attn_all

    def _L0_xattn_setup():
        import jax, jax.numpy as jnp
        import numpy as np
        HIDDEN = 128
        NUM_HEADS = 16
        HEAD_DIM = HIDDEN // NUM_HEADS
        GRID_SIZE = 5
        SPLINE_ORDER = 3
        NUM_COEF = GRID_SIZE + SPLINE_ORDER

        def make_grid(in_features):
            h = 2.0 / GRID_SIZE
            g = jnp.arange(-SPLINE_ORDER, GRID_SIZE + SPLINE_ORDER + 1, dtype=jnp.float32) * h - 1.0
            return jnp.broadcast_to(g, (in_features, g.shape[0]))

        def b_splines(x, grid):
            x = x[..., None]
            bases = ((x >= grid[:, :-1]) & (x < grid[:, 1:])).astype(x.dtype)
            for k in range(1, SPLINE_ORDER + 1):
                left = (x - grid[:, :-(k + 1)]) / (grid[:, k:-1] - grid[:, :-(k + 1)])
                right = (grid[:, k + 1:] - x) / (grid[:, k + 1:] - grid[:, 1:-k])
                bases = left * bases[..., :-1] + right * bases[..., 1:]
            return bases

        def kan_linear(x, base_w, spline_w, spline_scaler):
            in_f = x.shape[-1]
            x2 = x.reshape(-1, in_f)
            base = jax.nn.silu(x2) @ base_w.T
            bases = b_splines(x2, make_grid(in_f))
            sw = spline_w * spline_scaler[..., None]
            spline = bases.reshape(x2.shape[0], -1) @ sw.reshape(sw.shape[0], -1).T
            return (base + spline).reshape(*x.shape[:-1], base_w.shape[0])

        def apply_rope(x):
            d, s = (x.shape[-1], x.shape[-2])
            inv_freq = 1.0 / 10000.0 ** (jnp.arange(0, d, 2, dtype=jnp.float32) / d)
            freqs = jnp.arange(s, dtype=jnp.float32)[:, None] * inv_freq[None, :]
            cos = jnp.repeat(jnp.cos(freqs), 2, axis=-1)
            sin = jnp.repeat(jnp.sin(freqs), 2, axis=-1)
            x1, x2 = (x[..., 0::2], x[..., 1::2])
            rot = jnp.stack((-x2, x1), axis=-1).reshape(x.shape)
            return x * cos + rot * sin
        key = jax.random.key(seed)
        ks = jax.random.split(key, 10)
        B, S, H = (2, 256, HIDDEN)
        H3 = 3 * H
        scale = 0.02
        return {'q': jax.random.normal(ks[0], (B, S, H), jnp.float32), 'k': jax.random.normal(ks[1], (B, S, H), jnp.float32), 'v': jax.random.normal(ks[2], (B, S, H), jnp.float32), 'attn_mask': jnp.zeros((S, S), jnp.float32), 'qkv_base_w': jax.random.normal(ks[3], (H3, H3), jnp.float32) * scale, 'qkv_spline_w': jax.random.normal(ks[4], (H3, H3, NUM_COEF), jnp.float32) * scale, 'qkv_scaler': jnp.ones((H3, H3), jnp.float32), 'out_base_w': jax.random.normal(ks[5], (H, H), jnp.float32) * scale, 'out_spline_w': jax.random.normal(ks[6], (H, H, NUM_COEF), jnp.float32) * scale, 'out_scaler': jnp.ones((H, H), jnp.float32)}
    _L0_xattn_all = _L0_xattn_setup()
    _L0_xattn_in = {k: v for k, v in _L0_xattn_all.items() if k in ('qkv_base_w', 'qkv_spline_w', 'qkv_scaler', 'out_base_w', 'out_spline_w', 'out_scaler')}
    del _L0_xattn_all

    def _L0_ffn_setup():
        import jax, jax.numpy as jnp
        import numpy as np
        DIM = 128
        HIDDEN = 384
        SCALE = 1.0 / 127.0

        def _dequant(w_int, dtype):
            return w_int.astype(dtype) * jnp.asarray(SCALE, dtype)
        key = jax.random.key(seed)
        k_x, k_g, k_u, k_d = jax.random.split(key, 4)
        x = jax.random.normal(k_x, (4, 256, DIM), dtype=jnp.float32)
        w_gate = jax.random.randint(k_g, (HIDDEN, DIM), -127, 128, dtype=jnp.int32)
        w_up = jax.random.randint(k_u, (HIDDEN, DIM), -127, 128, dtype=jnp.int32)
        w_down = jax.random.randint(k_d, (DIM, HIDDEN), -127, 128, dtype=jnp.int32)
        return {'x': x, 'w_gate': w_gate, 'w_up': w_up, 'w_down': w_down}
    _L0_ffn_all = _L0_ffn_setup()
    _L0_ffn_in = {k: v for k, v in _L0_ffn_all.items() if k in ('w_gate', 'w_up', 'w_down')}
    del _L0_ffn_all
    return {'x': x, 'ctx_1024': ctx_1024, 'mask_SxS2_ff0': mask_SxS2_ff0, 'L0_attn_qk_w': _L0_attn_in['qk_w'], 'L0_attn_qk_b': _L0_attn_in['qk_b'], 'L0_attn_v_w': _L0_attn_in['v_w'], 'L0_attn_cproj_w': _L0_attn_in['cproj_w'], 'L0_attn_resid_gain': _L0_attn_in['resid_gain'], 'L0_attn_skip_gain': _L0_attn_in['skip_gain'], 'L0_attn_centre_gain': _L0_attn_in['centre_gain'], 'L0_xattn_qkv_base_w': _L0_xattn_in['qkv_base_w'], 'L0_xattn_qkv_spline_w': _L0_xattn_in['qkv_spline_w'], 'L0_xattn_qkv_scaler': _L0_xattn_in['qkv_scaler'], 'L0_xattn_out_base_w': _L0_xattn_in['out_base_w'], 'L0_xattn_out_spline_w': _L0_xattn_in['out_spline_w'], 'L0_xattn_out_scaler': _L0_xattn_in['out_scaler'], 'L0_ffn_w_gate': _L0_ffn_in['w_gate'], 'L0_ffn_w_up': _L0_ffn_in['w_up'], 'L0_ffn_w_down': _L0_ffn_in['w_down']}

def reference(x, ctx_1024, mask_SxS2_ff0, L0_attn_qk_w, L0_attn_qk_b, L0_attn_v_w, L0_attn_cproj_w, L0_attn_resid_gain, L0_attn_skip_gain, L0_attn_centre_gain, L0_xattn_qkv_base_w, L0_xattn_qkv_spline_w, L0_xattn_qkv_scaler, L0_xattn_out_base_w, L0_xattn_out_spline_w, L0_xattn_out_scaler, L0_ffn_w_gate, L0_ffn_w_up, L0_ffn_w_down):
    import jax
    import jax.numpy as jnp

    def _L0_attn_ref(x, qk_w, qk_b, v_w, cproj_w, resid_gain, skip_gain, centre_gain):
        import jax, jax.numpy as jnp
        import numpy as np
        B, S, D, H = (2, 256, 128, 16)
        HD = D // H
        b, s, d = x.shape
        h, hd = (H, d // H)
        qk = x @ qk_w + qk_b
        q, k = jnp.split(qk, 2, axis=-1)
        v = x @ v_w
        q = q.reshape(b, s, h, hd).transpose(0, 2, 1, 3)
        k = k.reshape(b, s, h, hd).transpose(0, 2, 1, 3)
        v = v.reshape(b, s, h, hd).transpose(0, 2, 1, 3)
        scores = jnp.einsum('bhqd,bhkd->bhqk', q, k) / jnp.sqrt(jnp.float32(hd))
        causal = jnp.tril(jnp.ones((s, s), dtype=bool))
        neg = jnp.finfo(scores.dtype).min
        scores = jnp.where(causal, scores, neg)
        attn = jax.nn.softmax(scores, axis=-1)
        row = jnp.arange(1, s + 1, dtype=jnp.float32)
        uniform = jnp.tril(jnp.ones((s, s), dtype=jnp.float32) / row[:, None])
        eye = jnp.eye(s, dtype=jnp.float32)
        new_attn = resid_gain * attn + skip_gain * eye[None, None] - centre_gain * uniform[None, None]
        out = jnp.einsum('bhqk,bhkd->bhqd', new_attn, v)
        out = out.transpose(0, 2, 1, 3).reshape(b, s, d)
        out = out @ cproj_w
        return out

    def _L0_xattn_ref(q, k, v, attn_mask, qkv_base_w, qkv_spline_w, qkv_scaler, out_base_w, out_spline_w, out_scaler):
        import jax, jax.numpy as jnp
        import numpy as np
        HIDDEN = 128
        NUM_HEADS = 16
        HEAD_DIM = HIDDEN // NUM_HEADS
        GRID_SIZE = 5
        SPLINE_ORDER = 3
        NUM_COEF = GRID_SIZE + SPLINE_ORDER

        def make_grid(in_features):
            h = 2.0 / GRID_SIZE
            g = jnp.arange(-SPLINE_ORDER, GRID_SIZE + SPLINE_ORDER + 1, dtype=jnp.float32) * h - 1.0
            return jnp.broadcast_to(g, (in_features, g.shape[0]))

        def b_splines(x, grid):
            x = x[..., None]
            bases = ((x >= grid[:, :-1]) & (x < grid[:, 1:])).astype(x.dtype)
            for k in range(1, SPLINE_ORDER + 1):
                left = (x - grid[:, :-(k + 1)]) / (grid[:, k:-1] - grid[:, :-(k + 1)])
                right = (grid[:, k + 1:] - x) / (grid[:, k + 1:] - grid[:, 1:-k])
                bases = left * bases[..., :-1] + right * bases[..., 1:]
            return bases

        def kan_linear(x, base_w, spline_w, spline_scaler):
            in_f = x.shape[-1]
            x2 = x.reshape(-1, in_f)
            base = jax.nn.silu(x2) @ base_w.T
            bases = b_splines(x2, make_grid(in_f))
            sw = spline_w * spline_scaler[..., None]
            spline = bases.reshape(x2.shape[0], -1) @ sw.reshape(sw.shape[0], -1).T
            return (base + spline).reshape(*x.shape[:-1], base_w.shape[0])

        def apply_rope(x):
            d, s = (x.shape[-1], x.shape[-2])
            inv_freq = 1.0 / 10000.0 ** (jnp.arange(0, d, 2, dtype=jnp.float32) / d)
            freqs = jnp.arange(s, dtype=jnp.float32)[:, None] * inv_freq[None, :]
            cos = jnp.repeat(jnp.cos(freqs), 2, axis=-1)
            sin = jnp.repeat(jnp.sin(freqs), 2, axis=-1)
            x1, x2 = (x[..., 0::2], x[..., 1::2])
            rot = jnp.stack((-x2, x1), axis=-1).reshape(x.shape)
            return x * cos + rot * sin
        B, S, H = q.shape
        x = jnp.concatenate((q, k, v), axis=2)
        qkv = kan_linear(x, qkv_base_w, qkv_spline_w, qkv_scaler)
        qkv = qkv.reshape(B, S, NUM_HEADS, 3 * HEAD_DIM).transpose(0, 2, 1, 3)
        queries, keys, values = jnp.split(qkv, 3, axis=-1)
        queries = apply_rope(queries)
        keys = apply_rope(keys)
        scores = jnp.einsum('bhqd,bhkd->bhqk', queries, keys) / HEAD_DIM ** 0.5 + attn_mask
        attention = jax.nn.softmax(scores, axis=-1)
        context = jnp.einsum('bhqk,bhkd->bhqd', attention, values)
        context = context.transpose(0, 2, 1, 3).reshape(B, S, H)
        return kan_linear(context, out_base_w, out_spline_w, out_scaler)

    def _L0_ffn_ref(x, w_gate, w_up, w_down):
        import jax, jax.numpy as jnp
        import numpy as np
        DIM = 128
        HIDDEN = 384
        SCALE = 1.0 / 127.0

        def _dequant(w_int, dtype):
            return w_int.astype(dtype) * jnp.asarray(SCALE, dtype)
        wg = _dequant(w_gate, x.dtype)
        wu = _dequant(w_up, x.dtype)
        wd = _dequant(w_down, x.dtype)
        gate = jnp.einsum('bsd,hd->bsh', x, wg)
        up = jnp.einsum('bsd,hd->bsh', x, wu)
        h = jax.nn.silu(gate) * up
        return jnp.einsum('bsh,dh->bsd', h, wd)
    x = x + _L0_attn_ref(_layernorm(x, axis=-1), L0_attn_qk_w, L0_attn_qk_b, L0_attn_v_w, L0_attn_cproj_w, L0_attn_resid_gain, L0_attn_skip_gain, L0_attn_centre_gain)
    x = x + _L0_xattn_ref(_layernorm(x, axis=-1), ctx_1024, ctx_1024, mask_SxS2_ff0, L0_xattn_qkv_base_w, L0_xattn_qkv_spline_w, L0_xattn_qkv_scaler, L0_xattn_out_base_w, L0_xattn_out_spline_w, L0_xattn_out_scaler)
    x = x + _L0_ffn_ref(_layernorm(x, axis=-1), L0_ffn_w_gate, L0_ffn_w_up, L0_ffn_w_down)
    return x

_drawn_inputs = setup_inputs


def setup_inputs(seed=0):
    import zlib

    import numpy as np

    out = dict(_drawn_inputs(seed))
    spreads = {'mask_SxS2_ff0': (0.0, 2.0),
     'L0_attn_qk_b': (0.0, 0.8),
     'L0_attn_resid_gain': (1.0, 0.6),
     'L0_attn_skip_gain': (1.0, 0.6),
     'L0_attn_centre_gain': (1.0, 0.6),
     'L0_xattn_qkv_scaler': (1.0, 0.6),
     'L0_xattn_out_scaler': (1.0, 0.2)}
    factors = {'L0_attn_qk_w': 8.0}
    for name, (base, spread) in spreads.items():
        noise = np.random.default_rng([zlib.crc32(name.encode()), seed]).standard_normal(out[name].shape)
        drawn = base * np.exp(spread * noise) if base else spread * noise
        out[name] = jnp.asarray(drawn.astype(out[name].dtype))
    for name, factor in factors.items():
        out[name] = (out[name] * factor).astype(out[name].dtype)
    return out
```

```python
from contextlib import ExitStack

import numpy as np

import concourse.bass as bass
from concourse import mybir
from concourse.alu_op_type import AluOpType as ALU

ACT = mybir.ActivationFunctionType
F32 = mybir.dt.float32
F32R = mybir.dt.float32r
BF16 = mybir.dt.bfloat16
I32 = mybir.dt.int32
AX = mybir.AxisListType

B, S, D, H = 8, 256, 128, 16
P = 128
HD = D // H
TILES = B * S // P
QT = S // P
HL = 4
HG = H // HL
ROWS = P // HL
KROWS = 3 * HD + 2
NB = 8
KP = NB + 1
FT = 3
NEG = -1.0e30
EPS = 1e-5
H_GRID = 0.4
SCALE = 1.0 / float(np.sqrt(HD))


def constants():
    p, q = np.arange(P)[:, None], np.arange(P)[None, :]
    causal_q = np.where(q <= p, 0.0, NEG)
    causal_k = np.where(q >= p, 0.0, NEG)
    sel_hi, sel_lo_q, sel_hi_k, sel_lo_k = (np.zeros((P, HG, P)) for _ in range(4))
    for g in range(HG):
        for l in range(HL):
            for d in range(HD):
                f, r = (g * HL + l) * HD + d, l * ROWS + d
                sel_hi[f, g, r] = sel_hi[f, g, r + 2 * HD] = 1
                sel_lo_q[f, g, r + HD] = 1
                sel_hi_k[f, g, r] = sel_hi_k[f, g, r + HD] = 1
                sel_lo_k[f, g, r + 2 * HD] = 1
    rope_rot = np.zeros((P, P))
    for f in range(0, P, 2):
        rope_rot[f + 1, f] = -1
        rope_rot[f, f + 1] = 1
    inv = np.float32(1.0) / np.float32(10000.0) ** (np.arange(0, HD, 2, dtype=np.float32) / np.float32(HD))
    angle = np.arange(S, dtype=np.float32)[:, None] * inv[None, :].astype(np.float32)
    cos = np.tile(np.repeat(np.cos(angle), 2, axis=1).T, (H, 1))
    sin = np.tile(np.repeat(np.sin(angle), 2, axis=1).T, (H, 1))
    cos2 = np.concatenate([cos * SCALE, cos], axis=1)
    sin2 = np.concatenate([sin * SCALE, sin], axis=1)
    s = np.arange(S)
    uni = np.where(s[:, None] <= s[None, :], -1.0 / (s[None, :] + 1), 0.0)
    neg_uniform = uni.reshape(QT, P, S).transpose(1, 0, 2)
    ones_rows = np.zeros((P, 1))
    ones_rows[[l * ROWS + r for l in range(HL) for r in (3 * HD, 3 * HD + 1)]] = 1
    k = np.arange(4)
    abs_bias = np.tile(np.append(1.5 - k, -2.0)[None, :], (P, 1))
    parts = [("ident", np.eye(P)), ("causal_q", causal_q), ("causal_k", causal_k),
             ("sel_hi", sel_hi), ("sel_lo_q", sel_lo_q), ("sel_hi_k", sel_hi_k), ("sel_lo_k", sel_lo_k),
             ("rope_rot", rope_rot), ("cos", cos2), ("sin", sin2), ("neg_uniform", neg_uniform),
             ("ones_rows", ones_rows), ("abs_bias", abs_bias)]
    staged = ("causal_q", "causal_k", "sel_hi", "sel_lo_q", "sel_hi_k", "sel_lo_k")
    at, kept, used = {}, [[], []], [0, 0]
    for name, a in parts:
        a, which = a.reshape(P, -1).astype(np.float32), int(name in staged)
        at[name] = (used[which], used[which] + a.shape[1])
        kept[which].append(a)
        used[which] += a.shape[1]
    return at, np.concatenate(kept[0], axis=1), np.concatenate(kept[1], axis=1)


CONST_AT, CONST, CONST_STAGED = constants()


class Event:

    def __init__(self, sem, per, unit=1):
        self.sem, self.per, self.unit = sem, per, unit

    def at(self, b, n=None):
        return (b * self.per + (self.per if n is None else n)) * self.unit


def build(nc, t, out):
    with ExitStack() as ctx:
        def sb(name, shape, dt=F32):
            return ctx.enter_context(nc.sbuf_tensor(name, shape, dt))

        def psum(name, shape):
            return ctx.enter_context(nc.psum_tensor(name, shape, F32))

        def sem(name):
            return ctx.enter_context(nc.semaphore(name))

        def event(name, per=1, unit=1):
            return Event(sem(name), per, unit)

        def await_(eng, ev, b, n=None):
            eng.wait_ge(ev.sem, ev.at(b, n))

        wait_taken = sem("wait_taken")

        def take_wait(act):
            act.sem_inc(wait_taken, 1)

        const = sb("const", [P, CONST.shape[1]])

        def cst(name):
            a, z = CONST_AT[name]
            return const[:, a:z]

        ident = cst("ident")
        ident_r = sb("ident_r", [P, P], F32R)
        ident_b = sb("ident_b", [P, P], BF16)
        causal_q_b = sb("causal_q_b", [P, P], BF16)
        causal_k_b = sb("causal_k_b", [P, P], BF16)
        sel_r = sb("sel_r", [P, 4, HG, P], F32R)
        sel_q_hi, sel_q_lo, sel_k_hi, sel_k_lo = (sel_r[:, n] for n in range(4))
        xres = sb("xres", [P, TILES, D])
        cosv = cst("cos")
        sinv = cst("sin")
        neg_uniform = cst("neg_uniform").rearrange("p (k q) -> p k q", k=QT)
        ones_rows = cst("ones_rows")
        abs_bias = cst("abs_bias")
        wqk = sb("wqk", [P, 2 * D])
        wv2 = sb("wv2", [P, 2, D])
        wvs = sb("wvs", [P, D])
        wproj = sb("wproj", [P, D])
        qk_bias = sb("qk_bias", [P, 2])
        kan_w = sb("kan_w", [P, 2, KP, 3 * D])
        kan_wo = sb("kan_wo", [P, KP, D])
        w_gate = sb("w_gate", [P, FT * P])
        w_up = sb("w_up", [P, FT * P])
        w_down = sb("w_down", [P, FT, D])
        mask_q = sb("mask_q", [P, 2, QT, S], F32R)
        mask_k = sb("mask_k", [P, 2, QT, S], F32R)
        xt = sb("xt", [P, 2, TILES * P])
        stats = sb("stats", [P, TILES, 6])
        mv = sb("mv", [P, TILES, 2])
        rstd = sb("rstd", [P, TILES])
        rstd_a = sb("rstd_a", [P, TILES])
        rstd_b = sb("rstd_b", [P, TILES])
        eps_col = sb("eps_col", [P, 1])

        bank = [psum(f"bank{n}", [P, 512]) for n in range(2)]
        wide = [psum(f"wide{n}", [P, 1024]) for n in range(2)]
        bank_pv = psum("bank_pv", [P, 512])
        bank_ms = psum("bank_ms", [P, 512])
        banks = [bank[0][:], bank[1][:], wide[0][:, 0:512], wide[0][:, 512:1024],
                 wide[1][:, 0:512], wide[1][:, 512:1024], bank_pv[:], bank_ms[:]]

        class Norm:

            def __init__(self, name):
                self.done, self.root = sem(name + "_done"), sem(name + "_root")

            def moments(self, dve):
                for n in range(TILES):
                    last = nc.vector.bn_stats(stats[:, n, :], xres[:, n, :])
                last.then_inc(self.done, 1)
                dve.wait_ge(self.done, 1)
                for n in range(TILES):
                    last = nc.vector.bn_aggr(mv[:, n, :], stats[:, n, :])
                last.then_inc(self.done, 1)

            def square_root(self, act):
                act.wait_ge(self.done, 2)
                nc.scalar.activation(rstd_a[:], mv[:, :, 1], ACT.Sqrt, bias=eps_col[:, 0:1]).then_inc(self.root, 1)

            def reciprocal_root(self, dve):
                dve.wait_ge(self.root, 1)
                nc.vector.reciprocal(rstd[:], rstd_a[:]).then_inc(self.done, 1)
                dve.wait_ge(self.done, 3)
                nc.vector.tensor_tensor(rstd_b[:], rstd[:], rstd[:], ALU.mult).then_inc(self.done, 1)
                dve.wait_ge(self.done, 4)
                nc.vector.scalar_tensor_tensor(out=rstd_b[:], in0=mv[:, :, 1], scalar=EPS, in1=rstd_b[:],
                                               op0=ALU.add, op1=ALU.mult).then_inc(self.done, 1)
                dve.wait_ge(self.done, 5)
                nc.vector.tensor_scalar(rstd_b[:], rstd_b[:], -0.5, 1.5, ALU.mult, ALU.add).then_inc(self.done, 1)
                dve.wait_ge(self.done, 6)
                nc.vector.tensor_tensor(rstd[:], rstd[:], rstd_b[:], ALU.mult).then_inc(self.done, 1)

        with ExitStack() as sctx:
            def ssb(name, shape, dt=F32):
                return sctx.enter_context(nc.sbuf_tensor(name, shape, dt))

            staged = ssb("staged", [P, CONST_STAGED.shape[1]])

            def stg(name):
                a, z = CONST_AT[name]
                return staged[:, a:z]

            spl = ssb("spl", [P, 3, 3 * D * NB])
            base = ssb("base", [P, 3, 3 * D])
            scaler = ssb("scaler", [P, 3, 3 * D])
            splo = ssb("splo", [P, D * NB])
            baseo = ssb("baseo", [P, D])
            scalero = ssb("scalero", [P, D])
            wint = ssb("wint", [P, 3, FT * P], I32)
            wflt = ssb("wflt", [P, 3, FT * P])
            gains = ssb("gains", [P, 3, H])
            vw = ssb("vw", [P, D])
            mask_n = ssb("mask_n", [P, QT, S])
            ctx_n = ssb("ctx_n", [P, TILES, D])
            maskt = ssb("maskt", [P, QT, S])

            ld = {n: sem("ld_" + n) for n in ("const", "x", "attn", "ffn", "mask", "ctx", "base", "out")}
            ld_spl = [sem(f"ld_spl{r}") for r in range(3)]
            pool_w = sem("pool_w")
            dve_w = sem("dve_w")
            norm1 = Norm("norm1")
            ready = sem("ready")
            pe_tr = sem("pe_tr")
            evac_act = sem("evac_act")
            evac_dve = sem("evac_dve")

            def turns():
                for r4 in range(TILES // 4):
                    yield ([ctx_n[:, 4 * r4 + i, :] for i in range(4)], (ld["ctx"], 16),
                           xt[:, 1, 512 * r4:512 * (r4 + 1)], None)
                yield ([mask_n[:, qt, kt * P:(kt + 1) * P] for kt in range(QT) for qt in range(QT)],
                       (ld["mask"], 16), maskt[:].rearrange("p k q -> p (k q)"), None)
                for n, dst in ((0, w_gate), (1, w_up)):
                    yield ([wflt[:, n, r * P:(r + 1) * P] for r in range(FT)], (dve_w, 1), dst[:], None)
                yield ([wflt[:, 2, r * P:(r + 1) * P] for r in range(FT)], (dve_w, 1),
                       w_down[:].rearrange("p r d -> p (r d)"), None)
                for c0 in (0, 4):
                    yield ([splo[:, c:D * NB:NB] for c in range(c0, c0 + 4)], (dve_w, 2),
                           kan_wo[:, c0:c0 + 4, :].rearrange("p c d -> p (c d)"), None)
                yield ([baseo[:]], (ld["out"], 48), kan_wo[:, NB, :], "half")
                for s in range(2):
                    yield ([base[:, r, s * P:(s + 1) * P] for r in range(3)], (pool_w, 1), kan_w[:, s, NB, :], "half features")
                for s in range(2):
                    for c in range(NB):
                        yield ([spl[:, r, s * P * NB + c:(s + 1) * P * NB:NB] for r in range(3)], (dve_w, 8),
                               kan_w[:, s, c, :], "features")

            jobs = list(turns())

            def evacuate(eng, odd):
                for n, (ins, _, dst, order) in enumerate(jobs):
                    if n % 2 != odd:
                        continue
                    src = banks[n % 8][:, 0:P * len(ins)]
                    half = 0.5 if order and "half" in order else 1.0
                    if order and "features" in order:
                        src = src.rearrange("p (h s d) -> p s h d", s=3, d=HD)
                        dst = dst.rearrange("p (s h d) -> p s h d", s=3, d=HD)
                    eng.wait_ge(pe_tr, n + 1)
                    if odd:
                        nc.vector.tensor_scalar(dst, src, half, None, ALU.mult).then_inc(evac_dve, 1)
                    else:
                        nc.scalar.activation(dst, src, ACT.Copy, scale=half).then_inc(evac_act, 1)

            with nc.Block() as block:
                @block.sync
                def _(sp):
                    sp.dma_start(const[:], t["const"]).then_inc(ld["const"], 16)
                    sp.dma_start(staged[:], t["const_staged"]).then_inc(ld["const"], 16)
                    sp.dma_start(base[:], t["L0_xattn_qkv_base_w"].rearrange("(r p) i -> p r i", p=P)).then_inc(ld["base"], 16)
                    sp.dma_start(scaler[:], t["L0_xattn_qkv_scaler"].rearrange("(r p) i -> p r i", p=P)).then_inc(ld["base"], 16)
                    for r in range(3):
                        sp.dma_start(spl[:, r, :], t["L0_xattn_qkv_spline_w"][r * P:(r + 1) * P].rearrange("p i c -> p (i c)"),
                                     ).then_inc(ld_spl[r], 16)
                    sp.dma_start(splo[:], t["L0_xattn_out_spline_w"].rearrange("o i c -> o (i c)")).then_inc(ld["out"], 16)
                    sp.dma_start(baseo[:], t["L0_xattn_out_base_w"]).then_inc(ld["out"], 16)
                    sp.dma_start(scalero[:], t["L0_xattn_out_scaler"]).then_inc(ld["out"], 16)

                @block.scalar
                def _(act):
                    act.dma_start(xres[:], t["x"].rearrange("b (t p) d -> p (b t) d", p=P)).then_inc(ld["x"], 16)
                    act.dma_start(ctx_n[:], t["ctx_1024"].rearrange("b (t p) d -> p (b t) d", p=P)).then_inc(ld["ctx"], 16)
                    act.dma_start(mask_n[:], t["mask_SxS2_ff0"].rearrange("(t p) k -> p t k", p=P)).then_inc(ld["mask"], 16)
                    act.dma_start(wint[:, 0, :].rearrange("p (r d) -> p r d", r=FT), t["L0_ffn_w_gate"].rearrange("(r p) d -> p r d", p=P)).then_inc(ld["ffn"], 16)
                    act.dma_start(wint[:, 1, :].rearrange("p (r d) -> p r d", r=FT), t["L0_ffn_w_up"].rearrange("(r p) d -> p r d", p=P)).then_inc(ld["ffn"], 16)
                    act.dma_start(wint[:, 2, :], t["L0_ffn_w_down"]).then_inc(ld["ffn"], 16)
                    evacuate(act, 0)
                    norm1.square_root(act)

                @block.gpsimd
                def _(pool):
                    names = ("resid", "centre", "skip")
                    for n, g in enumerate(names):
                        pool.dma_start(gains[:, n, :], t[f"L0_attn_{g}_gain"].rearrange("a h b c -> (a b c h)").partition_broadcast(P)).then_inc(ld["attn"], 16)
                    pool.dma_start(vw[:], t["L0_attn_v_w"]).then_inc(ld["attn"], 16)
                    pool.dma_start(wqk[:], t["L0_attn_qk_w"]).then_inc(ld["attn"], 16)
                    pool.dma_start(wproj[:], t["L0_attn_cproj_w"]).then_inc(ld["attn"], 16)
                    for s in range(2):
                        pool.dma_start(qk_bias[:, s:s + 1], t["L0_attn_qk_b"][s * P:(s + 1) * P].rearrange("(p o) -> p o", o=1)).then_inc(ld["attn"], 16)
                    pool.wait_ge(ld["base"], 32)
                    nc.gpsimd.tensor_tensor(base[:, :, P:2 * P], base[:, :, P:2 * P], base[:, :, 2 * P:3 * P], ALU.add).then_inc(pool_w, 1)

                @block.tensor
                def _(pe):
                    pe.wait_ge(ld["const"], 32)
                    for n, (ins, (s, v), _, _) in enumerate(jobs):
                        pe.wait_ge(s, v)
                        if n >= 8:
                            pe.wait_ge(evac_dve if n % 2 else evac_act, (n - 8) // 2 + 1)
                        for i, a in enumerate(ins):
                            last = nc.tensor.transpose(banks[n % 8][:, i * P:(i + 1) * P], a, ident)
                        last.then_inc(pe_tr, 1)

                @block.vector
                def _(dve):
                    nc.vector.memset(eps_col[:], EPS)
                    dve.wait_ge(ld["ffn"], 48)
                    nc.vector.tensor_scalar(wflt[:], wint[:], float(np.float32(1.0 / 127.0)), None, ALU.mult).then_inc(dve_w, 1)
                    dve.wait_ge(ld["out"], 48)
                    nc.vector.scalar_tensor_tensor(out=splo[:].rearrange("p (i c) -> p i c", c=NB),
                                                   in0=splo[:].rearrange("p (i c) -> p i c", c=NB), scalar=1.0 / 6.0,
                                                   in1=scalero[:].unsqueeze(2).broadcast_to([P, D, NB]),
                                                   op0=ALU.mult, op1=ALU.mult).then_inc(dve_w, 1)
                    dve.wait_ge(ld["x"], 16)
                    norm1.moments(dve)
                    dve.wait_ge(ld["base"], 32)
                    for r in range(3):
                        dve.wait_ge(ld_spl[r], 16)
                        v = spl[:, r, :].rearrange("p (i c) -> p i c", c=NB)
                        nc.vector.scalar_tensor_tensor(out=v, in0=v, scalar=1.0 / 6.0,
                                                       in1=scaler[:, r, :].unsqueeze(2).broadcast_to([P, 3 * D, NB]),
                                                       op0=ALU.mult, op1=ALU.mult).then_inc(dve_w, 1)
                    for r in range(3):
                        dve.wait_ge(dve_w, 3 + r)
                        a, b, c = P * NB, 2 * P * NB, 3 * P * NB
                        nc.vector.tensor_tensor(spl[:, r, a:b], spl[:, r, a:b], spl[:, r, b:c], ALU.add).then_inc(dve_w, 1)
                    dve.wait_ge(ld["const"], 32)
                    nc.vector.tensor_copy(ident_r[:], ident)
                    nc.vector.tensor_copy(ident_b[:], ident)
                    nc.vector.tensor_copy(causal_q_b[:], stg("causal_q"))
                    nc.vector.tensor_copy(causal_k_b[:], stg("causal_k"))
                    for n, name in enumerate(("sel_hi", "sel_lo_q", "sel_hi_k", "sel_lo_k")):
                        nc.vector.tensor_copy(sel_r[:, n], stg(name).rearrange("p (g m) -> p g m", g=HG))
                    dve.wait_ge(ld["attn"], 16 * 8)
                    for n, dst in ((0, wv2[:, 0]), (1, wv2[:, 1]), (2, wvs[:])):
                        nc.vector.tensor_tensor(dst.rearrange("p (h d) -> p h d", d=HD), vw[:].rearrange("p (h d) -> p h d", d=HD),
                                                gains[:, n, :].unsqueeze(2).broadcast_to([P, H, HD]), ALU.mult)
                    evacuate(dve, 1)
                    dve.wait_ge(ld["mask"], 16)
                    nc.vector.tensor_copy(mask_q[:, 0], mask_n[:]).then_inc(ready, 1)
                    dve.wait_ge(evac_act, 3)
                    nc.vector.tensor_copy(mask_k[:, 0], maskt[:]).then_inc(ready, 1)
                    dve.wait_ge(ready, 2)
                    nc.vector.tensor_tensor(mask_q[:, 1], mask_n[:], mask_q[:, 0].bitcast(F32), ALU.subtract)
                    nc.vector.tensor_tensor(mask_k[:, 1], maskt[:], mask_k[:, 0].bitcast(F32), ALU.subtract)
                    norm1.reciprocal_root(dve)


        actx = ExitStack()

        def asb(name, shape, dt=F32):
            return actx.enter_context(nc.sbuf_tensor(name, shape, dt))

        qk = asb("qk", [P, 2, S])
        qk_hi = asb("qk_hi", [P, 2, S], F32R)
        qk_lo = asb("qk_lo", [P, 2, S], F32R)
        q_stack = [asb(f"q_stack{n}", [P, HG, S], F32R) for n in range(2)]
        k_stack = [asb(f"k_stack{n}", [P, HG, S], F32R) for n in range(2)]
        v_aug = [asb(f"v_aug{n}", [P, QT, H, ROWS]) for n in range(2)]
        neg_max = [asb(f"neg_max{n}", [P, QT, H]) for n in range(2)]
        max_hi = asb("max_hi", [H, S], F32R)
        max_lo = asb("max_lo", [H, S], F32R)
        probs = [asb(f"probs{n}", [P, QT * HG * S]) for n in range(2)]
        o_lane = [asb(f"o_lane{n}", [P, HL, S]) for n in range(2)]
        rsum = asb("rsum", [P, QT, H])
        o_tok = asb("o_tok", [P, QT, D])
        o_feat = asb("o_feat", [P, S])

        class Attention:

            def __init__(self, name, causal):
                self.causal = causal
                self.max_pieces = HL * (3 if causal else 4)
                self.hi = event(name + "_hi")
                self.lo = event(name + "_lo")
                self.stacked = event(name + "_stacked", 2)
                self.q_ready = event(name + "_q_ready")
                self.k_ready = event(name + "_k_ready")
                self.s_ready = event(name + "_s_ready", self.max_pieces)
                self.s_max = event(name + "_s_max", self.max_pieces)
                self.m_turned = event(name + "_m_turned")
                self.m_hi = event(name + "_m_hi")
                self.m_lo = event(name + "_m_lo")
                self.m_placed = event(name + "_m_placed", 2 * HL, 16)
                self.e_ready = event(name + "_e_ready", 2 * HL)
                self.e_done = event(name + "_e_done", 2 * HL)
                self.pv = event(name + "_pv", HL)
                self.pv_out = event(name + "_pv_out", HL)
                self.o_turned = event(name + "_o_turned", QT)
                self.o_rsum = event(name + "_o_rsum", QT)
                self.o_norm = event(name + "_o_norm", QT)

            def pe_stacks(self, pe, b, p):
                await_(pe, self.hi, b)
                await_(pe, self.lo, b)
                for s, hi, lo in ((0, sel_q_hi, sel_q_lo), (1, sel_k_hi, sel_k_lo)):
                    for g in range(HG):
                        o = wide[s][:, g * S:(g + 1) * S]
                        nc.tensor.matmul(o, hi[:, g], qk_hi[:, s], start=True, stop=False)
                        last = nc.tensor.matmul(o, lo[:, g], qk_lo[:, s], start=False, stop=True)
                    last.then_inc(self.stacked.sem, 1)

            def act_stacks(self, act, b, p):
                await_(act, self.stacked, b, 1)
                nc.scalar.activation(q_stack[p][:].rearrange("p g q -> p (g q)"), wide[0][:], ACT.Copy).then_inc(self.q_ready.sem, 1)

            def dve_stacks(self, dve, b, p):
                await_(dve, self.stacked, b, 2)
                nc.vector.tensor_scalar(k_stack[p][:].rearrange("p g q -> p (g q)"), wide[1][:], ones_rows, None,
                                        ALU.add).then_inc(self.k_ready.sem, 1)

            def max_parts(self, lane):
                if self.causal:
                    return [(0, 0, HG, P), (1, 0, 2, S), (1, 2, 2, S)]
                return [(0, 0, 2, S), (0, 2, 2, S), (1, 0, 2, S), (1, 2, 2, S)]

            def pe_max(self, pe, b, p):
                await_(pe, self.q_ready, b)
                await_(pe, self.k_ready, b)
                n = 0
                for lane in range(HL):
                    r = lane * ROWS
                    for qt, g0, ng, keys in self.max_parts(lane):
                        o = bank[n % 2][:].rearrange("p (g k) -> p g k", g=ng)
                        if n >= 2:
                            await_(pe, self.s_max, b, n - 1)
                        if self.causal:
                            nc.tensor.matmul(o[:, :, keys - P:keys], ident_b[:],
                                             causal_q_b[:].unsqueeze(1).broadcast_to([P, ng, P]),
                                             start=True, stop=False, skip_group_check=True)
                        else:
                            for half in range(2):
                                nc.tensor.matmul(o, ident_r[:], mask_q[:, half, qt].unsqueeze(1).broadcast_to([P, ng, S]),
                                                 start=(half == 0), stop=False, skip_group_check=True)
                        for g in range(ng):
                            last = nc.tensor.matmul(o[:, g, :], q_stack[p][r:r + 3 * HD, g0 + g, qt * P:(qt + 1) * P],
                                                    k_stack[p][r:r + 3 * HD, g0 + g, 0:keys],
                                                    start=False, stop=(g == ng - 1), skip_group_check=True)
                        last.then_inc(self.s_ready.sem, 1)
                        n += 1

            def dve_max(self, dve, b, p):
                n = 0
                for lane in range(HL):
                    for qt, g0, ng, keys in self.max_parts(lane):
                        await_(dve, self.s_ready, b, n + 1)
                        a = lane * HG + g0
                        nc.vector.tensor_reduce(neg_max[p][:, qt, a:a + ng], bank[n % 2][:].rearrange("p (g k) -> p g k", g=ng),
                                                AX.X, ALU.max, negate=True).then_inc(self.s_max.sem, 1)
                        n += 1

            def pe_turn_max(self, pe, b, p):
                await_(pe, self.s_max, b)
                for qt in range(QT):
                    last = nc.tensor.transpose(bank_ms[0:H, qt * P:(qt + 1) * P], neg_max[p][:, qt, :], ident)
                last.then_inc(self.m_turned.sem, 1)

            def act_split_max(self, act, b, p):
                await_(act, self.m_turned, b)
                nc.scalar.activation(max_hi[:], bank_ms[0:H, 0:S], ACT.Copy).then_inc(self.m_hi.sem, 1)

            def dve_split_max(self, dve, b, p):
                await_(dve, self.m_hi, b)
                nc.vector.tensor_tensor(max_lo[:], bank_ms[0:H, 0:S], max_hi[:].bitcast(F32), ALU.subtract).then_inc(self.m_lo.sem, 1)

            def dma_max(self, sp, b, p):
                await_(sp, self.m_lo, b)
                for half, src in ((0, max_hi), (1, max_lo)):
                    for lane in range(HL):
                        row = lane * ROWS + 3 * HD + half
                        sp.dma_start(q_stack[p][row:row + 1, :, :].bitcast(F32),
                                     src[lane * HG:(lane + 1) * HG, :].bitcast(F32)).then_inc(self.m_placed.sem, 16)

            def queries(self, kt):
                return kt * P if self.causal else 0

            def probs_of(self, lane, kt):
                n = S - self.queries(kt)
                return probs[lane % 2][:, kt * HG * S:kt * HG * S + HG * n].rearrange("p (g q) -> p g q", g=HG)

            def pe_scores(self, pe, b, p, lane):
                if lane == 0:
                    await_(pe, self.m_placed, b)
                r = lane * ROWS
                for kt in range(QT):
                    q0 = self.queries(kt)
                    n = S - q0
                    o = wide[kt][:, 0:HG * n].rearrange("p (g q) -> p g q", g=HG)
                    if lane:
                        await_(pe, self.e_done, b, 2 * lane - 1 + kt)
                    gs = 512 // n
                    for g0 in range(0, HG, gs):
                        ob = o[:, g0:g0 + gs, :]
                        if self.causal:
                            nc.tensor.matmul(ob[:, :, 0:P], ident_b[:], causal_k_b[:].unsqueeze(1).broadcast_to([P, gs, P]),
                                             start=True, stop=False, skip_group_check=True)
                        else:
                            for half in range(2):
                                nc.tensor.matmul(ob, ident_r[:], mask_k[:, half, kt].unsqueeze(1).broadcast_to([P, gs, S]),
                                                 start=(half == 0), stop=False, skip_group_check=True)
                        for g in range(g0, g0 + gs):
                            last = nc.tensor.matmul(o[:, g, :], k_stack[p][r:r + KROWS, g, kt * P:(kt + 1) * P],
                                                    q_stack[p][r:r + KROWS, g, q0:S],
                                                    start=False, stop=True, skip_group_check=True)
                    last.then_inc(self.e_ready.sem, 1)

            def act_exp(self, act, b, p, lane):
                for kt in range(QT):
                    await_(act, self.e_ready, b, 2 * lane + kt + 1)
                    if lane >= 2 and kt == 0:
                        await_(act, self.pv, b, lane - 1)
                    n = HG * (S - self.queries(kt))
                    nc.scalar.activation(self.probs_of(lane, kt).rearrange("p g q -> p (g q)"), wide[kt][:, 0:n],
                                         ACT.Exp).then_inc(self.e_done.sem, 1)

            def pe_values(self, pe, b, p, lane):
                await_(pe, self.e_done, b, 2 * lane + 2)
                if lane:
                    await_(pe, self.pv_out, b, lane)
                for kt in range(QT):
                    for g in range(HG):
                        last = nc.tensor.matmul(bank_pv[g * ROWS:(g + 1) * ROWS, self.queries(kt):S],
                                                v_aug[p][:, kt, g * HL + lane, :], self.probs_of(lane, kt)[:, g, :],
                                                start=(kt == 0), stop=(kt == QT - 1), tile_position=(0, g * ROWS),
                                                skip_group_check=True)
                last.then_inc(self.pv.sem, 1)

            def dve_values(self, dve, b, p, lane):
                await_(dve, self.pv, b, lane + 1)
                nc.vector.tensor_copy(o_lane[p][:, lane, :], bank_pv[:, 0:S]).then_inc(self.pv_out.sem, 1)

            def pe_turn_out(self, pe, b, p):
                await_(pe, self.pv_out, b)
                for qt in range(QT):
                    for lane in range(HL):
                        last = nc.tensor.transpose(bank[qt][:, lane * P:(lane + 1) * P], o_lane[p][:, lane, qt * P:(qt + 1) * P], ident)
                    last.then_inc(self.o_turned.sem, 1)

            def dve_divide(self, dve, b, p):
                for qt in range(QT):
                    await_(dve, self.o_turned, b, qt + 1)
                    o = bank[qt][:].rearrange("p (l g r) -> p l g r", l=HL, g=HG)
                    nc.vector.reciprocal(rsum[:, qt].rearrange("p (l g) -> p l g", l=HL), o[:, :, :, HD]).then_inc(self.o_rsum.sem, 1)
                for qt in range(QT):
                    await_(dve, self.o_rsum, b, qt + 1)
                    o = bank[qt][:].rearrange("p (l g r) -> p l g r", l=HL, g=HG)
                    nc.vector.tensor_tensor(o_tok[:, qt].rearrange("p (g l d) -> p l g d", g=HG, l=HL), o[:, :, :, 0:HD],
                                            rsum[:, qt].rearrange("p (l g) -> p l g", l=HL).unsqueeze(3).broadcast_to([P, HL, HG, HD]),
                                            ALU.mult).then_inc(self.o_norm.sem, 1)

        with ExitStack() as lctx:
            def lsb(name, shape, dt=F32):
                return lctx.enter_context(nc.sbuf_tensor(name, shape, dt))

            xn = lsb("xn", [P, QT, D])
            xnt = lsb("xnt", [P, S])
            v_centre = lsb("v_centre", [P, QT, D])
            v_extra = lsb("v_extra", [P, QT, D])

            att = Attention("self", causal=True)
            vones = sem("vones")
            normed = event("normed", QT)
            turned = event("turned")
            turned_out = event("turned_out")
            projected = event("projected")
            qk_out = event("qk_out", 2)
            v_done = event("v_done", QT)
            v_out = event("v_out", QT)
            vc_out = event("vc_out", QT)
            extra = event("extra")
            extra_out = event("extra_out")
            summed = event("summed")
            o_flipped = event("o_flipped")
            o_flipped_out = event("o_flipped_out")
            o_proj = event("o_proj")
            x_added = event("x_added")

            with nc.Block() as block:
                @block.gpsimd
                def _(pool):
                    for p in range(2):
                        nc.gpsimd.memset(v_aug[p][:], 0.0).then_inc(vones, 1)
                    pool.wait_ge(vones, 2)
                    for p in range(2):
                        nc.gpsimd.memset(v_aug[p][:, :, :, HD:HD + 1], 1.0).then_inc(vones, 1)
                @block.sync
                def _(sp):
                    with sp.Fori(0, B // 2) as i:
                        for p in range(2):
                            att.dma_max(sp, 2 * i + p, p)

                @block.scalar
                def _(act):
                    act.wait_ge(vones, 4)
                    with act.Fori(0, B // 2) as i:
                        for p in range(2):
                            b = 2 * i + p
                            act.wait_ge(turned.sem, b + 2)
                            nc.scalar.activation(xnt[:], bank_ms[:, 0:S], ACT.Copy).then_inc(turned_out.sem, 1)
                            await_(act, qk_out, b)
                            nc.scalar.activation(qk_hi[:].rearrange("p s q -> p (s q)"), qk[:].rearrange("p s q -> p (s q)"), ACT.Copy).then_inc(att.hi.sem, 1)
                            for qt, src in ((0, bank_pv), (1, bank[1])):
                                await_(act, vc_out, b, qt + 1)
                                nc.scalar.activation(v_aug[p][:, qt, :, 0:HD], src[:, 0:D].rearrange("p (h d) -> p h d", d=HD), ACT.Copy).then_inc(v_out.sem, 1)
                            att.act_stacks(act, b, p)
                            att.act_split_max(act, b, p)
                            for lane in range(HL):
                                att.act_exp(act, b, p, lane)
                            await_(act, o_flipped, b)
                            nc.scalar.activation(o_feat[:], bank_ms[:, 0:S], ACT.Copy).then_inc(o_flipped_out.sem, 1)

                @block.tensor
                def _(pe):
                    with pe.Fori(0, B // 2) as i:
                        for p in range(2):
                            b = 2 * i + p
                            await_(pe, normed, b)
                            for qt in range(QT):
                                last = nc.tensor.transpose(bank_ms[:, qt * P:(qt + 1) * P], xn[:, qt, :], ident)
                            last.then_inc(turned.sem, 1)
                            await_(pe, turned_out, b)
                            for s in range(2):
                                last = nc.tensor.matmul(bank[0][:, s * S:(s + 1) * S], wqk[:, s * D:(s + 1) * D], xnt[:],
                                                        start=True, stop=True)
                            last.then_inc(projected.sem, 1)
                            pe.wait_ge(x_added.sem, b + 1)
                            for qt, o in ((0, bank_pv), (1, bank[1])):
                                nc.tensor.matmul(o[:, 0:2 * D], xnt[:, qt * P:(qt + 1) * P], wv2[:].rearrange("p c d -> p (c d)"),
                                                 start=True, stop=True).then_inc(v_done.sem, 1)
                            await_(pe, vc_out, b)
                            for qt in range(QT):
                                o = bank_ms[:, qt * D:(qt + 1) * D]
                                last = nc.tensor.matmul(o, xnt[:, qt * P:(qt + 1) * P], wvs[:], start=True, stop=False)
                                for kt in range(qt + 1):
                                    last = nc.tensor.matmul(o, neg_uniform[:, kt, qt * P:(qt + 1) * P], v_centre[:, kt, :],
                                                            start=False, stop=(kt == qt))
                            last.then_inc(extra.sem, 1)
                            att.pe_stacks(pe, b, p)
                            await_(pe, v_out, b)
                            att.pe_max(pe, b, p)
                            await_(pe, extra_out, b)
                            att.pe_turn_max(pe, b, p)
                            att.pe_scores(pe, b, p, 0)
                            for lane in range(HL):
                                if lane + 1 < HL:
                                    att.pe_scores(pe, b, p, lane + 1)
                                att.pe_values(pe, b, p, lane)
                            att.pe_turn_out(pe, b, p)
                            await_(pe, summed, b)
                            for qt in range(QT):
                                last = nc.tensor.transpose(bank_ms[:, qt * P:(qt + 1) * P], o_tok[:, qt, :], ident)
                            last.then_inc(o_flipped.sem, 1)
                            await_(pe, o_flipped_out, b)
                            for qt in range(QT):
                                last = nc.tensor.matmul(bank_pv[:, qt * D:(qt + 1) * D], o_feat[:, qt * P:(qt + 1) * P], wproj[:],
                                                        start=True, stop=True)
                            last.then_inc(o_proj.sem, 1)

                @block.vector
                def _(dve):
                    dve.sem_inc(x_added.sem, 1)
                    dve.sem_inc(turned.sem, 1)
                    with dve.Fori(0, B // 2) as i:
                        for p in range(2):
                            b = 2 * i + p
                            dve.wait_ge(turned.sem, b + 1)
                            for qt in range(QT):
                                n = b * QT + qt
                                nc.vector.tensor_scalar(xn[:, qt, :], xres[:, bass.ds(n, 1), :].rearrange("p a d -> p (a d)"),
                                                        mv[:, bass.ds(n, 1), 0:1].rearrange("p a c -> p (a c)"),
                                                        rstd[:, bass.ds(n, 1)], ALU.subtract, ALU.mult).then_inc(normed.sem, 1)
                            await_(dve, projected, b)
                            nc.vector.tensor_scalar(qk[:, 0], bank[0][:, 0:S], qk_bias[:, 0:1], SCALE, ALU.add, ALU.mult).then_inc(qk_out.sem, 1)
                            nc.vector.tensor_scalar(qk[:, 1], bank[0][:, S:2 * S], qk_bias[:, 1:2], None, ALU.add).then_inc(qk_out.sem, 1)
                            for qt, src in ((0, bank_pv), (1, bank[1])):
                                await_(dve, v_done, b, qt + 1)
                                nc.vector.tensor_copy(v_centre[:, qt, :], src[:, D:2 * D]).then_inc(vc_out.sem, 1)
                            await_(dve, att.hi, b)
                            nc.vector.tensor_tensor(qk_lo[:], qk[:], qk_hi[:].bitcast(F32), ALU.subtract).then_inc(att.lo.sem, 1)
                            await_(dve, extra, b)
                            nc.vector.tensor_copy(v_extra[:].rearrange("p q d -> p (q d)"), bank_ms[:, 0:QT * D]).then_inc(extra_out.sem, 1)
                            att.dve_stacks(dve, b, p)
                            att.dve_max(dve, b, p)
                            att.dve_split_max(dve, b, p)
                            for lane in range(HL):
                                att.dve_values(dve, b, p, lane)
                            att.dve_divide(dve, b, p)
                            await_(dve, att.o_norm, b)
                            await_(dve, extra_out, b)
                            nc.vector.tensor_tensor(o_tok[:], o_tok[:], v_extra[:], ALU.add).then_inc(summed.sem, 1)
                            await_(dve, o_proj, b)
                            xb = xres[:, bass.ds(b * QT, QT), :]
                            nc.vector.tensor_tensor(xb, xb, bank_pv[:, 0:QT * D].rearrange("p (q d) -> p q d", q=QT),
                                                    ALU.add).then_inc(x_added.sem, 1)

        def normalise_and_turn(name, dst):
            with nc.sbuf_tensor(name + "_xn", [P, TILES, D], F32) as xa:
                norm = Norm(name)
                scaled, turned, out_act, out_dve = (sem(name + x) for x in ("_scaled", "_turned", "_out_act", "_out_dve"))
                with nc.Block() as block:
                    @block.vector
                    def _(dve):
                        norm.moments(dve)
                        norm.reciprocal_root(dve)
                        dve.wait_ge(norm.done, 7)
                        for n in range(TILES):
                            nc.vector.tensor_scalar(xa[:, n, :], xres[:, n, :], mv[:, n, 0:1], rstd[:, n:n + 1],
                                                    ALU.subtract, ALU.mult).then_inc(scaled, 1)
                        for r in (1, 3):
                            dve.wait_ge(turned, r + 1)
                            nc.vector.tensor_copy(dst[:, 512 * r:512 * (r + 1)], banks[r]).then_inc(out_dve, 1)

                    @block.scalar
                    def _(act):
                        norm.square_root(act)
                        for r in (0, 2):
                            act.wait_ge(turned, r + 1)
                            nc.scalar.activation(dst[:, 512 * r:512 * (r + 1)], banks[r], ACT.Copy).then_inc(out_act, 1)

                    @block.tensor
                    def _(pe):
                        for n in range(TILES):
                            pe.wait_ge(scaled, n + 1)
                            last = nc.tensor.transpose(banks[n // 4][:, (n % 4) * P:(n % 4 + 1) * P], xa[:, n, :], ident)
                            if n % 4 == 3:
                                last.then_inc(turned, 1)

        class Splines:

            def __init__(self, name, pctx):
                def psb(n, shape):
                    return pctx.enter_context(nc.sbuf_tensor(f"{name}_{n}", shape, F32))
                self.u, self.near, self.far = (psb(n, [P, 2, 512]) for n in ("u", "near", "far"))
                self.near2, self.far2 = (psb(n, [P, 2, 512]) for n in ("near2", "far2"))
                self.tanh = psb("tanh", [P, 512])
                self.planes = psb("planes", [P, KP, 512])
                self.folded = event(name + "_folded", 4)
                self.u_out = event(name + "_u_out", 2)
                self.clipped = event(name + "_clipped", 4)
                self.squared = event(name + "_squared", 4)
                self.cubed = event(name + "_cubed", 4)
                self.basis = event(name + "_basis", 2)
                self.masked = event(name + "_masked")
                self.tanh_out = event(name + "_tanh_out")
                self.ready = event(name + "_ready")

            def credit(self, dve):
                dve.sem_inc(self.ready.sem, 1)

            def pe_wait(self, pe, b):
                pe.wait_ge(self.ready.sem, b + 2)

            def act(self, act, b, x):
                shape = "p (s q) -> p s q"
                for pair in range(2):
                    if pair:
                        await_(act, self.masked, b)
                    else:
                        act.wait_ge(self.ready.sem, b + 1)
                    take_wait(act)
                    for k in range(2):
                        nc.scalar.activation(self.u[:, k].rearrange(shape, s=x.shape[1]), x, ACT.Abs,
                                             bias=abs_bias[:, 2 * pair + k:2 * pair + k + 1], scale=1.0 / H_GRID).then_inc(self.folded.sem, 1)
                    await_(act, self.folded, b, 2 * pair + 2)
                    uf = self.u[:].rearrange("p k q -> p (k q)")
                    nc.scalar.activation(uf, uf, ACT.Abs, bias=abs_bias[:, 4:5]).then_inc(self.u_out.sem, 1)
                    for n, (src, dst) in enumerate(((self.far, self.far2), (self.near, self.near2))):
                        await_(act, self.clipped, b, 2 * pair + n + 1)
                        nc.scalar.activation(dst[:].rearrange("p k q -> p (k q)"), src[:].rearrange("p k q -> p (k q)"), ACT.Square).then_inc(self.squared.sem, 1)
                nc.scalar.activation(self.tanh[:].rearrange(shape, s=x.shape[1]), x, ACT.Tanh, scale=0.5).then_inc(self.tanh_out.sem, 1)

            def dve(self, dve, b, x):
                s = x.shape[1]
                for pair in range(2):
                    await_(dve, self.u_out, b, pair + 1)
                    nc.vector.tensor_scalar(self.far[:], self.u[:], 2.0, -2.0, ALU.min, ALU.add).then_inc(self.clipped.sem, 1)
                    nc.vector.tensor_scalar(self.near[:], self.u[:], 1.0, -1.0, ALU.min, ALU.add).then_inc(self.clipped.sem, 1)
                    await_(dve, self.squared, b, 2 * pair + 1)
                    nc.vector.tensor_tensor(self.far[:], self.far[:], self.far2[:], ALU.mult).then_inc(self.cubed.sem, 1)
                    await_(dve, self.squared, b, 2 * pair + 2)
                    nc.vector.scalar_tensor_tensor(out=self.near[:].rearrange("p k q -> p (k q)"), in0=self.near[:].rearrange("p k q -> p (k q)"), scalar=4.0,
                                                   in1=self.near2[:].rearrange("p k q -> p (k q)"), op0=ALU.mult, op1=ALU.mult).then_inc(self.cubed.sem, 1)
                    await_(dve, self.cubed, b, 2 * pair + 2)
                    nc.vector.tensor_tensor(self.u[:], self.near[:], self.far[:], ALU.subtract).then_inc(self.basis.sem, 1)
                    await_(dve, self.basis, b, pair + 1)
                    for k in range(2):
                        j = 2 * pair + k
                        r = self.u[:, k].rearrange("p (s q) -> p s q", s=s)
                        for plane, side in ((j, ALU.is_lt), (j + 4, ALU.is_ge)):
                            last = nc.vector.scalar_tensor_tensor(out=self.planes[:, plane].rearrange("p (s q) -> p s q", s=s), in0=x,
                                                                  scalar=H_GRID * (j - 1.5), in1=r, op0=side, op1=ALU.mult)
                    if pair == 0:
                        last.then_inc(self.masked.sem, 1)
                await_(dve, self.tanh_out, b)
                nc.vector.scalar_tensor_tensor(out=self.planes[:, NB].rearrange("p (s q) -> p s q", s=s), in0=self.tanh[:].rearrange("p (s q) -> p s q", s=s),
                                               scalar=1.0, in1=x, op0=ALU.add, op1=ALU.mult).then_inc(self.ready.sem, 1)

        normalise_and_turn("norm2", xt[:, 0])
        with ExitStack() as lctx:
            kan = Splines("kan", lctx)
            rope_a = lctx.enter_context(nc.sbuf_tensor("rope_a", [P, 2, S], F32))
            rope_b = lctx.enter_context(nc.sbuf_tensor("rope_b", [P, 2, S], F32))

            att = Attention("cross", causal=False)
            q_kan = event("q_kan")
            k_kan = event("k_kan")
            v_kan = event("v_kan", QT)
            v_kan_out = event("v_kan_out", QT)
            qk_kan_out = event("qk_kan_out", 2)
            rotated = event("rotated")
            roped = event("roped", 3)
            c_flipped = event("c_flipped")
            c_flipped_out = event("c_flipped_out")

            def kan_input(b):
                return xt[:, :, bass.ds(b * S, S)]

            with nc.Block() as block:
                @block.sync
                def _(sp):
                    with sp.Fori(0, B // 2) as i:
                        for p in range(2):
                            att.dma_max(sp, 2 * i + p, p)

                @block.scalar
                def _(act):
                    act.sem_inc(c_flipped_out.sem, 1)
                    with act.Fori(0, B // 2) as i:
                        for p in range(2):
                            b = 2 * i + p
                            kan.act(act, b, kan_input(b))
                            await_(act, q_kan, b)
                            nc.scalar.activation(qk[:, 0], bank[0][:, 0:S], ACT.Copy).then_inc(qk_kan_out.sem, 1)
                            await_(act, k_kan, b)
                            nc.scalar.activation(qk[:, 1], bank[1][:, 0:S], ACT.Copy).then_inc(qk_kan_out.sem, 1)
                            await_(act, roped, b)
                            nc.scalar.activation(qk_hi[:].rearrange("p s q -> p (s q)"), qk[:].rearrange("p s q -> p (s q)"), ACT.Copy).then_inc(att.hi.sem, 1)
                            for qt, src in ((0, bank_pv), (1, bank_ms)):
                                await_(act, v_kan, b, qt + 1)
                                nc.scalar.activation(v_aug[p][:, qt, :, 0:HD], src[:, 0:D].rearrange("p (h d) -> p h d", d=HD), ACT.Copy).then_inc(v_kan_out.sem, 1)
                            att.act_stacks(act, b, p)
                            att.act_split_max(act, b, p)
                            for lane in range(HL):
                                att.act_exp(act, b, p, lane)
                            await_(act, c_flipped, b)
                            take_wait(act)
                            nc.scalar.activation(xt[:, 0, bass.ds(b * S, S)], bank_ms[:, 0:S], ACT.Copy).then_inc(c_flipped_out.sem, 1)

                @block.tensor
                def _(pe):
                    with pe.Fori(0, B // 2) as i:
                        for p in range(2):
                            b = 2 * i + p
                            kan.pe_wait(pe, b)
                            planes = kan.planes[:].rearrange("p c (s q) -> p c s q", s=2)
                            parts = [(c, s) for c in range(KP) for s in range(2)]
                            for x, done in ((0, q_kan), (1, k_kan)):
                                for c, s in parts:
                                    last = nc.tensor.matmul(bank[x][:, 0:S], kan_w[:, s, c, x * D:(x + 1) * D], planes[:, c, s],
                                                            start=((c, s) == parts[0]), stop=((c, s) == parts[-1]))
                                last.then_inc(done.sem, 1)
                            pe.wait_ge(c_flipped_out.sem, b + 1)
                            for qt, o in ((0, bank_pv), (1, bank_ms)):
                                for c, s in parts:
                                    last = nc.tensor.matmul(o[:, 0:D], planes[:, c, s, qt * P:(qt + 1) * P], kan_w[:, s, c, 2 * D:3 * D],
                                                            start=((c, s) == parts[0]), stop=((c, s) == parts[-1]))
                                last.then_inc(v_kan.sem, 1)
                            await_(pe, qk_kan_out, b)
                            nc.tensor.matmul(wide[0][:, 0:2 * S], cst("rope_rot"), qk[:].rearrange("p s q -> p (s q)"),
                                             start=True, stop=True).then_inc(rotated.sem, 1)
                            att.pe_stacks(pe, b, p)
                            att.pe_max(pe, b, p)
                            await_(pe, v_kan_out, b)
                            att.pe_turn_max(pe, b, p)
                            att.pe_scores(pe, b, p, 0)
                            for lane in range(HL):
                                if lane + 1 < HL:
                                    att.pe_scores(pe, b, p, lane + 1)
                                att.pe_values(pe, b, p, lane)
                            att.pe_turn_out(pe, b, p)
                            await_(pe, att.o_norm, b)
                            for qt in range(QT):
                                last = nc.tensor.transpose(bank_ms[:, qt * P:(qt + 1) * P], o_tok[:, qt, :], ident)
                            last.then_inc(c_flipped.sem, 1)

                @block.vector
                def _(dve):
                    kan.credit(dve)
                    with dve.Fori(0, B // 2) as i:
                        for p in range(2):
                            b = 2 * i + p
                            kan.dve(dve, b, kan_input(b))
                            await_(dve, rotated, b)
                            flat = "p s q -> p (s q)"
                            nc.vector.tensor_tensor(rope_a[:].rearrange(flat), qk[:].rearrange(flat), cosv, ALU.mult).then_inc(roped.sem, 1)
                            nc.vector.tensor_tensor(rope_b[:].rearrange(flat), wide[0][:, 0:2 * S], sinv, ALU.mult).then_inc(roped.sem, 1)
                            await_(dve, roped, b, 2)
                            nc.vector.tensor_tensor(qk[:], rope_a[:], rope_b[:], ALU.add).then_inc(roped.sem, 1)
                            await_(dve, att.hi, b)
                            nc.vector.tensor_tensor(qk_lo[:], qk[:], qk_hi[:].bitcast(F32), ALU.subtract).then_inc(att.lo.sem, 1)
                            att.dve_stacks(dve, b, p)
                            att.dve_max(dve, b, p)
                            att.dve_split_max(dve, b, p)
                            for lane in range(HL):
                                att.dve_values(dve, b, p, lane)
                            att.dve_divide(dve, b, p)
        actx.close()

        CH = 512
        CT = CH // P
        NCH = TILES // CT
        with ExitStack() as lctx:
            kano = Splines("kano", lctx)
            ko_done = event("ko_done")
            ko_added = event("ko_added")

            def ctx_input(c):
                return xt[:, 0:1, bass.ds(c * CH, CH)]

            with nc.Block() as block:
                @block.scalar
                def _(act):
                    with act.Fori(0, NCH) as c:
                        kano.act(act, c, ctx_input(c))

                @block.tensor
                def _(pe):
                    with pe.Fori(0, NCH) as c:
                        kano.pe_wait(pe, c)
                        pe.wait_ge(ko_added.sem, c + 1)
                        for n in range(CT):
                            for k in range(KP):
                                last = nc.tensor.matmul(bank[0][:, n * P:(n + 1) * P], kano.planes[:, k, n * P:(n + 1) * P], kan_wo[:, k, :],
                                                        start=(k == 0), stop=(k == KP - 1))
                        last.then_inc(ko_done.sem, 1)

                @block.vector
                def _(dve):
                    kano.credit(dve)
                    dve.sem_inc(ko_added.sem, 1)
                    with dve.Fori(0, NCH) as c:
                        kano.dve(dve, c, ctx_input(c))
                        await_(dve, ko_done, c)
                        xc = xres[:, bass.ds(c * CT, CT), :]
                        nc.vector.tensor_tensor(xc, xc, bank[0][:].rearrange("p (n d) -> p n d", n=CT), ALU.add).then_inc(ko_added.sem, 1)

        normalise_and_turn("norm3", xt[:, 0])
        with ExitStack() as lctx:
            act_h = lctx.enter_context(nc.sbuf_tensor("act_h", [P, FT, CH], F32))
            gate_up = event("gate_up", 2 * FT)
            silu_out = event("silu_out", FT)
            h_out = event("h_out", FT)
            down = event("down")
            y_out = event("y_out")
            stored = event("stored", 1, 16)
            gate_bank = [banks[0], banks[1], banks[2]]
            up_bank = [banks[3], banks[4], banks[5]]
            with nc.Block() as block:
                @block.sync
                def _(sp):
                    with sp.Fori(0, NCH) as c:
                        sp.wait_ge(y_out.sem, c + 2)
                        sp.dma_start(out.rearrange("b (t p) d -> p (b t) d", p=P)[:, bass.ds(c * CT, CT), :],
                                     xres[:, bass.ds(c * CT, CT), :]).then_inc(stored.sem, 16)
                    sp.wait_ge(stored.sem, 16 * NCH)

                @block.scalar
                def _(act):
                    with act.Fori(0, NCH) as c:
                        for f in range(FT):
                            await_(act, gate_up, c, 2 * f + 1)
                            nc.scalar.activation(act_h[:, f, :], gate_bank[f], ACT.Silu).then_inc(silu_out.sem, 1)

                @block.tensor
                def _(pe):
                    with pe.Fori(0, NCH) as c:
                        xc = xt[:, 0, bass.ds(c * CH, CH)]
                        for f in range(FT):
                            nc.tensor.matmul(gate_bank[f], w_gate[:, f * P:(f + 1) * P], xc, start=True, stop=True).then_inc(gate_up.sem, 1)
                            nc.tensor.matmul(up_bank[f], w_up[:, f * P:(f + 1) * P], xc, start=True, stop=True).then_inc(gate_up.sem, 1)
                        await_(pe, h_out, c)
                        pe.wait_ge(y_out.sem, c + 1)
                        for n in range(CT):
                            for f in range(FT):
                                last = nc.tensor.matmul(bank_pv[:, n * P:(n + 1) * P], act_h[:, f, n * P:(n + 1) * P], w_down[:, f, :],
                                                        start=(f == 0), stop=(f == FT - 1))
                        last.then_inc(down.sem, 1)

                @block.vector
                def _(dve):
                    dve.sem_inc(y_out.sem, 1)
                    with dve.Fori(0, NCH) as c:
                        for f in range(FT):
                            await_(dve, silu_out, c, f + 1)
                            await_(dve, gate_up, c, 2 * f + 2)
                            nc.vector.tensor_tensor(act_h[:, f, :], act_h[:, f, :], up_bank[f], ALU.mult).then_inc(h_out.sem, 1)
                        await_(dve, down, c)
                        xc = xres[:, bass.ds(c * CT, CT), :]
                        nc.vector.tensor_tensor(xc, xc, bank_pv[:].rearrange("p (n d) -> p n d", n=CT), ALU.add).then_inc(y_out.sem, 1)


_OUTS = ((B, S, D), "float32")


def kernel(**inputs):
    import concourse.bacc as bacc
    from concourse.bass_utils import run_bass_kernel_spmd

    nc = bacc.Bacc("TRN2", target_bir_lowering=False, num_devices=1)
    arrays = {n: np.ascontiguousarray(a) for n, a in inputs.items()}
    arrays |= {"const": CONST, "const_staged": CONST_STAGED}
    aps = {n: nc.dram_tensor(f"in_{n}_dram", a.shape, mybir.dt.from_np(a.dtype), kind="ExternalInput").ap()
           for n, a in arrays.items()}
    out = nc.dram_tensor("out_dram", (B, S, D), F32, kind="ExternalOutput").ap()
    build(nc, aps, out)
    r = run_bass_kernel_spmd(nc, [{f"in_{n}_dram": a for n, a in arrays.items()}], core_ids=[0])
    return r.results[0]["out_dram"]
```

```python
from contextlib import ExitStack

import numpy as np

import concourse.bass as bass
from concourse import mybir
from concourse.alu_op_type import AluOpType as ALU

ACT = mybir.ActivationFunctionType
F32 = mybir.dt.float32
F32R = mybir.dt.float32r
BF16 = mybir.dt.bfloat16
I32 = mybir.dt.int32
AX = mybir.AxisListType

B, S, D, H = 8, 256, 128, 16
P = 128
HD = D // H
TILES = B * S // P
QT = S // P
HL = 4
HG = H // HL
ROWS = P // HL
KROWS = 3 * HD + 2
NB = 8
KP = NB + 1
FT = 3
LEAST = -3.0e38
NEG = -1.0e30
EPS = 1e-5
H_GRID = 0.4
SCALE = 1.0 / float(np.sqrt(HD))


def constants():
    p, q = np.arange(P)[:, None], np.arange(P)[None, :]
    causal_q = np.where(q <= p, 0.0, NEG)
    causal_k = np.where(q >= p, 0.0, NEG)
    sel_hi, sel_lo_q, sel_hi_k, sel_lo_k = (np.zeros((P, HG, P)) for _ in range(4))
    for g in range(HG):
        for l in range(HL):
            for d in range(HD):
                f, r = (g * HL + l) * HD + d, l * ROWS + d
                sel_hi[f, g, r] = sel_hi[f, g, r + 2 * HD] = 1
                sel_lo_q[f, g, r + HD] = 1
                sel_hi_k[f, g, r] = sel_hi_k[f, g, r + HD] = 1
                sel_lo_k[f, g, r + 2 * HD] = 1
    rope_rot = np.zeros((P, P))
    for f in range(0, P, 2):
        rope_rot[f + 1, f] = -1
        rope_rot[f, f + 1] = 1
    inv = np.float32(1.0) / np.float32(10000.0) ** (np.arange(0, HD, 2, dtype=np.float32) / np.float32(HD))
    angle = np.arange(S, dtype=np.float32)[:, None] * inv[None, :].astype(np.float32)
    cos = np.tile(np.repeat(np.cos(angle), 2, axis=1).T, (H, 1))
    sin = np.tile(np.repeat(np.sin(angle), 2, axis=1).T, (H, 1))
    cos2 = np.concatenate([cos * SCALE, cos], axis=1)
    sin2 = np.concatenate([sin * SCALE, sin], axis=1)
    s = np.arange(S)
    uni = np.where(s[:, None] <= s[None, :], -1.0 / (s[None, :] + 1), 0.0)
    neg_uniform = uni.reshape(QT, P, S).transpose(1, 0, 2)
    ones_rows = np.zeros((P, 1))
    ones_rows[[l * ROWS + r for l in range(HL) for r in (3 * HD, 3 * HD + 1)]] = 1
    k = np.arange(4)
    abs_bias = np.tile(np.append(1.5 - k, -2.0)[None, :], (P, 1))
    parts = [("ident", np.eye(P)), ("causal_q", causal_q), ("causal_k", causal_k),
             ("sel_hi", sel_hi), ("sel_lo_q", sel_lo_q), ("sel_hi_k", sel_hi_k), ("sel_lo_k", sel_lo_k),
             ("rope_rot", rope_rot), ("cos", cos2), ("sin", sin2), ("neg_uniform", neg_uniform),
             ("ones_rows", ones_rows), ("abs_bias", abs_bias)]
    staged = ("causal_q", "causal_k", "sel_hi", "sel_lo_q", "sel_hi_k", "sel_lo_k")
    at, kept, used = {}, [[], []], [0, 0]
    for name, a in parts:
        a, which = a.reshape(P, -1).astype(np.float32), int(name in staged)
        at[name] = (used[which], used[which] + a.shape[1])
        kept[which].append(a)
        used[which] += a.shape[1]
    return at, np.concatenate(kept[0], axis=1), np.concatenate(kept[1], axis=1)


CONST_AT, CONST, CONST_STAGED = constants()


class Event:

    def __init__(self, sem, per, unit=1):
        self.sem, self.per, self.unit = sem, per, unit

    def at(self, b, n=None):
        return (b * self.per + (self.per if n is None else n)) * self.unit


def build(nc, t, out):
    with ExitStack() as ctx:
        def sb(name, shape, dt=F32):
            return ctx.enter_context(nc.sbuf_tensor(name, shape, dt))

        def psum(name, shape):
            return ctx.enter_context(nc.psum_tensor(name, shape, F32))

        def sem(name):
            return ctx.enter_context(nc.semaphore(name))

        def event(name, per=1, unit=1):
            return Event(sem(name), per, unit)

        def await_(eng, ev, b, n=None):
            eng.wait_ge(ev.sem, ev.at(b, n))

        wait_taken = sem("wait_taken")

        def take_wait(act):
            act.sem_inc(wait_taken, 1)

        const = sb("const", [P, CONST.shape[1]])

        def cst(name):
            a, z = CONST_AT[name]
            return const[:, a:z]

        ident = cst("ident")
        ident_r = sb("ident_r", [P, P], F32R)
        ident_b = sb("ident_b", [P, P], BF16)
        causal_q_b = sb("causal_q_b", [P, P], BF16)
        causal_k_b = sb("causal_k_b", [P, P], BF16)
        sel_r = sb("sel_r", [P, 4, HG, P], F32R)
        sel_q_hi, sel_q_lo, sel_k_hi, sel_k_lo = (sel_r[:, n] for n in range(4))
        xres = sb("xres", [P, TILES, D])
        cosv = cst("cos")
        sinv = cst("sin")
        neg_uniform = cst("neg_uniform").rearrange("p (k q) -> p k q", k=QT)
        ones_rows = cst("ones_rows")
        abs_bias = cst("abs_bias")
        wqk = sb("wqk", [P, 2 * D])
        wv2 = sb("wv2", [P, 2, D])
        wvs = sb("wvs", [P, D])
        wproj = sb("wproj", [P, D])
        qk_bias = sb("qk_bias", [P, 2])
        kan_w = sb("kan_w", [P, 2, KP, 3 * D])
        kan_wo = sb("kan_wo", [P, KP, D])
        w_gate = sb("w_gate", [P, FT * P])
        w_up = sb("w_up", [P, FT * P])
        w_down = sb("w_down", [P, FT, D])
        mask_q = sb("mask_q", [P, QT, S])
        mask_k = sb("mask_k", [P, 2, QT, S], F32R)
        xt = sb("xt", [P, 2, TILES * P])
        stats = sb("stats", [P, TILES, 6])
        mv = sb("mv", [P, TILES, 2])
        rstd = sb("rstd", [P, TILES])
        rstd_a = sb("rstd_a", [P, TILES])
        rstd_b = sb("rstd_b", [P, TILES])
        eps_col = sb("eps_col", [P, 1])

        bank = [psum(f"bank{n}", [P, 512]) for n in range(2)]
        wide = [psum(f"wide{n}", [P, 1024]) for n in range(2)]
        bank_pv = psum("bank_pv", [P, 512])
        bank_ms = psum("bank_ms", [P, 512])
        banks = [bank[0][:], bank[1][:], wide[0][:, 0:512], wide[0][:, 512:1024],
                 wide[1][:, 0:512], wide[1][:, 512:1024], bank_pv[:], bank_ms[:]]

        class Norm:

            def __init__(self, name):
                self.done, self.root = sem(name + "_done"), sem(name + "_root")

            def moments(self, dve):
                for n in range(TILES):
                    last = nc.vector.bn_stats(stats[:, n, :], xres[:, n, :])
                last.then_inc(self.done, 1)
                dve.wait_ge(self.done, 1)
                for n in range(TILES):
                    last = nc.vector.bn_aggr(mv[:, n, :], stats[:, n, :])
                last.then_inc(self.done, 1)

            def square_root(self, act):
                act.wait_ge(self.done, 2)
                nc.scalar.activation(rstd_a[:], mv[:, :, 1], ACT.Sqrt, bias=eps_col[:, 0:1]).then_inc(self.root, 1)

            def reciprocal_root(self, dve):
                dve.wait_ge(self.root, 1)
                nc.vector.reciprocal(rstd[:], rstd_a[:]).then_inc(self.done, 1)
                dve.wait_ge(self.done, 3)
                nc.vector.tensor_tensor(rstd_b[:], rstd[:], rstd[:], ALU.mult).then_inc(self.done, 1)
                dve.wait_ge(self.done, 4)
                nc.vector.scalar_tensor_tensor(out=rstd_b[:], in0=mv[:, :, 1], scalar=EPS, in1=rstd_b[:],
                                               op0=ALU.add, op1=ALU.mult).then_inc(self.done, 1)
                dve.wait_ge(self.done, 5)
                nc.vector.tensor_scalar(rstd_b[:], rstd_b[:], -0.5, 1.5, ALU.mult, ALU.add).then_inc(self.done, 1)
                dve.wait_ge(self.done, 6)
                nc.vector.tensor_tensor(rstd[:], rstd[:], rstd_b[:], ALU.mult).then_inc(self.done, 1)

        with ExitStack() as sctx:
            def ssb(name, shape, dt=F32):
                return sctx.enter_context(nc.sbuf_tensor(name, shape, dt))

            staged = ssb("staged", [P, CONST_STAGED.shape[1]])

            def stg(name):
                a, z = CONST_AT[name]
                return staged[:, a:z]

            spl = ssb("spl", [P, 3, 3 * D * NB])
            base = ssb("base", [P, 3, 3 * D])
            scaler = ssb("scaler", [P, 3, 3 * D])
            splo = ssb("splo", [P, D * NB])
            baseo = ssb("baseo", [P, D])
            scalero = ssb("scalero", [P, D])
            wint = ssb("wint", [P, 3, FT * P], I32)
            wflt = ssb("wflt", [P, 3, FT * P])
            gains = ssb("gains", [P, 3, H])
            vw = ssb("vw", [P, D])
            mask_n = ssb("mask_n", [P, QT, S])
            ctx_n = ssb("ctx_n", [P, TILES, D])
            maskt = ssb("maskt", [P, QT, S])

            ld = {n: sem("ld_" + n) for n in ("const", "x", "attn", "ffn", "mask", "ctx", "base", "out")}
            ld_spl = [sem(f"ld_spl{r}") for r in range(3)]
            pool_w = sem("pool_w")
            dve_w = sem("dve_w")
            norm1 = Norm("norm1")
            ready = sem("ready")
            pe_tr = sem("pe_tr")
            evac_act = sem("evac_act")
            evac_dve = sem("evac_dve")

            def turns():
                for r4 in range(TILES // 4):
                    yield ([ctx_n[:, 4 * r4 + i, :] for i in range(4)], (ld["ctx"], 16),
                           xt[:, 1, 512 * r4:512 * (r4 + 1)], None)
                yield ([mask_n[:, qt, kt * P:(kt + 1) * P] for kt in range(QT) for qt in range(QT)],
                       (ld["mask"], 16), maskt[:].rearrange("p k q -> p (k q)"), None)
                for n, dst in ((0, w_gate), (1, w_up)):
                    yield ([wflt[:, n, r * P:(r + 1) * P] for r in range(FT)], (dve_w, 1), dst[:], None)
                yield ([wflt[:, 2, r * P:(r + 1) * P] for r in range(FT)], (dve_w, 1),
                       w_down[:].rearrange("p r d -> p (r d)"), None)
                for c0 in (0, 4):
                    yield ([splo[:, c:D * NB:NB] for c in range(c0, c0 + 4)], (dve_w, 2),
                           kan_wo[:, c0:c0 + 4, :].rearrange("p c d -> p (c d)"), None)
                yield ([baseo[:]], (ld["out"], 48), kan_wo[:, NB, :], "half")
                for s in range(2):
                    yield ([base[:, r, s * P:(s + 1) * P] for r in range(3)], (pool_w, 1), kan_w[:, s, NB, :], "half features")
                for s in range(2):
                    for c in range(NB):
                        yield ([spl[:, r, s * P * NB + c:(s + 1) * P * NB:NB] for r in range(3)], (dve_w, 8),
                               kan_w[:, s, c, :], "features")

            jobs = list(turns())

            def evacuate(eng, odd):
                for n, (ins, _, dst, order) in enumerate(jobs):
                    if n % 2 != odd:
                        continue
                    src = banks[n % 8][:, 0:P * len(ins)]
                    half = 0.5 if order and "half" in order else 1.0
                    if order and "features" in order:
                        src = src.rearrange("p (h s d) -> p s h d", s=3, d=HD)
                        dst = dst.rearrange("p (s h d) -> p s h d", s=3, d=HD)
                    eng.wait_ge(pe_tr, n + 1)
                    if odd:
                        nc.vector.tensor_scalar(dst, src, half, None, ALU.mult).then_inc(evac_dve, 1)
                    else:
                        nc.scalar.activation(dst, src, ACT.Copy, scale=half).then_inc(evac_act, 1)

            with nc.Block() as block:
                @block.sync
                def _(sp):
                    sp.dma_start(const[:], t["const"]).then_inc(ld["const"], 16)
                    sp.dma_start(staged[:], t["const_staged"]).then_inc(ld["const"], 16)
                    sp.dma_start(base[:], t["L0_xattn_qkv_base_w"].rearrange("(r p) i -> p r i", p=P)).then_inc(ld["base"], 16)
                    sp.dma_start(scaler[:], t["L0_xattn_qkv_scaler"].rearrange("(r p) i -> p r i", p=P)).then_inc(ld["base"], 16)
                    for r in range(3):
                        sp.dma_start(spl[:, r, :], t["L0_xattn_qkv_spline_w"][r * P:(r + 1) * P].rearrange("p i c -> p (i c)"),
                                     ).then_inc(ld_spl[r], 16)
                    sp.dma_start(splo[:], t["L0_xattn_out_spline_w"].rearrange("o i c -> o (i c)")).then_inc(ld["out"], 16)
                    sp.dma_start(baseo[:], t["L0_xattn_out_base_w"]).then_inc(ld["out"], 16)
                    sp.dma_start(scalero[:], t["L0_xattn_out_scaler"]).then_inc(ld["out"], 16)

                @block.scalar
                def _(act):
                    act.dma_start(xres[:], t["x"].rearrange("b (t p) d -> p (b t) d", p=P)).then_inc(ld["x"], 16)
                    act.dma_start(ctx_n[:], t["ctx_1024"].rearrange("b (t p) d -> p (b t) d", p=P)).then_inc(ld["ctx"], 16)
                    act.dma_start(mask_n[:], t["mask_SxS2_ff0"].rearrange("(t p) k -> p t k", p=P)).then_inc(ld["mask"], 16)
                    act.dma_start(wint[:, 0, :].rearrange("p (r d) -> p r d", r=FT), t["L0_ffn_w_gate"].rearrange("(r p) d -> p r d", p=P)).then_inc(ld["ffn"], 16)
                    act.dma_start(wint[:, 1, :].rearrange("p (r d) -> p r d", r=FT), t["L0_ffn_w_up"].rearrange("(r p) d -> p r d", p=P)).then_inc(ld["ffn"], 16)
                    act.dma_start(wint[:, 2, :], t["L0_ffn_w_down"]).then_inc(ld["ffn"], 16)
                    evacuate(act, 0)
                    norm1.square_root(act)

                @block.gpsimd
                def _(pool):
                    names = ("resid", "centre", "skip")
                    for n, g in enumerate(names):
                        pool.dma_start(gains[:, n, :], t[f"L0_attn_{g}_gain"].rearrange("a h b c -> (a b c h)").partition_broadcast(P)).then_inc(ld["attn"], 16)
                    pool.dma_start(vw[:], t["L0_attn_v_w"]).then_inc(ld["attn"], 16)
                    pool.dma_start(wqk[:], t["L0_attn_qk_w"]).then_inc(ld["attn"], 16)
                    pool.dma_start(wproj[:], t["L0_attn_cproj_w"]).then_inc(ld["attn"], 16)
                    for s in range(2):
                        pool.dma_start(qk_bias[:, s:s + 1], t["L0_attn_qk_b"][s * P:(s + 1) * P].rearrange("(p o) -> p o", o=1)).then_inc(ld["attn"], 16)
                    pool.wait_ge(ld["base"], 32)
                    nc.gpsimd.tensor_tensor(base[:, :, P:2 * P], base[:, :, P:2 * P], base[:, :, 2 * P:3 * P], ALU.add).then_inc(pool_w, 1)

                @block.tensor
                def _(pe):
                    pe.wait_ge(ld["const"], 32)
                    for n, (ins, (s, v), _, _) in enumerate(jobs):
                        pe.wait_ge(s, v)
                        if n >= 8:
                            pe.wait_ge(evac_dve if n % 2 else evac_act, (n - 8) // 2 + 1)
                        for i, a in enumerate(ins):
                            last = nc.tensor.transpose(banks[n % 8][:, i * P:(i + 1) * P], a, ident)
                        last.then_inc(pe_tr, 1)

                @block.vector
                def _(dve):
                    nc.vector.memset(eps_col[:], EPS)
                    dve.wait_ge(ld["ffn"], 48)
                    nc.vector.tensor_scalar(wflt[:], wint[:], float(np.float32(1.0 / 127.0)), None, ALU.mult).then_inc(dve_w, 1)
                    dve.wait_ge(ld["out"], 48)
                    nc.vector.scalar_tensor_tensor(out=splo[:].rearrange("p (i c) -> p i c", c=NB),
                                                   in0=splo[:].rearrange("p (i c) -> p i c", c=NB), scalar=1.0 / 6.0,
                                                   in1=scalero[:].unsqueeze(2).broadcast_to([P, D, NB]),
                                                   op0=ALU.mult, op1=ALU.mult).then_inc(dve_w, 1)
                    dve.wait_ge(ld["x"], 16)
                    norm1.moments(dve)
                    dve.wait_ge(ld["base"], 32)
                    for r in range(3):
                        dve.wait_ge(ld_spl[r], 16)
                        v = spl[:, r, :].rearrange("p (i c) -> p i c", c=NB)
                        nc.vector.scalar_tensor_tensor(out=v, in0=v, scalar=1.0 / 6.0,
                                                       in1=scaler[:, r, :].unsqueeze(2).broadcast_to([P, 3 * D, NB]),
                                                       op0=ALU.mult, op1=ALU.mult).then_inc(dve_w, 1)
                    for r in range(3):
                        dve.wait_ge(dve_w, 3 + r)
                        a, b, c = P * NB, 2 * P * NB, 3 * P * NB
                        nc.vector.tensor_tensor(spl[:, r, a:b], spl[:, r, a:b], spl[:, r, b:c], ALU.add).then_inc(dve_w, 1)
                    dve.wait_ge(ld["const"], 32)
                    nc.vector.tensor_copy(ident_r[:], ident)
                    nc.vector.tensor_copy(ident_b[:], ident)
                    nc.vector.tensor_copy(causal_q_b[:], stg("causal_q"))
                    nc.vector.tensor_copy(causal_k_b[:], stg("causal_k"))
                    for n, name in enumerate(("sel_hi", "sel_lo_q", "sel_hi_k", "sel_lo_k")):
                        nc.vector.tensor_copy(sel_r[:, n], stg(name).rearrange("p (g m) -> p g m", g=HG))
                    dve.wait_ge(ld["attn"], 16 * 8)
                    for n, dst in ((0, wv2[:, 0]), (1, wv2[:, 1]), (2, wvs[:])):
                        nc.vector.tensor_tensor(dst.rearrange("p (h d) -> p h d", d=HD), vw[:].rearrange("p (h d) -> p h d", d=HD),
                                                gains[:, n, :].unsqueeze(2).broadcast_to([P, H, HD]), ALU.mult)
                    evacuate(dve, 1)
                    dve.wait_ge(ld["mask"], 16)
                    nc.vector.tensor_copy(mask_q[:], mask_n[:])
                    dve.wait_ge(evac_act, 3)
                    nc.vector.tensor_copy(mask_k[:, 0], maskt[:]).then_inc(ready, 1)
                    dve.wait_ge(ready, 1)
                    nc.vector.tensor_tensor(mask_k[:, 1], maskt[:], mask_k[:, 0].bitcast(F32), ALU.subtract)
                    norm1.reciprocal_root(dve)


        actx = ExitStack()

        def asb(name, shape, dt=F32):
            return actx.enter_context(nc.sbuf_tensor(name, shape, dt))

        qk = asb("qk", [P, 2, S])
        qk_hi = asb("qk_hi", [P, 2, S], F32R)
        qk_lo = asb("qk_lo", [P, 2, S], F32R)
        q_stack = [asb(f"q_stack{n}", [P, HG, S], F32R) for n in range(2)]
        k_stack = [asb(f"k_stack{n}", [P, HG, S], F32R) for n in range(2)]
        v_aug = [asb(f"v_aug{n}", [P, QT, H, ROWS]) for n in range(2)]
        row_max = [asb(f"row_max{n}", [P, QT, H]) for n in range(2)]
        max_hi = asb("max_hi", [H, S], F32R)
        max_lo = asb("max_lo", [H, S], F32R)
        probs = [asb(f"probs{n}", [P, QT * HG * S]) for n in range(2)]
        o_lane = asb("o_lane", [P, HL, S])
        rsum = asb("rsum", [P, QT, H])
        o_tok = asb("o_tok", [P, QT, D])
        o_feat = asb("o_feat", [P, S])

        class Attention:

            def __init__(self, name, causal, out_banks):
                self.causal = causal
                self.out_banks = out_banks
                self.sign = 1.0 if causal else -1.0
                self.max_pieces = HL * (3 if causal else 4)
                self.hi = event(name + "_hi")
                self.lo = event(name + "_lo")
                self.stacked = event(name + "_stacked", 2)
                self.q_ready = event(name + "_q_ready")
                self.k_ready = event(name + "_k_ready")
                self.s_ready = event(name + "_s_ready", self.max_pieces)
                self.s_max = event(name + "_s_max", self.max_pieces)
                self.m_turned = event(name + "_m_turned")
                self.m_hi = event(name + "_m_hi")
                self.m_lo = event(name + "_m_lo")
                self.m_placed = event(name + "_m_placed", 2 * HL, 16)
                self.e_ready = event(name + "_e_ready", 2 * HL)
                self.e_done = event(name + "_e_done", 2 * HL)
                self.pv = event(name + "_pv", HL)
                self.pv_out = event(name + "_pv_out", HL)
                self.o_turned = event(name + "_o_turned", QT)
                self.o_rsum = event(name + "_o_rsum", QT)
                self.o_norm = event(name + "_o_norm", QT)

            def pe_stack(self, pe, b, s):
                hi, lo = ((sel_q_hi, sel_q_lo), (sel_k_hi, sel_k_lo))[s]
                if s == 0:
                    await_(pe, self.hi, b)
                    await_(pe, self.lo, b)
                for g in range(HG):
                    o = wide[s][:, g * S:(g + 1) * S]
                    nc.tensor.matmul(o, hi[:, g], qk_hi[:, s], start=True, stop=False)
                    last = nc.tensor.matmul(o, lo[:, g], qk_lo[:, s], start=False, stop=True)
                last.then_inc(self.stacked.sem, 1)

            def act_stack(self, act, b, p):
                await_(act, self.stacked, b, 1)
                nc.scalar.activation(q_stack[p][:].rearrange("p g q -> p (g q)"), wide[0][:], ACT.Copy).then_inc(self.q_ready.sem, 1)

            def dve_stack(self, dve, b, p):
                await_(dve, self.stacked, b, 2)
                nc.vector.tensor_scalar(k_stack[p][:].rearrange("p g q -> p (g q)"), wide[1][:], ones_rows, None,
                                        ALU.add).then_inc(self.k_ready.sem, 1)

            def max_parts(self, lane):
                parts = [(0, 0, HG, P), (1, 0, 2, S), (1, 2, 2, S)] if self.causal else \
                        [(0, 0, 2, S), (0, 2, 2, S), (1, 0, 2, S), (1, 2, 2, S)]
                return [(lane * len(parts) + n, *x) for n, x in enumerate(parts)]

            def pe_max(self, pe, b, p, lane, pieces=None):
                if lane == 0:
                    await_(pe, self.q_ready, b)
                    await_(pe, self.k_ready, b)
                r = lane * ROWS
                for n, qt, g0, ng, keys in self.max_parts(lane)[pieces or slice(None)]:
                    o = bank[n % 2][:].rearrange("p (g k) -> p g k", g=ng)
                    if n >= 2:
                        await_(pe, self.s_max, b, n - 1)
                    if self.causal:
                        nc.tensor.matmul(o[:, :, keys - P:keys], ident_b[:],
                                         causal_q_b[:].unsqueeze(1).broadcast_to([P, ng, P]),
                                         start=True, stop=False, skip_group_check=True)
                    for g in range(ng):
                        last = nc.tensor.matmul(o[:, g, :], q_stack[p][r:r + 3 * HD, g0 + g, qt * P:(qt + 1) * P],
                                                k_stack[p][r:r + 3 * HD, g0 + g, 0:keys],
                                                start=(g == 0 and not self.causal), stop=(g == ng - 1), skip_group_check=True)
                    last.then_inc(self.s_ready.sem, 1)

            def dve_max(self, dve, b, p, lane):
                for n, qt, g0, ng, keys in self.max_parts(lane):
                    await_(dve, self.s_ready, b, n + 1)
                    a = lane * HG + g0
                    o = bank[n % 2][:].rearrange("p (g k) -> p g k", g=ng)
                    if self.causal:
                        nc.vector.tensor_reduce(row_max[p][:, qt, a:a + ng], o, AX.X, ALU.max, negate=True).then_inc(self.s_max.sem, 1)
                    else:
                        take_wait(dve)
                        for g in range(ng):
                            last = nc.vector.tensor_tensor_reduce(o[:, g, :], o[:, g, :], mask_q[:, qt], 1.0, LEAST, ALU.add, ALU.max,
                                                                  row_max[p][:, qt, a + g:a + g + 1])
                        last.then_inc(self.s_max.sem, 1)

            def pe_turn_max(self, pe, b, p):
                await_(pe, self.s_max, b)
                for qt in range(QT):
                    last = nc.tensor.transpose(bank[0][0:H, qt * P:(qt + 1) * P], row_max[p][:, qt, :], ident)
                last.then_inc(self.m_turned.sem, 1)

            def act_split_max(self, act, b):
                await_(act, self.m_turned, b)
                nc.scalar.activation(max_hi[:], bank[0][0:H, 0:S], ACT.Copy, scale=self.sign).then_inc(self.m_hi.sem, 1)

            def dve_split_max(self, dve, b):
                await_(dve, self.m_hi, b)
                nc.vector.scalar_tensor_tensor(out=max_lo[:], in0=bank[0][0:H, 0:S], scalar=self.sign, in1=max_hi[:].bitcast(F32),
                                               op0=ALU.mult, op1=ALU.subtract).then_inc(self.m_lo.sem, 1)

            def dma_max(self, sp, b, p):
                await_(sp, self.m_lo, b)
                for half, src in ((0, max_hi), (1, max_lo)):
                    for lane in range(HL):
                        row = lane * ROWS + 3 * HD + half
                        sp.dma_start(q_stack[p][row:row + 1, :, :].bitcast(F32),
                                     src[lane * HG:(lane + 1) * HG, :].bitcast(F32)).then_inc(self.m_placed.sem, 16)

            def queries(self, kt):
                return kt * P if self.causal else 0

            def probs_of(self, lane, kt):
                n = S - self.queries(kt)
                return probs[lane % 2][:, kt * HG * S:kt * HG * S + HG * n].rearrange("p (g q) -> p g q", g=HG)

            def pe_scores(self, pe, b, p, lane, kts=range(QT)):
                if lane == 0:
                    await_(pe, self.m_placed, b)
                r = lane * ROWS
                for kt in kts:
                    q0 = self.queries(kt)
                    n = S - q0
                    o = wide[kt][:, 0:HG * n].rearrange("p (g q) -> p g q", g=HG)
                    if lane:
                        await_(pe, self.e_done, b, 2 * lane - 1 + kt)
                    gs = 512 // n
                    for g0 in range(0, HG, gs):
                        ob = o[:, g0:g0 + gs, :]
                        if self.causal:
                            nc.tensor.matmul(ob[:, :, 0:P], ident_b[:], causal_k_b[:].unsqueeze(1).broadcast_to([P, gs, P]),
                                             start=True, stop=False, skip_group_check=True)
                        else:
                            for half in range(2):
                                nc.tensor.matmul(ob, ident_r[:], mask_k[:, half, kt].unsqueeze(1).broadcast_to([P, gs, S]),
                                                 start=(half == 0), stop=False, skip_group_check=True)
                        for g in range(g0, g0 + gs):
                            last = nc.tensor.matmul(o[:, g, :], k_stack[p][r:r + KROWS, g, kt * P:(kt + 1) * P],
                                                    q_stack[p][r:r + KROWS, g, q0:S],
                                                    start=False, stop=True, skip_group_check=True)
                    last.then_inc(self.e_ready.sem, 1)

            def act_exp(self, act, b, p, lane):
                for kt in range(QT):
                    await_(act, self.e_ready, b, 2 * lane + kt + 1)
                    if lane >= 2 and kt == 0:
                        await_(act, self.pv, b, lane - 1)
                    n = HG * (S - self.queries(kt))
                    nc.scalar.activation(self.probs_of(lane, kt).rearrange("p g q -> p (g q)"), wide[kt][:, 0:n],
                                         ACT.Exp).then_inc(self.e_done.sem, 1)

            def pe_values(self, pe, b, p, lane):
                await_(pe, self.e_done, b, 2 * lane + 2)
                if lane:
                    await_(pe, self.pv_out, b, lane)
                for kt in range(QT):
                    for g in range(HG):
                        last = nc.tensor.matmul(bank_pv[g * ROWS:(g + 1) * ROWS, self.queries(kt):S],
                                                v_aug[p][:, kt, g * HL + lane, :], self.probs_of(lane, kt)[:, g, :],
                                                start=(kt == 0), stop=(kt == QT - 1), tile_position=(0, g * ROWS),
                                                skip_group_check=True)
                last.then_inc(self.pv.sem, 1)

            def dve_values(self, dve, b, p, lane):
                await_(dve, self.pv, b, lane + 1)
                nc.vector.tensor_copy(o_lane[:, lane, :], bank_pv[:, 0:S]).then_inc(self.pv_out.sem, 1)

            def pe_turn_out(self, pe, b):
                await_(pe, self.pv_out, b)
                for qt in range(QT):
                    for lane in range(HL):
                        last = nc.tensor.transpose(self.out_banks[qt][:, lane * P:(lane + 1) * P], o_lane[:, lane, qt * P:(qt + 1) * P], ident)
                    last.then_inc(self.o_turned.sem, 1)

            def dve_divide(self, dve, b):
                for qt in range(QT):
                    await_(dve, self.o_turned, b, qt + 1)
                    o = self.out_banks[qt].rearrange("p (l g r) -> p l g r", l=HL, g=HG)
                    nc.vector.reciprocal(rsum[:, qt].rearrange("p (l g) -> p l g", l=HL), o[:, :, :, HD]).then_inc(self.o_rsum.sem, 1)
                for qt in range(QT):
                    await_(dve, self.o_rsum, b, qt + 1)
                    o = self.out_banks[qt].rearrange("p (l g r) -> p l g r", l=HL, g=HG)
                    nc.vector.tensor_tensor(o_tok[:, qt].rearrange("p (g l d) -> p l g d", g=HG, l=HL), o[:, :, :, 0:HD],
                                            rsum[:, qt].rearrange("p (l g) -> p l g", l=HL).unsqueeze(3).broadcast_to([P, HL, HG, HD]),
                                            ALU.mult).then_inc(self.o_norm.sem, 1)

            def pe_flip(self, pe, o, after, b, done):
                await_(pe, after, b)
                for qt in range(QT):
                    last = nc.tensor.transpose(o[:, qt * P:(qt + 1) * P], o_tok[:, qt, :], ident)
                last.then_inc(done.sem, 1)

        with ExitStack() as lctx:
            def lsb(name, shape, dt=F32):
                return lctx.enter_context(nc.sbuf_tensor(name, shape, dt))

            xn = lsb("xn", [P, QT, D])
            xnt = lsb("xnt", [P, S])
            v_centre = lsb("v_centre", [P, QT, D])
            v_extra = [lsb(f"v_extra{n}", [P, QT, D]) for n in range(2)]

            att = Attention("self", causal=True, out_banks=[bank_pv[:], bank_ms[:]])
            vones = sem("vones")
            normed = event("normed", QT)
            turned = event("turned")
            turned_out = event("turned_out")
            projected = event("projected")
            qk_out = event("qk_out", 2)
            v_done = event("v_done")
            v_out = event("v_out")
            vc_out = event("vc_out")
            extra = event("extra")
            extra_out = event("extra_out")
            summed = event("summed")
            o_flipped = event("o_flipped")
            o_flipped_out = event("o_flipped_out")
            o_proj = event("o_proj")
            x_added = event("x_added")

            def self_batches(eng, body):
                body(0, 0, 0, 2)
                body(1, 1, 1, 2)
                with eng.Fori(1, (B - 2) // 2) as i:
                    for p in range(2):
                        body(2 * i + p, p, 1, 2)
                body(B - 2, 0, 1, 1)
                body(B - 1, 1, 1, 0)

            with nc.Block() as block:
                @block.gpsimd
                def _(pool):
                    for p in range(2):
                        nc.gpsimd.memset(v_aug[p][:], 0.0).then_inc(vones, 1)
                    pool.wait_ge(vones, 2)
                    for p in range(2):
                        nc.gpsimd.memset(v_aug[p][:, :, :, HD:HD + 1], 1.0).then_inc(vones, 1)

                @block.sync
                def _(sp):
                    att.dma_max(sp, 0, 0)

                    def body(b, p, before, ahead):
                        if ahead >= 1:
                            att.dma_max(sp, b + 1, 1 - p)

                    self_batches(sp, body)

                @block.scalar
                def _(act):
                    def flip_out(b):
                        await_(act, o_flipped, b)
                        nc.scalar.activation(o_feat[:], bank_ms[:, 0:S], ACT.Copy).then_inc(o_flipped_out.sem, 1)

                    def turn_out(b):
                        nc.scalar.activation(xnt[:], bank_ms[:, S:2 * S], ACT.Copy).then_inc(turned_out.sem, 1)

                    def high(b):
                        await_(act, qk_out, b)
                        nc.scalar.activation(qk_hi[:].rearrange("p s q -> p (s q)"), qk[:].rearrange("p s q -> p (s q)"), ACT.Copy).then_inc(att.hi.sem, 1)

                    def values(b, p):
                        await_(act, vc_out, b)
                        nc.scalar.activation(v_aug[p][:, :, :, 0:HD], bank_ms[:].rearrange("p (q c h d) -> p q c h d", q=QT, c=2, d=HD)[:, :, 0],
                                             ACT.Copy).then_inc(v_out.sem, 1)

                    def prepare(b, p):
                        act.wait_ge(turned.sem, b + 2)
                        turn_out(b)
                        high(b)
                        values(b, p)
                        att.act_stack(act, b, p)

                    act.wait_ge(vones, 4)
                    prepare(0, 0)
                    att.act_split_max(act, 0)
                    prepare(1, 1)

                    def body(b, p, before, ahead):
                        att.act_exp(act, b, p, 0)
                        att.act_exp(act, b, p, 1)
                        if ahead >= 2:
                            act.wait_ge(turned.sem, b + 4)
                        if before:
                            flip_out(b - 1)
                        if ahead >= 2:
                            turn_out(b + 2)
                        att.act_exp(act, b, p, 2)
                        if ahead >= 2:
                            high(b + 2)
                        att.act_exp(act, b, p, 3)
                        if ahead >= 2:
                            await_(act, att.pv, b)
                            values(b + 2, p)
                        if ahead >= 1:
                            att.act_split_max(act, b + 1)
                        if ahead >= 2:
                            att.act_stack(act, b + 2, p)

                    self_batches(act, body)
                    flip_out(B - 1)

                @block.tensor
                def _(pe):
                    def flip(b):
                        att.pe_flip(pe, bank_ms, summed, b, o_flipped)

                    def turn(b):
                        await_(pe, normed, b)
                        for qt in range(QT):
                            last = nc.tensor.transpose(bank_ms[:, S + qt * P:S + (qt + 1) * P], xn[:, qt, :], ident)
                        last.then_inc(turned.sem, 1)

                    def project(b):
                        await_(pe, turned_out, b)
                        for s in range(2):
                            last = nc.tensor.matmul(bank_ms[:, s * S:(s + 1) * S], wqk[:, s * D:(s + 1) * D], xnt[:],
                                                    start=True, stop=True)
                        last.then_inc(projected.sem, 1)

                    def values(b):
                        await_(pe, qk_out, b)
                        for qt in range(QT):
                            last = nc.tensor.matmul(bank_ms[:, qt * 2 * D:(qt + 1) * 2 * D], xnt[:, qt * P:(qt + 1) * P],
                                                    wv2[:].rearrange("p c d -> p (c d)"), start=True, stop=True)
                        last.then_inc(v_done.sem, 1)

                    def extras(b):
                        await_(pe, vc_out, b)
                        for qt in range(QT):
                            o = bank[1][:, qt * D:(qt + 1) * D]
                            last = nc.tensor.matmul(o, xnt[:, qt * P:(qt + 1) * P], wvs[:], start=True, stop=False)
                            for kt in range(qt + 1):
                                last = nc.tensor.matmul(o, neg_uniform[:, kt, qt * P:(qt + 1) * P], v_centre[:, kt, :],
                                                        start=False, stop=(kt == qt))
                        last.then_inc(extra.sem, 1)

                    def output(b):
                        await_(pe, o_flipped_out, b)
                        for qt in range(QT):
                            last = nc.tensor.matmul(bank_pv[:, S + qt * D:S + (qt + 1) * D], o_feat[:, qt * P:(qt + 1) * P], wproj[:],
                                                    start=True, stop=True)
                        last.then_inc(o_proj.sem, 1)

                    def prepare(b):
                        turn(b)
                        project(b)
                        values(b)
                        att.pe_stack(pe, b, 0)
                        att.pe_stack(pe, b, 1)
                        extras(b)

                    def maxima(b, p, lane, pieces=None):
                        if lane == 0:
                            await_(pe, extra_out, b)
                            if not (isinstance(b, int) and b == 0):
                                await_(pe, att.m_lo, b - 1)
                        att.pe_max(pe, b, p, lane, pieces)

                    prepare(0)
                    for lane in range(HL):
                        maxima(0, 0, lane)
                    att.pe_turn_max(pe, 0, 0)
                    await_(pe, v_out, 0)
                    prepare(1)

                    def body(b, p, before, ahead):
                        def scores(lane):
                            if lane == 0 and ahead >= 1:
                                await_(pe, att.q_ready, b + 1)
                            att.pe_scores(pe, b, p, lane, [0])
                            if ahead >= 1:
                                maxima(b + 1, 1 - p, lane, slice(0, 2))
                            att.pe_scores(pe, b, p, lane, [1])
                            if ahead >= 1:
                                att.pe_max(pe, b + 1, 1 - p, lane, slice(2, 3))

                        scores(0)
                        scores(1)
                        if before:
                            flip(b - 1)
                        elif ahead >= 2:
                            await_(pe, v_out, b + 1)
                        if ahead >= 2:
                            turn(b + 2)
                        att.pe_values(pe, b, p, 0)
                        scores(2)
                        if ahead >= 2:
                            project(b + 2)
                        if before:
                            await_(pe, att.pv_out, b, 1)
                            output(b - 1)
                        att.pe_values(pe, b, p, 1)
                        scores(3)
                        if ahead >= 2:
                            values(b + 2)
                        if before:
                            await_(pe, x_added, b - 1)
                        att.pe_values(pe, b, p, 2)
                        att.pe_values(pe, b, p, 3)
                        if ahead >= 1:
                            att.pe_turn_max(pe, b + 1, 1 - p)
                        if ahead >= 2:
                            att.pe_stack(pe, b + 2, 0)
                            att.pe_stack(pe, b + 2, 1)
                            await_(pe, v_out, b + 2)
                        att.pe_turn_out(pe, b)
                        if ahead >= 2:
                            extras(b + 2)

                    self_batches(pe, body)
                    flip(B - 1)
                    output(B - 1)

                @block.vector
                def _(dve):
                    def normalise(b):
                        dve.wait_ge(turned.sem, b + 1)
                        for qt in range(QT):
                            n = b * QT + qt
                            nc.vector.tensor_scalar(xn[:, qt, :], xres[:, bass.ds(n, 1), :].rearrange("p a d -> p (a d)"),
                                                    mv[:, bass.ds(n, 1), 0:1].rearrange("p a c -> p (a c)"),
                                                    rstd[:, bass.ds(n, 1)], ALU.subtract, ALU.mult).then_inc(normed.sem, 1)

                    def projected_out(b):
                        await_(dve, projected, b)
                        nc.vector.tensor_scalar(qk[:, 0], bank_ms[:, 0:S], qk_bias[:, 0:1], SCALE, ALU.add, ALU.mult).then_inc(qk_out.sem, 1)
                        nc.vector.tensor_scalar(qk[:, 1], bank_ms[:, S:2 * S], qk_bias[:, 1:2], None, ALU.add).then_inc(qk_out.sem, 1)

                    def low(b):
                        await_(dve, att.hi, b)
                        nc.vector.tensor_tensor(qk_lo[:], qk[:], qk_hi[:].bitcast(F32), ALU.subtract).then_inc(att.lo.sem, 1)

                    def centre_out(b):
                        await_(dve, v_done, b)
                        nc.vector.tensor_copy(v_centre[:], bank_ms[:].rearrange("p (q c d) -> p q c d", q=QT, c=2)[:, :, 1]).then_inc(vc_out.sem, 1)

                    def extras_out(b, p):
                        await_(dve, extra, b)
                        nc.vector.tensor_copy(v_extra[p][:].rearrange("p q d -> p (q d)"), bank[1][:, 0:QT * D]).then_inc(extra_out.sem, 1)

                    def residual(b):
                        await_(dve, o_proj, b)
                        xb = xres[:, bass.ds(b * QT, QT), :]
                        nc.vector.tensor_tensor(xb, xb, bank_pv[:, S:S + QT * D].rearrange("p (q d) -> p q d", q=QT),
                                                ALU.add).then_inc(x_added.sem, 1)

                    def prepare(b, p):
                        normalise(b)
                        projected_out(b)
                        low(b)
                        centre_out(b)
                        att.dve_stack(dve, b, p)
                        extras_out(b, p)

                    dve.sem_inc(turned.sem, 1)
                    prepare(0, 0)
                    for lane in range(HL):
                        att.dve_max(dve, 0, 0, lane)
                    att.dve_split_max(dve, 0)
                    prepare(1, 1)

                    def body(b, p, before, ahead):
                        if ahead >= 2:
                            normalise(b + 2)
                        if ahead >= 1:
                            att.dve_max(dve, b + 1, 1 - p, 0)
                            att.dve_max(dve, b + 1, 1 - p, 1)
                        att.dve_values(dve, b, p, 0)
                        if ahead >= 1:
                            att.dve_max(dve, b + 1, 1 - p, 2)
                        if ahead >= 2:
                            projected_out(b + 2)
                        att.dve_values(dve, b, p, 1)
                        if before:
                            residual(b - 1)
                        if ahead >= 1:
                            att.dve_max(dve, b + 1, 1 - p, 3)
                        if ahead >= 2:
                            low(b + 2)
                            centre_out(b + 2)
                        att.dve_values(dve, b, p, 2)
                        att.dve_values(dve, b, p, 3)
                        if ahead >= 1:
                            att.dve_split_max(dve, b + 1)
                        if ahead >= 2:
                            att.dve_stack(dve, b + 2, p)
                        att.dve_divide(dve, b)
                        await_(dve, att.o_norm, b)
                        await_(dve, extra_out, b)
                        nc.vector.tensor_tensor(o_tok[:], o_tok[:], v_extra[p][:], ALU.add).then_inc(summed.sem, 1)
                        if ahead >= 2:
                            await_(dve, summed, b)
                            extras_out(b + 2, p)

                    self_batches(dve, body)
                    residual(B - 1)

        def normalise_and_turn(name, dst):
            with nc.sbuf_tensor(name + "_xn", [P, TILES, D], F32) as xa:
                norm = Norm(name)
                scaled, turned, out_act, out_dve = (sem(name + x) for x in ("_scaled", "_turned", "_out_act", "_out_dve"))
                with nc.Block() as block:
                    @block.vector
                    def _(dve):
                        norm.moments(dve)
                        norm.reciprocal_root(dve)
                        dve.wait_ge(norm.done, 7)
                        for n in range(TILES):
                            nc.vector.tensor_scalar(xa[:, n, :], xres[:, n, :], mv[:, n, 0:1], rstd[:, n:n + 1],
                                                    ALU.subtract, ALU.mult).then_inc(scaled, 1)
                        for r in (1, 3):
                            dve.wait_ge(turned, r + 1)
                            nc.vector.tensor_copy(dst[:, 512 * r:512 * (r + 1)], banks[r]).then_inc(out_dve, 1)

                    @block.scalar
                    def _(act):
                        norm.square_root(act)
                        for r in (0, 2):
                            act.wait_ge(turned, r + 1)
                            nc.scalar.activation(dst[:, 512 * r:512 * (r + 1)], banks[r], ACT.Copy).then_inc(out_act, 1)

                    @block.tensor
                    def _(pe):
                        for n in range(TILES):
                            pe.wait_ge(scaled, n + 1)
                            last = nc.tensor.transpose(banks[n // 4][:, (n % 4) * P:(n % 4 + 1) * P], xa[:, n, :], ident)
                            if n % 4 == 3:
                                last.then_inc(turned, 1)

        class Splines:

            def __init__(self, name, pctx):
                def psb(n, shape):
                    return pctx.enter_context(nc.sbuf_tensor(f"{name}_{n}", shape, F32))
                self.near, self.far, self.near2, self.far2, self.tanh = \
                    (psb(n, [P, 512]) for n in ("near", "far", "near2", "far2", "tanh"))
                self.us = [psb(f"u{n}", [P, 512]) for n in range(2)]
                self.planes = [psb(f"planes{n}", [P, KP, 512]) for n in range(2)]
                self.folded = event(name + "_folded", 4)
                self.u_out = event(name + "_u_out", 4)
                self.clipped = event(name + "_clipped", 8)
                self.squared = event(name + "_squared", 8)
                self.cubed = event(name + "_cubed", 8)
                self.basis = event(name + "_basis", 4)
                self.masked = event(name + "_masked", 4)
                self.tanh_out = event(name + "_tanh_out")
                self.ready = event(name + "_ready")

            def credit(self, dve):
                dve.sem_inc(self.masked.sem, 2)
                dve.sem_inc(self.ready.sem, 1)

            def pe_wait(self, pe, b):
                pe.wait_ge(self.ready.sem, b + 2)

            def act_fold(self, act, b, k, x):
                act.wait_ge(self.masked.sem, 4 * b + k + 1)
                take_wait(act)
                nc.scalar.activation(self.us[k % 2][:].rearrange("p (s q) -> p s q", s=x.shape[1]), x, ACT.Abs,
                                     bias=abs_bias[:, k:k + 1], scale=1.0 / H_GRID).then_inc(self.folded.sem, 1)
                await_(act, self.folded, b, k + 1)
                nc.scalar.activation(self.us[k % 2][:], self.us[k % 2][:], ACT.Abs, bias=abs_bias[:, 4:5]).then_inc(self.u_out.sem, 1)

            def act_square(self, act, b, k):
                for n, (src, dst) in enumerate(((self.far, self.far2), (self.near, self.near2))):
                    await_(act, self.clipped, b, 2 * k + n + 1)
                    nc.scalar.activation(dst[:], src[:], ACT.Square).then_inc(self.squared.sem, 1)

            def act_tanh(self, act, b, x):
                act.wait_ge(self.ready.sem, b + 1)
                take_wait(act)
                nc.scalar.activation(self.tanh[:].rearrange("p (s q) -> p s q", s=x.shape[1]), x, ACT.Tanh, scale=0.5).then_inc(self.tanh_out.sem, 1)

            def dve_clip(self, dve, b, k):
                await_(dve, self.u_out, b, k + 1)
                nc.vector.tensor_scalar(self.far[:], self.us[k % 2][:], 2.0, -2.0, ALU.min, ALU.add).then_inc(self.clipped.sem, 1)
                nc.vector.tensor_scalar(self.near[:], self.us[k % 2][:], 1.0, -1.0, ALU.min, ALU.add).then_inc(self.clipped.sem, 1)

            def dve_cube(self, dve, b, k, x, q):
                s = x.shape[1]
                await_(dve, self.squared, b, 2 * k + 1)
                nc.vector.tensor_tensor(self.far[:], self.far[:], self.far2[:], ALU.mult).then_inc(self.cubed.sem, 1)
                await_(dve, self.squared, b, 2 * k + 2)
                nc.vector.scalar_tensor_tensor(out=self.near[:], in0=self.near[:], scalar=4.0, in1=self.near2[:],
                                               op0=ALU.mult, op1=ALU.mult).then_inc(self.cubed.sem, 1)
                await_(dve, self.cubed, b, 2 * k + 2)
                nc.vector.tensor_tensor(self.us[k % 2][:], self.near[:], self.far[:], ALU.subtract).then_inc(self.basis.sem, 1)
                await_(dve, self.basis, b, k + 1)
                for plane, side in ((k, ALU.is_lt), (k + 4, ALU.is_ge)):
                    last = nc.vector.scalar_tensor_tensor(out=self.planes[q][:, plane].rearrange("p (s q) -> p s q", s=s), in0=x,
                                                          scalar=H_GRID * (k - 1.5), in1=self.us[k % 2][:].rearrange("p (s q) -> p s q", s=s),
                                                          op0=side, op1=ALU.mult)
                last.then_inc(self.masked.sem, 1)

            def dve_silu(self, dve, b, x, q):
                s = x.shape[1]
                await_(dve, self.tanh_out, b)
                nc.vector.scalar_tensor_tensor(out=self.planes[q][:, NB].rearrange("p (s q) -> p s q", s=s),
                                               in0=self.tanh[:].rearrange("p (s q) -> p s q", s=s),
                                               scalar=1.0, in1=x, op0=ALU.add, op1=ALU.mult).then_inc(self.ready.sem, 1)

            def act_all(self, act, b, x):
                self.act_fold(act, b, 0, x)
                for k in range(4):
                    if k < 3:
                        self.act_fold(act, b, k + 1, x)
                    self.act_square(act, b, k)
                self.act_tanh(act, b, x)

            def dve_all(self, dve, b, x, q):
                for k in range(4):
                    self.dve_clip(dve, b, k)
                    self.dve_cube(dve, b, k, x, q)
                self.dve_silu(dve, b, x, q)

        normalise_and_turn("norm2", xt[:, 0])
        with ExitStack() as lctx:
            kan = Splines("kan", lctx)
            rope_a = lctx.enter_context(nc.sbuf_tensor("rope_a", [P, 2, S], F32))
            rope_b = lctx.enter_context(nc.sbuf_tensor("rope_b", [P, 2, S], F32))

            att = Attention("cross", causal=False, out_banks=banks[2:4])
            qk_kan = event("qk_kan")
            v_kan = event("v_kan", QT)
            v_kan_out = event("v_kan_out", QT)
            qk_kan_out = event("qk_kan_out")
            rotated = event("rotated")
            roped = event("roped", 3)
            c_flipped = event("c_flipped")
            c_flipped_out = event("c_flipped_out")

            def kan_input(b):
                return xt[:, :, bass.ds(b * S, S)]

            parts = [(c, s) for c in range(KP) for s in range(2)]
            planes = [a[:].rearrange("p c (s q) -> p c s q", s=2) for a in kan.planes]
            flat = "p s q -> p (s q)"

            def cross_batches(eng, body):
                n = (B - 3) // 2
                with eng.Fori(0, n) as i:
                    for p in range(2):
                        body(2 * i + p, p, 3)
                for b in range(2 * n, B):
                    body(b, b % 2, B - 1 - b)

            with nc.Block() as block:
                @block.sync
                def _(sp):
                    att.dma_max(sp, 0, 0)

                    def body(b, p, ahead):
                        if ahead >= 1:
                            att.dma_max(sp, b + 1, 1 - p)

                    cross_batches(sp, body)

                @block.scalar
                def _(act):
                    def projected_out(b):
                        await_(act, qk_kan, b)
                        nc.scalar.activation(qk[:].rearrange(flat), bank_ms[:], ACT.Copy).then_inc(qk_kan_out.sem, 1)

                    def value_out(b, p, qt):
                        await_(act, v_kan, b, qt + 1)
                        nc.scalar.activation(v_aug[p][:, qt, :, 0:HD], banks[4 + qt][:, 0:D].rearrange("p (h d) -> p h d", d=HD), ACT.Copy).then_inc(v_kan_out.sem, 1)

                    def high(b):
                        await_(act, roped, b)
                        nc.scalar.activation(qk_hi[:].rearrange(flat), qk[:].rearrange(flat), ACT.Copy).then_inc(att.hi.sem, 1)

                    def project(b, p):
                        projected_out(b)
                        value_out(b, p, 0)
                        high(b)
                        value_out(b, p, 1)
                        att.act_stack(act, b, p)

                    act.sem_inc(c_flipped_out.sem, 1)
                    kan.act_all(act, 0, kan_input(0))
                    kan.act_all(act, 1, kan_input(1))
                    project(0, 0)
                    att.act_split_max(act, 0)
                    kan.act_all(act, 2, kan_input(2))
                    project(1, 1)

                    def body(b, p, ahead):
                        if ahead >= 3:
                            kan.act_fold(act, b + 3, 0, kan_input(b + 3))
                        for lane in range(HL):
                            att.act_exp(act, b, p, lane)
                            if ahead >= 3:
                                kan.act_square(act, b + 3, lane)
                                if lane + 1 < HL:
                                    kan.act_fold(act, b + 3, lane + 1, kan_input(b + 3))
                        if ahead >= 2:
                            projected_out(b + 2)
                        if ahead >= 1:
                            att.act_split_max(act, b + 1)
                        if ahead >= 3:
                            kan.act_tanh(act, b + 3, kan_input(b + 3))
                        if ahead >= 2:
                            value_out(b + 2, p, 0)
                            high(b + 2)
                            value_out(b + 2, p, 1)
                            att.act_stack(act, b + 2, p)
                        await_(act, c_flipped, b)
                        take_wait(act)
                        nc.scalar.activation(xt[:, 0, bass.ds(b * S, S)], bank_ms[:, 0:S], ACT.Copy).then_inc(c_flipped_out.sem, 1)

                    cross_batches(act, body)

                @block.tensor
                def _(pe):
                    def project(b, p, piece):
                        x, half = divmod(piece, 2)
                        if piece == 0:
                            kan.pe_wait(pe, b)
                        n = len(parts) // 2
                        for c, s in parts[half * n:(half + 1) * n]:
                            last = nc.tensor.matmul(bank_ms[:, x * S:(x + 1) * S], kan_w[:, s, c, x * D:(x + 1) * D], planes[p][:, c, s],
                                                    start=((c, s) == parts[0]), stop=((c, s) == parts[-1]), skip_group_check=True)
                        if piece == 3:
                            last.then_inc(qk_kan.sem, 1)

                    def values(b, p, qt):
                        for c, s in parts:
                            last = nc.tensor.matmul(banks[4 + qt][:, 0:D], planes[p][:, c, s, qt * P:(qt + 1) * P], kan_w[:, s, c, 2 * D:3 * D],
                                                    start=((c, s) == parts[0]), stop=((c, s) == parts[-1]))
                        last.then_inc(v_kan.sem, 1)

                    def rotate(b):
                        await_(pe, qk_kan_out, b)
                        nc.tensor.matmul(bank[1][:], cst("rope_rot"), qk[:].rearrange(flat), start=True, stop=True).then_inc(rotated.sem, 1)

                    def stacks(b):
                        att.pe_stack(pe, b, 0)
                        await_(pe, v_kan_out, b)
                        att.pe_stack(pe, b, 1)

                    def prologue(b, p):
                        for piece in range(4):
                            project(b, p, piece)
                        values(b, p, 0)
                        rotate(b)
                        values(b, p, 1)
                        stacks(b)

                    def maxima(b, p, lane, pieces=None):
                        if lane == 0 and not (isinstance(b, int) and b == 0):
                            await_(pe, att.m_lo, b - 1)
                        att.pe_max(pe, b, p, lane, pieces)

                    prologue(0, 0)
                    for lane in range(HL):
                        maxima(0, 0, lane)
                    att.pe_turn_max(pe, 0, 0)
                    prologue(1, 1)

                    def body(b, p, ahead):
                        def scores(lane):
                            if lane == 0 and ahead >= 1:
                                await_(pe, att.q_ready, b + 1)
                            if lane == 0:
                                att.pe_scores(pe, b, p, lane, [0])
                            if ahead >= 1:
                                maxima(b + 1, 1 - p, lane, slice(0, 2))
                            if lane > 0:
                                att.pe_scores(pe, b, p, lane, [0])
                            att.pe_scores(pe, b, p, lane, [1])
                            if ahead >= 1:
                                att.pe_max(pe, b + 1, 1 - p, lane, slice(2, 4))

                        scores(0)
                        pe.wait_ge(c_flipped_out.sem, b + 1)
                        for lane in range(HL):
                            if lane + 1 < HL:
                                scores(lane + 1)
                            if ahead >= 2:
                                project(b + 2, p, lane)
                            att.pe_values(pe, b, p, lane)
                        if ahead >= 1:
                            att.pe_turn_max(pe, b + 1, 1 - p)
                        if ahead >= 2:
                            values(b + 2, p, 0)
                            rotate(b + 2)
                        att.pe_turn_out(pe, b)
                        if ahead >= 2:
                            values(b + 2, p, 1)
                            stacks(b + 2)
                        att.pe_flip(pe, bank_ms, att.o_norm, b, c_flipped)

                    cross_batches(pe, body)

                @block.vector
                def _(dve):
                    def rope(b):
                        await_(dve, qk_kan_out, b)
                        nc.vector.tensor_tensor(rope_a[:].rearrange(flat), qk[:].rearrange(flat), cosv, ALU.mult).then_inc(roped.sem, 1)
                        await_(dve, rotated, b)
                        nc.vector.tensor_tensor(rope_b[:].rearrange(flat), bank[1][:], sinv, ALU.mult).then_inc(roped.sem, 1)
                        await_(dve, roped, b, 2)
                        nc.vector.tensor_tensor(qk[:], rope_a[:], rope_b[:], ALU.add).then_inc(roped.sem, 1)

                    def low(b):
                        await_(dve, att.hi, b)
                        nc.vector.tensor_tensor(qk_lo[:], qk[:], qk_hi[:].bitcast(F32), ALU.subtract).then_inc(att.lo.sem, 1)

                    def project(b, p):
                        rope(b)
                        low(b)
                        att.dve_stack(dve, b, p)

                    kan.credit(dve)
                    kan.dve_all(dve, 0, kan_input(0), 0)
                    kan.dve_all(dve, 1, kan_input(1), 1)
                    project(0, 0)
                    for lane in range(HL):
                        att.dve_max(dve, 0, 0, lane)
                    att.dve_split_max(dve, 0)
                    kan.dve_all(dve, 2, kan_input(2), 0)
                    project(1, 1)

                    def body(b, p, ahead):
                        if ahead >= 1:
                            att.dve_max(dve, b + 1, 1 - p, 0)
                        for lane in range(HL):
                            if ahead >= 3:
                                kan.dve_clip(dve, b + 3, lane)
                            if ahead >= 1 and lane + 1 < HL:
                                att.dve_max(dve, b + 1, 1 - p, lane + 1)
                            if ahead >= 3:
                                kan.dve_cube(dve, b + 3, lane, kan_input(b + 3), 1 - p)
                            att.dve_values(dve, b, p, lane)
                        if ahead >= 1:
                            att.dve_split_max(dve, b + 1)
                        if ahead >= 3:
                            kan.dve_silu(dve, b + 3, kan_input(b + 3), 1 - p)
                        if ahead >= 2:
                            rope(b + 2)
                        att.dve_divide(dve, b)
                        if ahead >= 2:
                            low(b + 2)
                            att.dve_stack(dve, b + 2, p)

                    cross_batches(dve, body)
        actx.close()

        CH = 512
        CT = CH // P
        NCH = TILES // CT
        with ExitStack() as lctx:
            kano = Splines("kano", lctx)
            ko_done = event("ko_done")
            ko_added = event("ko_added")

            def ctx_input(c):
                return xt[:, 0:1, bass.ds(c * CH, CH)]

            with nc.Block() as block:
                @block.scalar
                def _(act):
                    with act.Fori(0, NCH) as c:
                        kano.act_all(act, c, ctx_input(c))

                @block.tensor
                def _(pe):
                    with pe.Fori(0, NCH) as c:
                        kano.pe_wait(pe, c)
                        pe.wait_ge(ko_added.sem, c + 1)
                        for n in range(CT):
                            for k in range(KP):
                                last = nc.tensor.matmul(bank[0][:, n * P:(n + 1) * P], kano.planes[0][:, k, n * P:(n + 1) * P], kan_wo[:, k, :],
                                                        start=(k == 0), stop=(k == KP - 1))
                        last.then_inc(ko_done.sem, 1)

                @block.vector
                def _(dve):
                    kano.credit(dve)
                    dve.sem_inc(ko_added.sem, 1)
                    with dve.Fori(0, NCH) as c:
                        kano.dve_all(dve, c, ctx_input(c), 0)
                        await_(dve, ko_done, c)
                        xc = xres[:, bass.ds(c * CT, CT), :]
                        nc.vector.tensor_tensor(xc, xc, bank[0][:].rearrange("p (n d) -> p n d", n=CT), ALU.add).then_inc(ko_added.sem, 1)

        normalise_and_turn("norm3", xt[:, 0])
        with ExitStack() as lctx:
            act_h = lctx.enter_context(nc.sbuf_tensor("act_h", [P, FT, CH], F32))
            gate_up = event("gate_up", 2 * FT)
            silu_out = event("silu_out", FT)
            h_out = event("h_out", FT)
            down = event("down")
            y_out = event("y_out")
            stored = event("stored", 1, 16)
            gate_bank = [banks[0], banks[1], banks[2]]
            up_bank = [banks[3], banks[4], banks[5]]
            with nc.Block() as block:
                @block.sync
                def _(sp):
                    with sp.Fori(0, NCH) as c:
                        sp.wait_ge(y_out.sem, c + 2)
                        sp.dma_start(out.rearrange("b (t p) d -> p (b t) d", p=P)[:, bass.ds(c * CT, CT), :],
                                     xres[:, bass.ds(c * CT, CT), :]).then_inc(stored.sem, 16)
                    sp.wait_ge(stored.sem, 16 * NCH)

                @block.scalar
                def _(act):
                    with act.Fori(0, NCH) as c:
                        for f in range(FT):
                            await_(act, gate_up, c, 2 * f + 1)
                            nc.scalar.activation(act_h[:, f, :], gate_bank[f], ACT.Silu).then_inc(silu_out.sem, 1)

                @block.tensor
                def _(pe):
                    with pe.Fori(0, NCH) as c:
                        xc = xt[:, 0, bass.ds(c * CH, CH)]
                        for f in range(FT):
                            nc.tensor.matmul(gate_bank[f], w_gate[:, f * P:(f + 1) * P], xc, start=True, stop=True).then_inc(gate_up.sem, 1)
                            nc.tensor.matmul(up_bank[f], w_up[:, f * P:(f + 1) * P], xc, start=True, stop=True).then_inc(gate_up.sem, 1)
                        await_(pe, h_out, c)
                        pe.wait_ge(y_out.sem, c + 1)
                        for n in range(CT):
                            for f in range(FT):
                                last = nc.tensor.matmul(bank_pv[:, n * P:(n + 1) * P], act_h[:, f, n * P:(n + 1) * P], w_down[:, f, :],
                                                        start=(f == 0), stop=(f == FT - 1))
                        last.then_inc(down.sem, 1)

                @block.vector
                def _(dve):
                    dve.sem_inc(y_out.sem, 1)
                    with dve.Fori(0, NCH) as c:
                        for f in range(FT):
                            await_(dve, silu_out, c, f + 1)
                            await_(dve, gate_up, c, 2 * f + 2)
                            nc.vector.tensor_tensor(act_h[:, f, :], act_h[:, f, :], up_bank[f], ALU.mult).then_inc(h_out.sem, 1)
                        await_(dve, down, c)
                        xc = xres[:, bass.ds(c * CT, CT), :]
                        nc.vector.tensor_tensor(xc, xc, bank_pv[:].rearrange("p (n d) -> p n d", n=CT), ALU.add).then_inc(y_out.sem, 1)


_OUTS = ((B, S, D), "float32")


def kernel(**inputs):
    import concourse.bacc as bacc
    from concourse.bass_utils import run_bass_kernel_spmd

    nc = bacc.Bacc("TRN2", target_bir_lowering=False, num_devices=1)
    arrays = {n: np.ascontiguousarray(a) for n, a in inputs.items()}
    arrays |= {"const": CONST, "const_staged": CONST_STAGED}
    aps = {n: nc.dram_tensor(f"in_{n}_dram", a.shape, mybir.dt.from_np(a.dtype), kind="ExternalInput").ap()
           for n, a in arrays.items()}
    out = nc.dram_tensor("out_dram", (B, S, D), F32, kind="ExternalOutput").ap()
    build(nc, aps, out)
    r = run_bass_kernel_spmd(nc, [{f"in_{n}_dram": a for n, a in arrays.items()}], core_ids=[0])
    return r.results[0]["out_dram"]
```

```python
from contextlib import ExitStack

import numpy as np

import concourse.bass as bass
from concourse import mybir
from concourse.alu_op_type import AluOpType as ALU

ACT = mybir.ActivationFunctionType
F32 = mybir.dt.float32
F32R = mybir.dt.float32r
BF16 = mybir.dt.bfloat16
I32 = mybir.dt.int32
AX = mybir.AxisListType

B, S, D, H = 8, 256, 128, 16
P = 128
HD = D // H
TILES = B * S // P
QT = S // P
HL = 4
HG = H // HL
ROWS = P // HL
KROWS = 3 * HD + 2
NB = 8
KP = NB + 1
FT = 3
LEAST = -3.0e38
NEG = -1.0e30
EPS = 1e-5
H_GRID = 0.4
SCALE = 1.0 / float(np.sqrt(HD))


def constants():
    p, q = np.arange(P)[:, None], np.arange(P)[None, :]
    causal_q = np.where(q <= p, 0.0, NEG)
    causal_k = np.where(q >= p, 0.0, NEG)
    sel_hi, sel_lo_q, sel_hi_k, sel_lo_k = (np.zeros((P, HG, P)) for _ in range(4))
    for g in range(HG):
        for l in range(HL):
            for d in range(HD):
                f, r = (g * HL + l) * HD + d, l * ROWS + d
                sel_hi[f, g, r] = sel_hi[f, g, r + 2 * HD] = 1
                sel_lo_q[f, g, r + HD] = 1
                sel_hi_k[f, g, r] = sel_hi_k[f, g, r + HD] = 1
                sel_lo_k[f, g, r + 2 * HD] = 1
    rope_rot = np.zeros((P, P))
    for f in range(0, P, 2):
        rope_rot[f + 1, f] = -1
        rope_rot[f, f + 1] = 1
    inv = np.float32(1.0) / np.float32(10000.0) ** (np.arange(0, HD, 2, dtype=np.float32) / np.float32(HD))
    angle = np.arange(S, dtype=np.float32)[:, None] * inv[None, :].astype(np.float32)
    cos = np.tile(np.repeat(np.cos(angle), 2, axis=1).T, (H, 1))
    sin = np.tile(np.repeat(np.sin(angle), 2, axis=1).T, (H, 1))
    cos2 = np.concatenate([cos * SCALE, cos], axis=1)
    sin2 = np.concatenate([sin * SCALE, sin], axis=1)
    s = np.arange(S)
    uni = np.where(s[:, None] <= s[None, :], -1.0 / (s[None, :] + 1), 0.0)
    neg_uniform = uni.reshape(QT, P, S).transpose(1, 0, 2)
    ones_rows = np.zeros((P, 1))
    ones_rows[[l * ROWS + r for l in range(HL) for r in (3 * HD, 3 * HD + 1)]] = 1
    k = np.arange(4)
    abs_bias = np.tile(np.concatenate([1.5 - k, [-2.0, 2.0, 1.0]])[None, :], (P, 1))
    parts = [("ident", np.eye(P)), ("causal_q", causal_q), ("causal_k", causal_k),
             ("sel_hi", sel_hi), ("sel_lo_q", sel_lo_q), ("sel_hi_k", sel_hi_k), ("sel_lo_k", sel_lo_k),
             ("rope_rot", rope_rot), ("cos", cos2), ("sin", sin2), ("neg_uniform", neg_uniform),
             ("ones_rows", ones_rows), ("abs_bias", abs_bias)]
    staged = ("causal_q", "causal_k", "sel_hi", "sel_lo_q", "sel_hi_k", "sel_lo_k")
    at, kept, used = {}, [[], []], [0, 0]
    for name, a in parts:
        a, which = a.reshape(P, -1).astype(np.float32), int(name in staged)
        at[name] = (used[which], used[which] + a.shape[1])
        kept[which].append(a)
        used[which] += a.shape[1]
    return at, np.concatenate(kept[0], axis=1), np.concatenate(kept[1], axis=1)


CONST_AT, CONST, CONST_STAGED = constants()


class Event:

    def __init__(self, sem, per, unit=1):
        self.sem, self.per, self.unit = sem, per, unit

    def at(self, b, n=None):
        return (b * self.per + (self.per if n is None else n)) * self.unit


def build(nc, t, out):
    with ExitStack() as ctx:
        def sb(name, shape, dt=F32):
            return ctx.enter_context(nc.sbuf_tensor(name, shape, dt))

        def psum(name, shape):
            return ctx.enter_context(nc.psum_tensor(name, shape, F32))

        def sem(name):
            return ctx.enter_context(nc.semaphore(name))

        def event(name, per=1, unit=1):
            return Event(sem(name), per, unit)

        def await_(eng, ev, b, n=None):
            eng.wait_ge(ev.sem, ev.at(b, n))

        wait_taken = sem("wait_taken")

        def take_wait(act):
            act.sem_inc(wait_taken, 1)

        const = sb("const", [P, CONST.shape[1]])

        def cst(name):
            a, z = CONST_AT[name]
            return const[:, a:z]

        ident = cst("ident")
        ident_r = sb("ident_r", [P, P], F32R)
        ident_b = sb("ident_b", [P, P], BF16)
        causal_q_b = sb("causal_q_b", [P, P], BF16)
        causal_k_b = sb("causal_k_b", [P, P], BF16)
        sel_r = sb("sel_r", [P, 4, HG, P], F32R)
        sel_q_hi, sel_q_lo, sel_k_hi, sel_k_lo = (sel_r[:, n] for n in range(4))
        xres_room = sb("xres_room", [P, QT + TILES, D])
        xres = xres_room[:, QT:QT + TILES]
        cosv = cst("cos")
        sinv = cst("sin")
        neg_uniform = cst("neg_uniform").rearrange("p (k q) -> p k q", k=QT)
        ones_rows = cst("ones_rows")
        abs_bias = cst("abs_bias")
        wqk = sb("wqk", [P, 2 * D])
        wv2 = sb("wv2", [P, 2, D])
        wvs = sb("wvs", [P, D])
        wproj = sb("wproj", [P, D])
        qk_bias = sb("qk_bias", [P, 2])
        kan_w = sb("kan_w", [P, 2, KP, 3 * D])
        kan_wo = sb("kan_wo", [P, KP, D])
        w_gate = sb("w_gate", [P, FT * P])
        w_up = sb("w_up", [P, FT * P])
        w_down = sb("w_down", [P, FT, D])
        mask_q = sb("mask_q", [P, QT, S])
        mask_k = sb("mask_k", [P, 2, QT, S], F32R)
        xt_room = sb("xt_room", [P, S + 2 * TILES * P])
        xt = xt_room[:, S:S + 2 * TILES * P].rearrange("p (s q) -> p s q", s=2)
        ctx_qk = sb("ctx_qk", [P, B, 2 * S])
        stats = sb("stats", [P, TILES, 6])
        mv = sb("mv", [P, TILES, 2])
        rstd = sb("rstd", [P, TILES])
        rstd_a = sb("rstd_a", [P, TILES])
        rstd_b = sb("rstd_b", [P, TILES])
        eps_col = sb("eps_col", [P, 1])

        bank = [psum(f"bank{n}", [P, 512]) for n in range(2)]
        wide = [psum(f"wide{n}", [P, 1024]) for n in range(2)]
        bank_pv = psum("bank_pv", [P, 512])
        bank_ms = psum("bank_ms", [P, 512])
        banks = [bank[0][:], bank[1][:], wide[0][:, 0:512], wide[0][:, 512:1024],
                 wide[1][:, 0:512], wide[1][:, 512:1024], bank_pv[:], bank_ms[:]]

        class Norm:

            def __init__(self, name, t0, t1):
                self.tiles, self.at = range(t0, t1), slice(t0, t1)
                self.done, self.root = sem(name + "_done"), sem(name + "_root")

            def moments(self, dve):
                for n in self.tiles:
                    last = nc.vector.bn_stats(stats[:, n, :], xres[:, n, :])
                last.then_inc(self.done, 1)
                dve.wait_ge(self.done, 1)
                for n in self.tiles:
                    last = nc.vector.bn_aggr(mv[:, n, :], stats[:, n, :])
                last.then_inc(self.done, 1)

            def square_root(self, act):
                act.wait_ge(self.done, 2)
                nc.scalar.activation(rstd_a[:, self.at], mv[:, self.at, 1], ACT.Sqrt, bias=eps_col[:, 0:1]).then_inc(self.root, 1)

            def reciprocal_root(self, dve):
                r, b = rstd[:, self.at], rstd_b[:, self.at]
                dve.wait_ge(self.root, 1)
                nc.vector.reciprocal(r, rstd_a[:, self.at]).then_inc(self.done, 1)
                dve.wait_ge(self.done, 3)
                nc.vector.tensor_tensor(b, r, r, ALU.mult).then_inc(self.done, 1)
                dve.wait_ge(self.done, 4)
                nc.vector.scalar_tensor_tensor(out=b, in0=mv[:, self.at, 1], scalar=EPS, in1=b,
                                               op0=ALU.add, op1=ALU.mult).then_inc(self.done, 1)
                dve.wait_ge(self.done, 5)
                nc.vector.tensor_scalar(b, b, -0.5, 1.5, ALU.mult, ALU.add).then_inc(self.done, 1)
                dve.wait_ge(self.done, 6)
                nc.vector.tensor_tensor(r, r, b, ALU.mult).then_inc(self.done, 1)

        with ExitStack() as sctx:
            def ssb(name, shape, dt=F32):
                return sctx.enter_context(nc.sbuf_tensor(name, shape, dt))

            staged = ssb("staged", [P, CONST_STAGED.shape[1]])

            def stg(name):
                a, z = CONST_AT[name]
                return staged[:, a:z]

            spl = ssb("spl", [P, 3, 3 * D * NB])
            base = ssb("base", [P, 3, 3 * D])
            scaler = ssb("scaler", [P, 3, 3 * D])
            splo = ssb("splo", [P, D * NB])
            baseo = ssb("baseo", [P, D])
            scalero = ssb("scalero", [P, D])
            wint = ssb("wint", [P, 3, FT * P], I32)
            wflt = ssb("wflt", [P, 3, FT * P])
            gains = ssb("gains", [P, 3, H])
            vw = ssb("vw", [P, D])
            mask_n = ssb("mask_n", [P, QT, S])
            ctx_n = ssb("ctx_n", [P, TILES, D])
            maskt = ssb("maskt", [P, QT, S])

            ld = {n: sem("ld_" + n) for n in ("const", "x", "attn", "ffn", "mask", "ctx", "base", "out")}
            ld_spl = [sem(f"ld_spl{r}") for r in range(3)]
            pool_w = sem("pool_w")
            dve_spl = sem("dve_spl")
            dve_ffn = sem("dve_ffn")
            dve_out = sem("dve_out")
            norm1 = Norm("norm1", 0, TILES)
            ready = sem("ready")
            pe_tr = sem("pe_tr")
            evac_act = sem("evac_act")
            evac_dve = sem("evac_dve")

            def turns():
                for r4 in range(TILES // 4):
                    yield ([ctx_n[:, 4 * r4 + i, :] for i in range(4)], (ld["ctx"], 16),
                           xt[:, 1, 512 * r4:512 * (r4 + 1)], None)
                yield ([mask_n[:, qt, kt * P:(kt + 1) * P] for kt in range(QT) for qt in range(QT)],
                       (ld["mask"], 16), maskt[:].rearrange("p k q -> p (k q)"), None)
                for s in range(2):
                    yield ([base[:, r, s * P:(s + 1) * P] for r in range(3)], (pool_w, 1), kan_w[:, s, NB, :], "half features")
                for s in (1, 0):
                    for c in range(NB):
                        yield ([spl[:, r, s * P * NB + c:(s + 1) * P * NB:NB] for r in range(3)], (dve_spl, 6),
                               kan_w[:, s, c, :], "features")
                for n, dst in ((0, w_gate), (1, w_up)):
                    yield ([wflt[:, n, r * P:(r + 1) * P] for r in range(FT)], (dve_ffn, 1), dst[:], None)
                yield ([wflt[:, 2, r * P:(r + 1) * P] for r in range(FT)], (dve_ffn, 1),
                       w_down[:].rearrange("p r d -> p (r d)"), None)
                for c0 in (0, 4):
                    yield ([splo[:, c:D * NB:NB] for c in range(c0, c0 + 4)], (dve_out, 1),
                           kan_wo[:, c0:c0 + 4, :].rearrange("p c d -> p (c d)"), None)
                yield ([baseo[:]], (ld["out"], 48), kan_wo[:, NB, :], "half")

            jobs = list(turns())

            EARLY = TILES // 4 + 1 + 2 + 2 * NB

            def evacuate(eng, odd, first=0, end=len(jobs)):
                for n in range(first, end):
                    ins, _, dst, order = jobs[n]
                    if n % 2 != odd:
                        continue
                    src = banks[n % 8][:, 0:P * len(ins)]
                    half = 0.5 if order and "half" in order else 1.0
                    if order and "features" in order:
                        src = src.rearrange("p (h s d) -> p s h d", s=3, d=HD)
                        dst = dst.rearrange("p (s h d) -> p s h d", s=3, d=HD)
                    eng.wait_ge(pe_tr, n + 1)
                    if odd:
                        nc.vector.tensor_scalar(dst, src, half, None, ALU.mult).then_inc(evac_dve, 1)
                    else:
                        nc.scalar.activation(dst, src, ACT.Copy, scale=half).then_inc(evac_act, 1)

            with nc.Block() as block:
                @block.sync
                def _(sp):
                    sp.dma_start(const[:], t["const"]).then_inc(ld["const"], 16)
                    sp.dma_start(base[:], t["L0_xattn_qkv_base_w"].rearrange("(r p) i -> p r i", p=P)).then_inc(ld["base"], 16)
                    sp.dma_start(scaler[:], t["L0_xattn_qkv_scaler"].rearrange("(r p) i -> p r i", p=P)).then_inc(ld["base"], 16)
                    for r in range(3):
                        sp.dma_start(spl[:, r, :], t["L0_xattn_qkv_spline_w"][r * P:(r + 1) * P].rearrange("p i c -> p (i c)"),
                                     ).then_inc(ld_spl[r], 16)
                    sp.dma_start(splo[:], t["L0_xattn_out_spline_w"].rearrange("o i c -> o (i c)")).then_inc(ld["out"], 16)
                    sp.dma_start(baseo[:], t["L0_xattn_out_base_w"]).then_inc(ld["out"], 16)
                    sp.dma_start(scalero[:], t["L0_xattn_out_scaler"]).then_inc(ld["out"], 16)
                    sp.dma_start(wint[:, 0, :].rearrange("p (r d) -> p r d", r=FT), t["L0_ffn_w_gate"].rearrange("(r p) d -> p r d", p=P)).then_inc(ld["ffn"], 16)
                    sp.dma_start(wint[:, 1, :].rearrange("p (r d) -> p r d", r=FT), t["L0_ffn_w_up"].rearrange("(r p) d -> p r d", p=P)).then_inc(ld["ffn"], 16)
                    sp.dma_start(wint[:, 2, :], t["L0_ffn_w_down"]).then_inc(ld["ffn"], 16)

                @block.scalar
                def _(act):
                    act.dma_start(xres, t["x"].rearrange("b (t p) d -> p (b t) d", p=P)).then_inc(ld["x"], 16)
                    act.dma_start(ctx_n[:], t["ctx_1024"].rearrange("b (t p) d -> p (b t) d", p=P)).then_inc(ld["ctx"], 16)
                    act.dma_start(mask_n[:], t["mask_SxS2_ff0"].rearrange("(t p) k -> p t k", p=P)).then_inc(ld["mask"], 16)
                    act.dma_start(staged[:], t["const_staged"]).then_inc(ld["const"], 16)
                    norm1.square_root(act)
                    evacuate(act, 0)

                @block.gpsimd
                def _(pool):
                    names = ("resid", "centre", "skip")
                    for n, g in enumerate(names):
                        pool.dma_start(gains[:, n, :], t[f"L0_attn_{g}_gain"].rearrange("a h b c -> (a b c h)").partition_broadcast(P)).then_inc(ld["attn"], 16)
                    pool.dma_start(vw[:], t["L0_attn_v_w"]).then_inc(ld["attn"], 16)
                    pool.dma_start(wqk[:], t["L0_attn_qk_w"]).then_inc(ld["attn"], 16)
                    pool.dma_start(wproj[:], t["L0_attn_cproj_w"]).then_inc(ld["attn"], 16)
                    for s in range(2):
                        pool.dma_start(qk_bias[:, s:s + 1], t["L0_attn_qk_b"][s * P:(s + 1) * P].rearrange("(p o) -> p o", o=1)).then_inc(ld["attn"], 16)
                    pool.wait_ge(ld["base"], 32)
                    nc.gpsimd.tensor_tensor(base[:, :, P:2 * P], base[:, :, P:2 * P], base[:, :, 2 * P:3 * P], ALU.add).then_inc(pool_w, 1)

                @block.tensor
                def _(pe):
                    pe.wait_ge(ld["const"], 32)
                    for n, (ins, (s, v), _, _) in enumerate(jobs):
                        pe.wait_ge(s, v)
                        if n >= 8:
                            pe.wait_ge(evac_dve if n % 2 else evac_act, (n - 8) // 2 + 1)
                        for i, a in enumerate(ins):
                            last = nc.tensor.transpose(banks[n % 8][:, i * P:(i + 1) * P], a, ident)
                        last.then_inc(pe_tr, 1)

                @block.vector
                def _(dve):
                    def casts():
                        dve.wait_ge(ld["const"], 32)
                        nc.vector.tensor_copy(ident_r[:], ident)
                        nc.vector.tensor_copy(ident_b[:], ident)
                        nc.vector.tensor_copy(causal_q_b[:], stg("causal_q"))
                        nc.vector.tensor_copy(causal_k_b[:], stg("causal_k"))
                        for n, name in enumerate(("sel_hi", "sel_lo_q", "sel_hi_k", "sel_lo_k")):
                            nc.vector.tensor_copy(sel_r[:, n], stg(name).rearrange("p (g m) -> p g m", g=HG))

                    def mask_parts():
                        dve.wait_ge(ld["mask"], 16)
                        nc.vector.tensor_copy(mask_q[:], mask_n[:])
                        dve.wait_ge(evac_act, 3)
                        nc.vector.tensor_copy(mask_k[:, 0], maskt[:]).then_inc(ready, 1)
                        dve.wait_ge(ready, 1)
                        nc.vector.tensor_tensor(mask_k[:, 1], maskt[:], mask_k[:, 0].bitcast(F32), ALU.subtract)

                    nc.vector.memset(eps_col[:], EPS)
                    dve.wait_ge(ld["x"], 16)
                    norm1.moments(dve)
                    norm1.reciprocal_root(dve)
                    dve.wait_ge(ld["base"], 32)
                    for r in range(3):
                        if r == 1:
                            casts()
                        dve.wait_ge(ld_spl[r], 16)
                        v = spl[:, r, :].rearrange("p (i c) -> p i c", c=NB)
                        nc.vector.scalar_tensor_tensor(out=v, in0=v, scalar=1.0 / 6.0,
                                                       in1=scaler[:, r, :].unsqueeze(2).broadcast_to([P, 3 * D, NB]),
                                                       op0=ALU.mult, op1=ALU.mult).then_inc(dve_spl, 1)
                        dve.wait_ge(dve_spl, 2 * r + 1)
                        a, b, c = P * NB, 2 * P * NB, 3 * P * NB
                        nc.vector.tensor_tensor(spl[:, r, a:b], spl[:, r, a:b], spl[:, r, b:c], ALU.add).then_inc(dve_spl, 1)
                    evacuate(dve, 1, 0, EARLY)
                    mask_parts()
                    dve.wait_ge(ld["attn"], 16 * 8)
                    for n, dst in ((0, wv2[:, 0]), (1, wv2[:, 1]), (2, wvs[:])):
                        nc.vector.tensor_tensor(dst.rearrange("p (h d) -> p h d", d=HD), vw[:].rearrange("p (h d) -> p h d", d=HD),
                                                gains[:, n, :].unsqueeze(2).broadcast_to([P, H, HD]), ALU.mult)
                    dve.wait_ge(ld["ffn"], 48)
                    nc.vector.tensor_scalar(wflt[:], wint[:], float(np.float32(1.0 / 127.0)), None, ALU.mult).then_inc(dve_ffn, 1)
                    dve.wait_ge(ld["out"], 48)
                    nc.vector.scalar_tensor_tensor(out=splo[:].rearrange("p (i c) -> p i c", c=NB),
                                                   in0=splo[:].rearrange("p (i c) -> p i c", c=NB), scalar=1.0 / 6.0,
                                                   in1=scalero[:].unsqueeze(2).broadcast_to([P, D, NB]),
                                                   op0=ALU.mult, op1=ALU.mult).then_inc(dve_out, 1)
                    evacuate(dve, 1, EARLY)


        def asb(name, shape, dt=F32):
            return ctx.enter_context(nc.sbuf_tensor(name, shape, dt))

        qk = asb("qk", [P, 2, S])
        qk_hi = asb("qk_hi", [P, 2, S], F32R)
        qk_lo = asb("qk_lo", [P, 2, S], F32R)
        q_stack = [asb(f"q_stack{n}", [P, HG, S], F32R) for n in range(2)]
        k_stack = [asb(f"k_stack{n}", [P, HG, S], F32R) for n in range(2)]
        v_aug = [asb(f"v_aug{n}", [P, QT, H, ROWS]) for n in range(2)]
        row_max = [asb(f"row_max{n}", [P, QT, H]) for n in range(2)]
        max_hi = asb("max_hi", [H, S], F32R)
        max_lo = asb("max_lo", [H, S], F32R)
        probs = [asb(f"probs{n}", [P, QT * HG * S]) for n in range(2)]
        o_lane = asb("o_lane", [P, HL, S])
        rsum = asb("rsum", [P, QT, H])
        o_tok = asb("o_tok", [P, QT, D])
        o_feat = asb("o_feat", [P, S])

        class Attention:

            def __init__(self, name, causal, out_banks):
                self.causal = causal
                self.out_banks = out_banks
                self.sign = 1.0 if causal else -1.0
                self.max_pieces = HL * (3 if causal else 4)
                self.hi = event(name + "_hi")
                self.lo = event(name + "_lo")
                self.stacked = event(name + "_stacked", 2)
                self.q_ready = event(name + "_q_ready")
                self.k_ready = event(name + "_k_ready")
                self.s_ready = event(name + "_s_ready", self.max_pieces)
                self.s_max = event(name + "_s_max", self.max_pieces)
                self.m_turned = event(name + "_m_turned")
                self.m_hi = event(name + "_m_hi")
                self.m_lo = event(name + "_m_lo")
                self.m_placed = event(name + "_m_placed", 2, 16)
                self.e_ready = event(name + "_e_ready", 2 * HL)
                self.e_done = event(name + "_e_done", 2 * HL)
                self.pv = event(name + "_pv", HL)
                self.pv_out = event(name + "_pv_out", HL)
                self.o_turned = event(name + "_o_turned", QT)
                self.o_rsum = event(name + "_o_rsum", QT)
                self.o_norm = event(name + "_o_norm", QT)

            def pe_stack(self, pe, b, s):
                hi, lo = ((sel_q_hi, sel_q_lo), (sel_k_hi, sel_k_lo))[s]
                if s == 0:
                    await_(pe, self.hi, b)
                    await_(pe, self.lo, b)
                for g in range(HG):
                    o = wide[s][:, g * S:(g + 1) * S]
                    nc.tensor.matmul(o, hi[:, g], qk_hi[:, s], start=True, stop=False)
                    last = nc.tensor.matmul(o, lo[:, g], qk_lo[:, s], start=False, stop=True)
                last.then_inc(self.stacked.sem, 1)

            def act_stack(self, act, b, p):
                await_(act, self.stacked, b, 1)
                nc.scalar.activation(q_stack[p][:].rearrange("p g q -> p (g q)"), wide[0][:], ACT.Copy).then_inc(self.q_ready.sem, 1)

            def dve_stack(self, dve, b, p):
                await_(dve, self.stacked, b, 2)
                nc.vector.tensor_scalar(k_stack[p][:].rearrange("p g q -> p (g q)"), wide[1][:], ones_rows, None,
                                        ALU.add).then_inc(self.k_ready.sem, 1)

            def max_parts(self, lane):
                parts = [(0, 0, HG, P), (1, 0, 2, S), (1, 2, 2, S)] if self.causal else \
                        [(0, 0, 2, S), (0, 2, 2, S), (1, 0, 2, S), (1, 2, 2, S)]
                return [(lane * len(parts) + n, *x) for n, x in enumerate(parts)]

            def pe_max(self, pe, b, p, lane, pieces=slice(None)):
                if lane == 0:
                    await_(pe, self.q_ready, b)
                    await_(pe, self.k_ready, b)
                r = lane * ROWS
                for n, qt, g0, ng, keys in self.max_parts(lane)[pieces]:
                    o = bank[n % 2][:].rearrange("p (g k) -> p g k", g=ng)
                    if n >= 2:
                        await_(pe, self.s_max, b, n - 1)
                    if self.causal:
                        nc.tensor.matmul(o[:, :, keys - P:keys], ident_b[:],
                                         causal_q_b[:].unsqueeze(1).broadcast_to([P, ng, P]),
                                         start=True, stop=False, skip_group_check=True)
                    for g in range(ng):
                        last = nc.tensor.matmul(o[:, g, :], q_stack[p][r:r + 3 * HD, g0 + g, qt * P:(qt + 1) * P],
                                                k_stack[p][r:r + 3 * HD, g0 + g, 0:keys],
                                                start=(g == 0 and not self.causal), stop=(g == ng - 1), skip_group_check=True)
                    last.then_inc(self.s_ready.sem, 1)

            def dve_max(self, dve, b, p, lane, pieces=slice(None)):
                for n, qt, g0, ng, keys in self.max_parts(lane)[pieces]:
                    await_(dve, self.s_ready, b, n + 1)
                    a = lane * HG + g0
                    o = bank[n % 2][:].rearrange("p (g k) -> p g k", g=ng)
                    if self.causal:
                        nc.vector.tensor_reduce(row_max[p][:, qt, a:a + ng], o, AX.X, ALU.max, negate=True).then_inc(self.s_max.sem, 1)
                    else:
                        take_wait(dve)
                        for g in range(ng):
                            last = nc.vector.tensor_tensor_reduce(o[:, g, :], o[:, g, :], mask_q[:, qt], 1.0, LEAST, ALU.add, ALU.max,
                                                                  row_max[p][:, qt, a + g:a + g + 1])
                        last.then_inc(self.s_max.sem, 1)

            def pe_turn_max(self, pe, b, p):
                await_(pe, self.s_max, b)
                for qt in range(QT):
                    last = nc.tensor.transpose(bank[0][0:H, qt * P:(qt + 1) * P], row_max[p][:, qt, :], ident)
                last.then_inc(self.m_turned.sem, 1)

            def act_split_max(self, act, b):
                await_(act, self.m_turned, b)
                nc.scalar.activation(max_hi[:], bank[0][0:H, 0:S], ACT.Copy, scale=self.sign).then_inc(self.m_hi.sem, 1)

            def dve_split_max(self, dve, b):
                await_(dve, self.m_hi, b)
                nc.vector.scalar_tensor_tensor(out=max_lo[:], in0=bank[0][0:H, 0:S], scalar=self.sign, in1=max_hi[:].bitcast(F32),
                                               op0=ALU.mult, op1=ALU.subtract).then_inc(self.m_lo.sem, 1)

            def dma_max(self, sp, b, p):
                await_(sp, self.m_lo, b)
                for half, src in ((0, max_hi), (1, max_lo)):
                    sp.dma_start(q_stack[p][3 * HD + half:P:ROWS, :, :].bitcast(F32), src[:].bitcast(F32)).then_inc(self.m_placed.sem, 16)

            def queries(self, kt):
                return kt * P if self.causal else 0

            def probs_of(self, lane, kt):
                n = S - self.queries(kt)
                return probs[lane % 2][:, kt * HG * S:kt * HG * S + HG * n].rearrange("p (g q) -> p g q", g=HG)

            def pe_scores(self, pe, b, p, lane, kts=range(QT)):
                if lane == 0:
                    await_(pe, self.m_placed, b)
                r = lane * ROWS
                for kt in kts:
                    q0 = self.queries(kt)
                    n = S - q0
                    o = wide[kt][:, 0:HG * n].rearrange("p (g q) -> p g q", g=HG)
                    if lane:
                        await_(pe, self.e_done, b, 2 * lane - 1 + kt)
                    gs = 512 // n
                    for g0 in range(0, HG, gs):
                        ob = o[:, g0:g0 + gs, :]
                        if self.causal:
                            nc.tensor.matmul(ob[:, :, 0:P], ident_b[:], causal_k_b[:].unsqueeze(1).broadcast_to([P, gs, P]),
                                             start=True, stop=False, skip_group_check=True)
                        else:
                            for half in range(2):
                                nc.tensor.matmul(ob, ident_r[:], mask_k[:, half, kt].unsqueeze(1).broadcast_to([P, gs, S]),
                                                 start=(half == 0), stop=False, skip_group_check=True)
                        for g in range(g0, g0 + gs):
                            last = nc.tensor.matmul(o[:, g, :], k_stack[p][r:r + KROWS, g, kt * P:(kt + 1) * P],
                                                    q_stack[p][r:r + KROWS, g, q0:S],
                                                    start=False, stop=True, skip_group_check=True)
                    last.then_inc(self.e_ready.sem, 1)

            def act_exp(self, act, b, p, lane):
                for kt in range(QT):
                    await_(act, self.e_ready, b, 2 * lane + kt + 1)
                    if lane >= 2 and kt == 0:
                        await_(act, self.pv, b, lane - 1)
                    n = HG * (S - self.queries(kt))
                    nc.scalar.activation(self.probs_of(lane, kt).rearrange("p g q -> p (g q)"), wide[kt][:, 0:n],
                                         ACT.Exp).then_inc(self.e_done.sem, 1)

            def pe_values(self, pe, b, p, lane):
                await_(pe, self.e_done, b, 2 * lane + 2)
                if lane:
                    await_(pe, self.pv_out, b, lane)
                for kt in range(QT):
                    for g in range(HG):
                        last = nc.tensor.matmul(bank_pv[g * ROWS:(g + 1) * ROWS, self.queries(kt):S],
                                                v_aug[p][:, kt, g * HL + lane, :], self.probs_of(lane, kt)[:, g, :],
                                                start=(kt == 0), stop=(kt == QT - 1), tile_position=(0, g * ROWS),
                                                skip_group_check=True)
                last.then_inc(self.pv.sem, 1)

            def dve_values(self, dve, b, p, lane):
                await_(dve, self.pv, b, lane + 1)
                nc.vector.tensor_copy(o_lane[:, lane, :], bank_pv[:, 0:S]).then_inc(self.pv_out.sem, 1)

            def pe_turn_out(self, pe, b):
                await_(pe, self.pv_out, b)
                for qt in range(QT):
                    for lane in range(HL):
                        last = nc.tensor.transpose(self.out_banks[qt][:, lane * P:(lane + 1) * P], o_lane[:, lane, qt * P:(qt + 1) * P], ident)
                    last.then_inc(self.o_turned.sem, 1)

            def dve_divide(self, dve, b):
                for qt in range(QT):
                    await_(dve, self.o_turned, b, qt + 1)
                    o = self.out_banks[qt].rearrange("p (l g r) -> p l g r", l=HL, g=HG)
                    nc.vector.reciprocal(rsum[:, qt].rearrange("p (l g) -> p l g", l=HL), o[:, :, :, HD]).then_inc(self.o_rsum.sem, 1)
                for qt in range(QT):
                    await_(dve, self.o_rsum, b, qt + 1)
                    o = self.out_banks[qt].rearrange("p (l g r) -> p l g r", l=HL, g=HG)
                    nc.vector.tensor_tensor(o_tok[:, qt].rearrange("p (g l d) -> p l g d", g=HG, l=HL), o[:, :, :, 0:HD],
                                            rsum[:, qt].rearrange("p (l g) -> p l g", l=HL).unsqueeze(3).broadcast_to([P, HL, HG, HD]),
                                            ALU.mult).then_inc(self.o_norm.sem, 1)

            def pe_flip(self, pe, o, after, b, done):
                await_(pe, after, b)
                for qt in range(QT):
                    last = nc.tensor.transpose(o[:, qt * P:(qt + 1) * P], o_tok[:, qt, :], ident)
                last.then_inc(done.sem, 1)

        class Splines:

            def __init__(self, name, pctx, cols, buffers):
                def psb(n, shape):
                    return pctx.enter_context(nc.sbuf_tensor(f"{name}_{n}", shape, F32))
                self.near, self.far, self.near2, self.far2 = (psb(n, [P, cols]) for n in ("near", "far", "near2", "far2"))
                self.us = [psb(f"u{n}", [P, cols]) for n in range(2)]
                self.planes = [psb(f"planes{n}", [P, KP, cols]) for n in range(buffers)]
                self.folded = event(name + "_folded", 4)
                self.u_out = event(name + "_u_out", 4)
                self.clipped = event(name + "_clipped", 8)
                self.squared = event(name + "_squared", 8)
                self.cubed = event(name + "_cubed", 8)
                self.basis = event(name + "_basis", 4)
                self.masked = event(name + "_masked", 4)
                self.tanh_out = event(name + "_tanh_out")
                self.ready = event(name + "_ready")

            def credit(self, dve):
                dve.sem_inc(self.masked.sem, 2)
                dve.sem_inc(self.basis.sem, 1)
                dve.sem_inc(self.ready.sem, 1)

            def pe_wait(self, pe, b):
                pe.wait_ge(self.ready.sem, b + 2)

            def act_fold(self, act, b, k, x):
                act.wait_ge(self.masked.sem, 4 * b + k + 1)
                take_wait(act)
                nc.scalar.activation(self.us[k % 2][:].rearrange("p (s q) -> p s q", s=x.shape[1]), x, ACT.Abs,
                                     bias=abs_bias[:, k:k + 1], scale=1.0 / H_GRID).then_inc(self.folded.sem, 1)
                await_(act, self.folded, b, k + 1)
                nc.scalar.activation(self.us[k % 2][:], self.us[k % 2][:], ACT.Abs, bias=abs_bias[:, 4:5]).then_inc(self.u_out.sem, 1)

            def act_powers(self, act, b, k):
                await_(act, self.u_out, b, k + 1)
                act.wait_ge(self.basis.sem, 4 * b + k + 1)
                for n, dst in enumerate((self.far, self.near)):
                    nc.scalar.activation(dst[:], self.us[k % 2][:], ACT.Relu, bias=abs_bias[:, 5 + n:6 + n], scale=-1.0).then_inc(self.clipped.sem, 1)
                for n, (src, dst) in enumerate(((self.far, self.far2), (self.near, self.near2))):
                    await_(act, self.clipped, b, 2 * k + n + 1)
                    nc.scalar.activation(dst[:], src[:], ACT.Square).then_inc(self.squared.sem, 1)

            def act_tanh(self, act, b, x, q):
                act.wait_ge(self.ready.sem, b + 1)
                take_wait(act)
                nc.scalar.activation(self.planes[q][:, NB].rearrange("p (s q) -> p s q", s=x.shape[1]), x, ACT.Tanh, scale=0.5).then_inc(self.tanh_out.sem, 1)

            def dve_cube(self, dve, b, k):
                u = self.us[k % 2]
                await_(dve, self.squared, b, 2 * k + 1)
                nc.vector.tensor_tensor(self.far[:], self.far[:], self.far2[:], ALU.mult).then_inc(self.cubed.sem, 1)
                await_(dve, self.squared, b, 2 * k + 2)
                nc.vector.scalar_tensor_tensor(out=self.near[:], in0=self.near[:], scalar=4.0, in1=self.near2[:],
                                               op0=ALU.mult, op1=ALU.mult).then_inc(self.cubed.sem, 1)
                await_(dve, self.cubed, b, 2 * k + 2)
                nc.vector.tensor_tensor(u[:], self.far[:], self.near[:], ALU.subtract).then_inc(self.basis.sem, 1)

            def dve_mask(self, dve, b, k, x, q):
                s, u = x.shape[1], self.us[k % 2]
                dve.wait_ge(self.basis.sem, 4 * b + k + 2)
                for plane, side in ((k, ALU.is_lt), (k + 4, ALU.is_ge)):
                    last = nc.vector.scalar_tensor_tensor(out=self.planes[q][:, plane].rearrange("p (s q) -> p s q", s=s), in0=x,
                                                          scalar=H_GRID * (k - 1.5), in1=u[:].rearrange("p (s q) -> p s q", s=s),
                                                          op0=side, op1=ALU.mult)
                last.then_inc(self.masked.sem, 1)

            def dve_silu(self, dve, b, x, q):
                s = x.shape[1]
                await_(dve, self.tanh_out, b)
                nc.vector.scalar_tensor_tensor(out=self.planes[q][:, NB].rearrange("p (s q) -> p s q", s=s),
                                               in0=self.planes[q][:, NB].rearrange("p (s q) -> p s q", s=s),
                                               scalar=1.0, in1=x, op0=ALU.add, op1=ALU.mult).then_inc(self.ready.sem, 1)

            def act_all(self, act, b, x, q):
                self.act_fold(act, b, 0, x)
                for k in range(4):
                    if k < 3:
                        self.act_fold(act, b, k + 1, x)
                    self.act_powers(act, b, k)
                self.act_tanh(act, b, x, q)

            def dve_all(self, dve, b, x, q):
                for k in range(4):
                    self.dve_cube(dve, b, k)
                    self.dve_mask(dve, b, k, x, q)
                self.dve_silu(dve, b, x, q)

        kan = Splines("kan", ctx, cols=S, buffers=2)

        def kan_input(n):
            source, b = (1, 0) if isinstance(n, int) and n == 0 else (0, n - B)
            return xt[:, source:source + 1, bass.ds(b * S, S)]

        c_v_out = event("c_v_out")
        x2_out = event("x2_out")

        qk_kan = event("qk_kan")
        qk_products = [(x, c) for x in range(2) for c in range(KP)]
        PIECES = HL + 1

        def project_qk(pe, b, p, piece):
            if piece == 0:
                kan.pe_wait(pe, B + b)
            n = len(qk_products)
            for x, c in qk_products[piece * n // PIECES:(piece + 1) * n // PIECES]:
                last = nc.tensor.matmul(bank_ms[:, x * S:(x + 1) * S], kan_w[:, 0, c, x * D:(x + 1) * D], kan.planes[p][:, c],
                                        start=(c == 0), stop=(c == KP - 1), skip_group_check=True)
            if piece == PIECES - 1:
                last.then_inc(qk_kan.sem, 1)

        def self_attention(block):
            def lsb(name, shape, dt=F32):
                return ctx.enter_context(nc.sbuf_tensor(name, shape, dt))

            xn = lsb("xn", [P, QT, D])
            xnt = lsb("xnt", [P, S])
            v_centre = lsb("v_centre", [P, QT, D])
            v_extra = [lsb(f"v_extra{n}", [P, QT, D]) for n in range(2)]

            c_qk = event("c_qk")
            c_qk_out = event("c_qk_out")
            c_v = event("c_v")

            def splines_input(n, ahead):
                return xt[:, 1:2, bass.ds(n * S, S)] if ahead else kan_input(n)

            stats2 = lsb("stats2", [P, QT, 6])
            mv2 = lsb("mv2", [P, QT, 2])
            root2 = lsb("root2", [P, QT])
            rstd2 = lsb("rstd2", [P, QT])
            newton2 = lsb("newton2", [P, QT])
            xn2 = lsb("xn2", [P, QT, D])
            norm2 = event("norm2", 7)
            root2_out = event("root2_out")
            normed2 = event("normed2", QT)
            turned2 = event("turned2")

            att = Attention("self", causal=True, out_banks=[bank_pv[:], bank_ms[:]])
            vones = sem("vones")
            normed = event("normed", QT)
            turned = event("turned")
            turned_out = event("turned_out")
            projected = event("projected")
            qk_out = event("qk_out", 2)
            v_done = event("v_done")
            v_out = event("v_out")
            vc_out = event("vc_out")
            extra = event("extra")
            extra_out = event("extra_out")
            summed = event("summed")
            o_flipped = event("o_flipped")
            o_flipped_out = event("o_flipped_out")
            o_proj = event("o_proj")
            x_added = event("x_added")

            def self_batches(eng, body):
                body(0, 0, 0, 2)
                body(1, 1, 1, 2)
                with eng.Fori(1, (B - 2) // 2) as i:
                    for p in range(2):
                        body(2 * i + p, p, 2, 2)
                body(B - 2, 0, 2, 1)
                body(B - 1, 1, 2, 0)

            @block.gpsimd
            def _(pool):
                for p in range(2):
                    nc.gpsimd.memset(v_aug[p][:], 0.0).then_inc(vones, 1)
                pool.wait_ge(vones, 2)
                for p in range(2):
                    nc.gpsimd.memset(v_aug[p][:, :, :, HD:HD + 1], 1.0).then_inc(vones, 1)

            @block.sync
            def _(sp):
                att.dma_max(sp, 0, 0)

                def body(b, p, before, ahead):
                    if ahead >= 1:
                        att.dma_max(sp, b + 1, 1 - p)

                self_batches(sp, body)

            @block.scalar
            def _(act):
                def flip_out(b):
                    await_(act, o_flipped, b)
                    nc.scalar.activation(o_feat[:], bank_ms[:, 0:S], ACT.Copy).then_inc(o_flipped_out.sem, 1)

                def turn_out(b):
                    nc.scalar.activation(xnt[:], bank_ms[:, S:2 * S], ACT.Copy).then_inc(turned_out.sem, 1)

                def high(b):
                    await_(act, qk_out, b)
                    nc.scalar.activation(qk_hi[:].rearrange("p s q -> p (s q)"), qk[:].rearrange("p s q -> p (s q)"), ACT.Copy).then_inc(att.hi.sem, 1)

                def values(b, p):
                    await_(act, vc_out, b)
                    nc.scalar.activation(v_aug[p][:, :, :, 0:HD], bank_ms[:].rearrange("p (q c h d) -> p q c h d", q=QT, c=2, d=HD)[:, :, 0],
                                         ACT.Copy).then_inc(v_out.sem, 1)

                def prepare(b, p):
                    act.wait_ge(turned.sem, b + 2)
                    turn_out(b)
                    high(b)
                    act.wait_ge(vones, 4)
                    values(b, p)
                    att.act_stack(act, b, p)

                def square_root(b):
                    await_(act, norm2, b, 2)
                    nc.scalar.activation(root2[:], mv2[:, :, 1], ACT.Sqrt, bias=eps_col[:, 0:1]).then_inc(root2_out.sem, 1)

                def context_qk_out(b):
                    await_(act, c_qk, b)
                    take_wait(act)
                    nc.scalar.activation(ctx_qk[:, bass.ds(b, 1), :].rearrange("p b q -> p (b q)"), banks[5], ACT.Copy).then_inc(c_qk_out.sem, 1)

                def context_v_out(b):
                    await_(act, c_v, b)
                    take_wait(act)
                    nc.scalar.activation(xt[:, 1, bass.ds(b * S, S)], banks[5][:, 0:S], ACT.Copy).then_inc(c_v_out.sem, 1)

                prepare(0, 0)
                kan.act_fold(act, 0, 0, kan_input(0))
                for k in range(4):
                    if k < 3:
                        kan.act_fold(act, 0, k + 1, kan_input(0))
                    kan.act_powers(act, 0, k)
                    if k == 0:
                        act.wait_ge(turned.sem, 3)
                        turn_out(1)
                    elif k == 1:
                        high(1)
                    elif k == 2:
                        values(1, 1)
                        att.act_stack(act, 1, 1)
                att.act_split_max(act, 0)
                kan.act_tanh(act, 0, kan_input(0), 0)

                def body(b, p, before, ahead):
                    x = splines_input(b + 1, ahead)

                    def splines(k):
                        kan.act_powers(act, b + 1, k)
                        if k < 3:
                            kan.act_fold(act, b + 1, k + 1, x)

                    kan.act_fold(act, b + 1, 0, x)
                    att.act_exp(act, b, p, 0)
                    splines(0)
                    if before == 2:
                        square_root(b - 2)
                    att.act_exp(act, b, p, 1)
                    if ahead >= 2:
                        act.wait_ge(turned.sem, b + 4)
                    if before:
                        flip_out(b - 1)
                    if ahead >= 2:
                        turn_out(b + 2)
                    splines(1)
                    att.act_exp(act, b, p, 2)
                    if ahead >= 2:
                        high(b + 2)
                    context_qk_out(b)
                    splines(2)
                    att.act_exp(act, b, p, 3)
                    context_v_out(b)
                    if ahead >= 1:
                        att.act_split_max(act, b + 1)
                    if ahead >= 2:
                        await_(act, att.pv, b)
                        values(b + 2, p)
                    splines(3)
                    if ahead >= 2:
                        att.act_stack(act, b + 2, p)
                    kan.act_tanh(act, b + 1, x, 1 - p)

                self_batches(act, body)
                square_root(B - 2)
                flip_out(B - 1)
                kan.act_fold(act, B + 1, 0, kan_input(B + 1))
                for k in range(4):
                    kan.act_powers(act, B + 1, k)
                    if k < 3:
                        kan.act_fold(act, B + 1, k + 1, kan_input(B + 1))
                    if k == 0:
                        square_root(B - 1)
                kan.act_tanh(act, B + 1, kan_input(B + 1), 1)

            @block.tensor
            def _(pe):
                def flip(b):
                    att.pe_flip(pe, bank_ms, summed, b, o_flipped)

                def turn(b):
                    await_(pe, normed, b)
                    for qt in range(QT):
                        last = nc.tensor.transpose(bank_ms[:, S + qt * P:S + (qt + 1) * P], xn[:, qt, :], ident)
                    last.then_inc(turned.sem, 1)

                def project(b):
                    await_(pe, turned_out, b)
                    for s in range(2):
                        last = nc.tensor.matmul(bank_ms[:, s * S:(s + 1) * S], wqk[:, s * D:(s + 1) * D], xnt[:],
                                                start=True, stop=True)
                    last.then_inc(projected.sem, 1)

                def values(b):
                    await_(pe, qk_out, b)
                    for qt in range(QT):
                        last = nc.tensor.matmul(bank_ms[:, qt * 2 * D:(qt + 1) * 2 * D], xnt[:, qt * P:(qt + 1) * P],
                                                wv2[:].rearrange("p c d -> p (c d)"), start=True, stop=True)
                    last.then_inc(v_done.sem, 1)

                def extras(b):
                    await_(pe, vc_out, b)
                    for qt in range(QT):
                        o = bank[1][:, qt * D:(qt + 1) * D]
                        last = nc.tensor.matmul(o, xnt[:, qt * P:(qt + 1) * P], wvs[:], start=True, stop=False)
                        for kt in range(qt + 1):
                            last = nc.tensor.matmul(o, neg_uniform[:, kt, qt * P:(qt + 1) * P], v_centre[:, kt, :],
                                                    start=False, stop=(kt == qt))
                    last.then_inc(extra.sem, 1)

                def output(b):
                    await_(pe, o_flipped_out, b)
                    for qt in range(QT):
                        last = nc.tensor.matmul(bank_pv[:, S + qt * D:S + (qt + 1) * D], o_feat[:, qt * P:(qt + 1) * P], wproj[:],
                                                start=True, stop=True)
                    last.then_inc(o_proj.sem, 1)

                def prepare(b):
                    turn(b)
                    project(b)
                    values(b)
                    att.pe_stack(pe, b, 0)
                    att.pe_stack(pe, b, 1)
                    extras(b)

                def maxima(b, p, lane, pieces=slice(None)):
                    if lane == 0:
                        await_(pe, extra_out, b)
                        if not (isinstance(b, int) and b == 0):
                            await_(pe, att.m_lo, b - 1)
                    att.pe_max(pe, b, p, lane, pieces)

                c_products = [(x, c) for x in range(2) for c in range(KP)]

                def context_qk(b, p, piece):
                    if piece == 0:
                        kan.pe_wait(pe, b)
                    n = len(c_products) // 3
                    for x, c in c_products[piece * n:(piece + 1) * n]:
                        last = nc.tensor.matmul(banks[5][:, x * S:(x + 1) * S], kan_w[:, 1, c, x * D:(x + 1) * D], kan.planes[p][:, c],
                                                start=(c == 0), stop=(c == KP - 1), skip_group_check=True)
                    if piece == 2:
                        last.then_inc(c_qk.sem, 1)

                def context_v(b, p):
                    await_(pe, c_qk_out, b)
                    for qt in range(QT):
                        for c in range(KP):
                            last = nc.tensor.matmul(banks[5][:, qt * D:(qt + 1) * D], kan.planes[p][:, c, qt * P:(qt + 1) * P],
                                                    kan_w[:, 1, c, 2 * D:3 * D], start=(c == 0), stop=(c == KP - 1))
                    last.then_inc(c_v.sem, 1)

                def turn2(b, o=bank_pv):
                    await_(pe, normed2, b)
                    for qt in range(QT):
                        last = nc.tensor.transpose(o[:, S + qt * P:S + (qt + 1) * P], xn2[:, qt, :], ident)
                    last.then_inc(turned2.sem, 1)

                prepare(0)
                await_(pe, v_out, 0)
                turn(1)
                maxima(0, 0, 0)
                project(1)
                maxima(0, 0, 1)
                values(1)
                maxima(0, 0, 2)
                att.pe_stack(pe, 1, 0)
                att.pe_stack(pe, 1, 1)
                maxima(0, 0, 3)
                att.pe_turn_max(pe, 0, 0)
                extras(1)

                def body(b, p, before, ahead):
                    def scores(lane):
                        if lane == 0 and ahead >= 1:
                            await_(pe, att.q_ready, b + 1)
                        att.pe_scores(pe, b, p, lane, [0])
                        if lane == 0:
                            if ahead >= 1:
                                await_(pe, att.k_ready, b + 1)
                            att.pe_scores(pe, b, p, lane, [1])
                        if ahead >= 1:
                            maxima(b + 1, 1 - p, lane, slice(0, 2))
                        if lane:
                            att.pe_scores(pe, b, p, lane, [1])
                        if ahead >= 1:
                            att.pe_max(pe, b + 1, 1 - p, lane, slice(2, 3))

                    scores(0)
                    if before:
                        await_(pe, c_v_out, b - 1)
                    context_qk(b, p, 0)
                    scores(1)
                    context_qk(b, p, 1)
                    if before:
                        flip(b - 1)
                    elif ahead >= 2:
                        await_(pe, v_out, b + 1)
                    if ahead >= 2:
                        turn(b + 2)
                    if before == 2:
                        turn2(b - 2)
                    att.pe_values(pe, b, p, 0)
                    scores(2)
                    if ahead >= 2:
                        project(b + 2)
                    context_qk(b, p, 2)
                    if before:
                        await_(pe, att.pv_out, b, 1)
                        if before == 2:
                            await_(pe, x2_out, b - 2)
                        output(b - 1)
                    att.pe_values(pe, b, p, 1)
                    scores(3)
                    if ahead >= 2:
                        values(b + 2)
                    context_v(b, p)
                    if before:
                        await_(pe, x_added, b - 1)
                    att.pe_values(pe, b, p, 2)
                    if ahead >= 1:
                        att.pe_turn_max(pe, b + 1, 1 - p)
                    att.pe_values(pe, b, p, 3)
                    if ahead >= 2:
                        att.pe_stack(pe, b + 2, 0)
                        await_(pe, c_v_out, b)
                        att.pe_stack(pe, b + 2, 1)
                        await_(pe, v_out, b + 2)
                    att.pe_turn_out(pe, b)
                    if ahead >= 2:
                        extras(b + 2)

                self_batches(pe, body)
                flip(B - 1)
                turn2(B - 2, bank[1])
                output(B - 1)
                for piece in range(PIECES):
                    project_qk(pe, 0, 0, piece)
                await_(pe, x2_out, B - 2)
                turn2(B - 1, bank[1])

            @block.vector
            def _(dve):
                def normalise(b):
                    dve.wait_ge(turned.sem, b + 1)
                    for qt in range(QT):
                        n = b * QT + qt
                        nc.vector.tensor_scalar(xn[:, qt, :], xres[:, bass.ds(n, 1), :].rearrange("p a d -> p (a d)"),
                                                mv[:, bass.ds(n, 1), 0:1].rearrange("p a c -> p (a c)"),
                                                rstd[:, bass.ds(n, 1)], ALU.subtract, ALU.mult).then_inc(normed.sem, 1)

                def projected_out(b):
                    await_(dve, projected, b)
                    nc.vector.tensor_scalar(qk[:, 0], bank_ms[:, 0:S], qk_bias[:, 0:1], SCALE, ALU.add, ALU.mult).then_inc(qk_out.sem, 1)
                    nc.vector.tensor_scalar(qk[:, 1], bank_ms[:, S:2 * S], qk_bias[:, 1:2], None, ALU.add).then_inc(qk_out.sem, 1)

                def low(b):
                    await_(dve, att.hi, b)
                    nc.vector.tensor_tensor(qk_lo[:], qk[:], qk_hi[:].bitcast(F32), ALU.subtract).then_inc(att.lo.sem, 1)

                def centre_out(b):
                    await_(dve, v_done, b)
                    nc.vector.tensor_copy(v_centre[:], bank_ms[:].rearrange("p (q c d) -> p q c d", q=QT, c=2)[:, :, 1]).then_inc(vc_out.sem, 1)

                def extras_out(b, p):
                    await_(dve, extra, b)
                    nc.vector.tensor_copy(v_extra[p][:].rearrange("p q d -> p (q d)"), bank[1][:, 0:QT * D]).then_inc(extra_out.sem, 1)

                def residual(b):
                    await_(dve, o_proj, b)
                    xb = xres[:, bass.ds(b * QT, QT), :]
                    nc.vector.tensor_tensor(xb, xb, bank_pv[:, S:S + QT * D].rearrange("p (q d) -> p q d", q=QT),
                                            ALU.add).then_inc(x_added.sem, 1)

                def moments(b, step):
                    if step == 0:
                        await_(dve, x_added, b)
                        take_wait(dve)
                        for qt in range(QT):
                            last = nc.vector.bn_stats(stats2[:, qt, :], xres[:, bass.ds(b * QT + qt, 1), :].rearrange("p a d -> p (a d)"))
                    else:
                        await_(dve, norm2, b, 1)
                        take_wait(dve)
                        for qt in range(QT):
                            last = nc.vector.bn_aggr(mv2[:, qt, :], stats2[:, qt, :])
                    last.then_inc(norm2.sem, 1)

                def normalise2(b):
                    await_(dve, root2_out, b)
                    nc.vector.reciprocal(rstd2[:], root2[:]).then_inc(norm2.sem, 1)
                    await_(dve, norm2, b, 3)
                    nc.vector.tensor_tensor(newton2[:], rstd2[:], rstd2[:], ALU.mult).then_inc(norm2.sem, 1)
                    await_(dve, norm2, b, 4)
                    nc.vector.scalar_tensor_tensor(out=newton2[:], in0=mv2[:, :, 1], scalar=EPS, in1=newton2[:],
                                                   op0=ALU.add, op1=ALU.mult).then_inc(norm2.sem, 1)
                    await_(dve, norm2, b, 5)
                    nc.vector.tensor_scalar(newton2[:], newton2[:], -0.5, 1.5, ALU.mult, ALU.add).then_inc(norm2.sem, 1)
                    await_(dve, norm2, b, 6)
                    nc.vector.tensor_tensor(rstd2[:], rstd2[:], newton2[:], ALU.mult).then_inc(norm2.sem, 1)
                    await_(dve, norm2, b, 7)
                    for qt in range(QT):
                        nc.vector.tensor_scalar(xn2[:, qt, :], xres[:, bass.ds(b * QT + qt, 1), :].rearrange("p a d -> p (a d)"),
                                                mv2[:, qt, 0:1], rstd2[:, qt:qt + 1], ALU.subtract, ALU.mult).then_inc(normed2.sem, 1)

                def turned2_out(b, o=bank_pv):
                    await_(dve, turned2, b)
                    nc.vector.tensor_copy(xt[:, 0, bass.ds(b * S, S)], o[:, S:2 * S]).then_inc(x2_out.sem, 1)

                def prepare(b, p):
                    normalise(b)
                    projected_out(b)
                    low(b)
                    centre_out(b)
                    att.dve_stack(dve, b, p)
                    extras_out(b, p)

                dve.sem_inc(turned.sem, 1)
                kan.credit(dve)
                prepare(0, 0)
                normalise(1)
                for lane in range(HL):
                    att.dve_max(dve, 0, 0, lane)
                    if lane == 1:
                        projected_out(1)
                    elif lane == 2:
                        low(1)
                        centre_out(1)
                    kan.dve_cube(dve, 0, lane)
                    kan.dve_mask(dve, 0, lane, kan_input(0), 0)
                    if lane == 2:
                        att.dve_stack(dve, 1, 1)
                att.dve_split_max(dve, 0)
                extras_out(1, 1)
                kan.dve_silu(dve, 0, kan_input(0), 0)

                def body(b, p, before, ahead):
                    x = splines_input(b + 1, ahead)

                    def splines(k):
                        kan.dve_cube(dve, b + 1, k)
                        kan.dve_mask(dve, b + 1, k, x, 1 - p)

                    if ahead >= 2:
                        normalise(b + 2)
                    if ahead >= 1:
                        att.dve_max(dve, b + 1, 1 - p, 0)
                        att.dve_max(dve, b + 1, 1 - p, 1)
                    if before == 2:
                        normalise2(b - 2)
                    splines(0)
                    att.dve_values(dve, b, p, 0)
                    if before == 2:
                        turned2_out(b - 2)
                    if ahead >= 1:
                        att.dve_max(dve, b + 1, 1 - p, 2)
                    if ahead >= 2:
                        projected_out(b + 2)
                    att.dve_values(dve, b, p, 1)
                    if before:
                        residual(b - 1)
                    if ahead >= 1:
                        att.dve_max(dve, b + 1, 1 - p, 3)
                    if before:
                        moments(b - 1, 0)
                    splines(1)
                    if before:
                        moments(b - 1, 1)
                    if ahead >= 2:
                        low(b + 2)
                        centre_out(b + 2)
                    splines(2)
                    att.dve_values(dve, b, p, 2)
                    if ahead >= 1:
                        att.dve_split_max(dve, b + 1)
                    att.dve_values(dve, b, p, 3)
                    splines(3)
                    if ahead >= 2:
                        att.dve_stack(dve, b + 2, p)
                    att.dve_divide(dve, b)
                    await_(dve, att.o_norm, b)
                    await_(dve, extra_out, b)
                    nc.vector.tensor_tensor(o_tok[:], o_tok[:], v_extra[p][:], ALU.add).then_inc(summed.sem, 1)
                    if ahead >= 2:
                        await_(dve, summed, b)
                        extras_out(b + 2, p)
                    kan.dve_silu(dve, b + 1, x, 1 - p)

                self_batches(dve, body)
                normalise2(B - 2)
                turned2_out(B - 2, bank[1])
                residual(B - 1)
                moments(B - 1, 0)
                moments(B - 1, 1)
                for k in range(4):
                    kan.dve_cube(dve, B + 1, k)
                    kan.dve_mask(dve, B + 1, k, kan_input(B + 1), 1)
                    if k == 1:
                        normalise2(B - 1)
                    if k == 2:
                        turned2_out(B - 1, bank[1])
                kan.dve_silu(dve, B + 1, kan_input(B + 1), 1)

        def cross_attention_and_swiglu(block):
            kano = Splines("kano", ctx, cols=S, buffers=1)
            ko_done = event("ko_done")
            ko_added = event("ko_added")
            rope_sin = ctx.enter_context(nc.sbuf_tensor("rope_sin", [P, 2, S], F32))

            att = Attention("cross", causal=False, out_banks=banks[2:4])
            v_kan = event("v_kan", QT)
            v_kan_out = event("v_kan_out", QT)
            qk_kan_out = event("qk_kan_out")
            rotated = event("rotated")
            roped = event("roped", 3)
            c_flipped = event("c_flipped")
            c_flipped_out = event("c_flipped_out")

            def kano_input(b):
                return xt_room[:, bass.ds(b * S, S)].unsqueeze(1)

            flat = "p s q -> p (s q)"

            def cross_batches(eng, body):
                n = (B - 4) // 2
                with eng.Fori(0, n) as i:
                    for p in range(2):
                        body(2 * i + p, p, 4)
                for b in range(2 * n, B):
                    body(b, b % 2, B - 1 - b)

            CH = 2 * S
            CT = CH // P
            NCH = TILES // CT
            norm3 = [Norm("norm3a", 0, TILES - CT), Norm("norm3b", TILES - CT, TILES)]
            normed3 = sem("normed3")
            turned3 = sem("turned3")
            x3_out = sem("x3_out")
            gate_up = event("gate_up", 2 * FT)
            silu_out = event("silu_out", FT)
            h_out = event("h_out", FT)
            down = event("down")
            y_out = event("y_out")
            stored = event("stored", 1, 16)
            xn3 = [a.rearrange("p s (n d) -> p (s n) d", d=D) for a in (rope_sin[:], qk[:])]
            h = [a[:, 0:FT * CH].rearrange("p (f q) -> p f q", f=FT) for a in probs]
            turned3_bank = [bank[0], bank[1], bank_pv, bank_pv]
            gate_bank, up_bank = [banks[2], banks[4], banks[0]], [banks[3], banks[5], banks[1]]

            def ffn_input(c):
                return xt[:, 0, c * CH:(c + 1) * CH]

            @block.sync
            def _(sp):
                att.dma_max(sp, 0, 0)

                def body(b, p, ahead):
                    if ahead >= 1:
                        att.dma_max(sp, b + 1, 1 - p)

                cross_batches(sp, body)
                for c in range(NCH):
                    await_(sp, y_out, c)
                    sp.dma_start(out.rearrange("b (t p) d -> p (b t) d", p=P)[:, c * CT:(c + 1) * CT, :],
                                 xres[:, c * CT:(c + 1) * CT, :]).then_inc(stored.sem, 16)
                await_(sp, stored, NCH - 1)

            @block.scalar
            def _(act):
                def high(b):
                    await_(act, roped, b)
                    nc.scalar.activation(qk_hi[:].rearrange(flat), qk[:].rearrange(flat), ACT.Copy).then_inc(att.hi.sem, 1)

                def kano_start(b):
                    kano.act_fold(act, b, 0, kano_input(b))
                    kano.act_fold(act, b, 1, kano_input(b))
                    kano.act_powers(act, b, 0)

                def project(b, p):
                    high(b)
                    att.act_stack(act, b, p)

                def turned3_out(c):
                    act.wait_ge(turned3, c + 1)
                    nc.scalar.activation(ffn_input(c), turned3_bank[c][:], ACT.Copy).then_inc(x3_out, 1)

                def gate(c):
                    for f in range(FT):
                        await_(act, gate_up, c, 2 * f + 1)
                        if c >= 2:
                            await_(act, down, c - 2)
                        nc.scalar.activation(h[c % 2][:, f, :], gate_bank[f], ACT.Silu).then_inc(silu_out.sem, 1)

                nc.scalar.activation(xt_room[:, 0:S], xt_room[:, S:2 * S], ACT.Copy, scale=0.0).then_inc(c_flipped_out.sem, 1)
                project(0, 0)
                kan.act_all(act, B + 2, kan_input(B + 2), 0)
                att.act_split_max(act, 0)
                project(1, 1)
                act.wait_ge(c_flipped_out.sem, 1)
                kano_start(0)
                kan.act_fold(act, B + 3, 0, kan_input(B + 3))

                def body(b, p, ahead):
                    for lane in range(HL):
                        att.act_exp(act, b, p, lane)
                        if lane == HL - 1 and ahead >= 1:
                            att.act_split_max(act, b + 1)
                        if lane < 3:
                            kano.act_powers(act, b, lane + 1)
                        if ahead >= 3:
                            kan.act_powers(act, B + b + 3, lane)
                            if lane + 1 < HL:
                                kan.act_fold(act, B + b + 3, lane + 1, kan_input(B + b + 3))
                        if lane < 2:
                            kano.act_fold(act, b, lane + 2, kano_input(b))
                    act.wait_ge(ko_added.sem, b + 1)
                    kano.act_tanh(act, b, kano_input(b), 0)
                    if ahead >= 3:
                        kan.act_tanh(act, B + b + 3, kan_input(B + b + 3), 1 - p)
                    if ahead >= 2:
                        high(b + 2)
                    if ahead == 0:
                        norm3[0].square_root(act)
                        turned3_out(0)
                    await_(act, c_flipped, b)
                    take_wait(act)
                    nc.scalar.activation(xt[:, 0, bass.ds(b * S, S)], bank_ms[:, 0:S], ACT.Copy).then_inc(c_flipped_out.sem, 1)
                    if ahead >= 2:
                        att.act_stack(act, b + 2, p)
                    if ahead == 0:
                        turned3_out(1)
                    act.wait_ge(c_flipped_out.sem, b + 2)
                    kano_start(b + 1)
                    if ahead >= 4:
                        kan.act_fold(act, B + b + 4, 0, kan_input(B + b + 4))

                cross_batches(act, body)
                kano.act_powers(act, B, 1)
                kano.act_fold(act, B, 2, kano_input(B))
                turned3_out(2)
                gate(0)
                kano.act_powers(act, B, 2)
                kano.act_fold(act, B, 3, kano_input(B))
                kano.act_powers(act, B, 3)
                await_(act, ko_added, B)
                kano.act_tanh(act, B, kano_input(B), 0)
                gate(1)
                gate(2)
                norm3[1].square_root(act)
                turned3_out(3)
                gate(3)

            @block.tensor
            def _(pe):
                def values(b, p, qt):
                    for c in range(KP):
                        last = nc.tensor.matmul(banks[4 + qt][:, 0:D], kan.planes[p][:, c, qt * P:(qt + 1) * P], kan_w[:, 0, c, 2 * D:3 * D],
                                                start=(c == 0), stop=(c == KP - 1))
                    last.then_inc(v_kan.sem, 1)

                def turn3(c):
                    if c >= 2:
                        await_(pe, ko_added, B - 1 if c == 2 else B + 1)
                    pe.wait_ge(normed3, (c + 1) * CT)
                    for n in range(CT):
                        last = nc.tensor.transpose(turned3_bank[c][:, n * P:(n + 1) * P], xn3[c % 2][:, n, :], ident)
                    last.then_inc(turned3, 1)

                def gate_and_up(c):
                    pe.wait_ge(x3_out, c + 1)
                    for f in range(FT):
                        if c:
                            await_(pe, h_out, c - 1, f + 1)
                        elif f == FT - 1:
                            turn3(2)
                            pe.wait_ge(x3_out, 2)
                        nc.tensor.matmul(gate_bank[f], w_gate[:, f * P:(f + 1) * P], ffn_input(c), start=True, stop=True).then_inc(gate_up.sem, 1)
                        nc.tensor.matmul(up_bank[f], w_up[:, f * P:(f + 1) * P], ffn_input(c), start=True, stop=True).then_inc(gate_up.sem, 1)

                def project_down(c):
                    await_(pe, h_out, c)
                    if c:
                        await_(pe, y_out, c - 1)
                    for n in range(CT):
                        for f in range(FT):
                            last = nc.tensor.matmul(bank_ms[:, n * P:(n + 1) * P], h[c % 2][:, f, n * P:(n + 1) * P], w_down[:, f, :],
                                                    start=(f == 0), stop=(f == FT - 1))
                    last.then_inc(down.sem, 1)

                def output(b):
                    kano.pe_wait(pe, b)
                    for n in range(QT):
                        for k in range(KP):
                            last = nc.tensor.matmul(bank_pv[:, n * P:(n + 1) * P], kano.planes[0][:, k, n * P:(n + 1) * P], kan_wo[:, k, :],
                                                    start=(k == 0), stop=(k == KP - 1))
                    last.then_inc(ko_done.sem, 1)

                def rotate(b):
                    if isinstance(b, int) and b == 0:
                        await_(pe, x2_out, B - 1)
                    await_(pe, qk_kan_out, b)
                    nc.tensor.matmul(bank[1][:], cst("rope_rot"), qk[:].rearrange(flat), start=True, stop=True).then_inc(rotated.sem, 1)

                def stacks(b):
                    att.pe_stack(pe, b, 0)
                    await_(pe, v_kan_out, b)
                    att.pe_stack(pe, b, 1)

                def prologue(b, p):
                    values(b, p, 0)
                    rotate(b)
                    values(b, p, 1)
                    stacks(b)

                def maxima(b, p, lane, pieces=slice(None)):
                    if lane == 0 and not (isinstance(b, int) and b == 0):
                        await_(pe, att.m_lo, b - 1)
                    att.pe_max(pe, b, p, lane, pieces)

                await_(pe, c_v_out, B - 1)
                prologue(0, 0)
                for lane in range(HL):
                    maxima(0, 0, lane)
                    project_qk(pe, 1, 1, lane)
                att.pe_turn_max(pe, 0, 0)
                project_qk(pe, 1, 1, HL)
                prologue(1, 1)

                def body(b, p, ahead):
                    def scores(lane):
                        if lane == 0 and ahead >= 1:
                            await_(pe, att.q_ready, b + 1)
                        if lane == 0:
                            att.pe_scores(pe, b, p, lane, [0])
                        if ahead >= 1:
                            maxima(b + 1, 1 - p, lane, slice(0, 2))
                        if lane > 0:
                            att.pe_scores(pe, b, p, lane, [0])
                        att.pe_scores(pe, b, p, lane, [1])
                        if ahead >= 1:
                            att.pe_max(pe, b + 1, 1 - p, lane, slice(2, 4))

                    scores(0)
                    pe.wait_ge(c_flipped_out.sem, b + 1)
                    if ahead >= 2:
                        project_qk(pe, b + 2, p, 0)
                    for lane in range(HL):
                        if lane + 1 < HL:
                            scores(lane + 1)
                        elif ahead >= 1:
                            att.pe_turn_max(pe, b + 1, 1 - p)
                        if ahead >= 2:
                            project_qk(pe, b + 2, p, lane + 1)
                        if lane == 0:
                            pe.wait_ge(ko_added.sem, b + 1)
                        att.pe_values(pe, b, p, lane)
                    if ahead >= 2:
                        values(b + 2, p, 0)
                        rotate(b + 2)
                    att.pe_turn_out(pe, b)
                    if ahead == 0:
                        turn3(0)
                    if ahead >= 2:
                        values(b + 2, p, 1)
                    att.pe_flip(pe, bank_ms, att.o_norm, b, c_flipped)
                    if ahead >= 2:
                        stacks(b + 2)
                    if ahead == 0:
                        turn3(1)
                    output(b)

                cross_batches(pe, body)
                gate_and_up(0)
                gate_and_up(1)
                await_(pe, c_flipped_out, B)
                project_down(0)
                pe.wait_ge(x3_out, 3)
                output(B)
                gate_and_up(2)
                project_down(1)
                project_down(2)
                turn3(3)
                gate_and_up(3)
                project_down(3)

            @block.vector
            def _(dve):
                def projected_out(b):
                    await_(dve, qk_kan, b)
                    nc.vector.tensor_tensor(qk[:].rearrange(flat), bank_ms[:], ctx_qk[:, bass.ds(b, 1), :].rearrange("p b q -> p (b q)"),
                                            ALU.add).then_inc(qk_kan_out.sem, 1)

                def value_out(b, p, qt):
                    await_(dve, v_kan, b, qt + 1)
                    nc.vector.tensor_tensor(v_aug[p][:, qt, :, 0:HD], banks[4 + qt][:, 0:D].rearrange("p (h d) -> p h d", d=HD),
                                            xt[:, 1, bass.ds(b * S + qt * P, P)].rearrange("p (h d) -> p h d", d=HD),
                                            ALU.add).then_inc(v_kan_out.sem, 1)

                def rope(b):
                    await_(dve, qk_kan_out, b)
                    await_(dve, rotated, b)
                    nc.vector.tensor_tensor(rope_sin[:].rearrange(flat), bank[1][:], sinv, ALU.mult).then_inc(roped.sem, 1)
                    nc.vector.tensor_tensor(qk[:].rearrange(flat), qk[:].rearrange(flat), cosv, ALU.mult).then_inc(roped.sem, 1)
                    await_(dve, roped, b, 2)
                    nc.vector.tensor_tensor(qk[:], qk[:], rope_sin[:], ALU.add).then_inc(roped.sem, 1)

                def low(b):
                    await_(dve, att.hi, b)
                    nc.vector.tensor_tensor(qk_lo[:], qk[:], qk_hi[:].bitcast(F32), ALU.subtract).then_inc(att.lo.sem, 1)

                def project(b, p):
                    projected_out(b)
                    value_out(b, p, 0)
                    rope(b)
                    low(b)
                    value_out(b, p, 1)
                    att.dve_stack(dve, b, p)

                def add_output(b):
                    await_(dve, ko_done, b)
                    xb = xres_room[:, bass.ds(b * QT, QT), :]
                    nc.vector.tensor_tensor(xb, xb, bank_pv[:, 0:QT * P].rearrange("p (q d) -> p q d", q=QT), ALU.add).then_inc(ko_added.sem, 1)

                def normalise3(c):
                    dve.wait_ge(norm3[c == NCH - 1].done, 7)
                    if c >= 2:
                        dve.wait_ge(turned3, c - 1)
                    for n in range(CT):
                        t = c * CT + n
                        nc.vector.tensor_scalar(xn3[c % 2][:, n, :], xres[:, t, :], mv[:, t, 0:1], rstd[:, t:t + 1],
                                                ALU.subtract, ALU.mult).then_inc(normed3, 1)

                def gated(c):
                    for f in range(FT):
                        await_(dve, silu_out, c, f + 1)
                        await_(dve, gate_up, c, 2 * f + 2)
                        nc.vector.tensor_tensor(h[c % 2][:, f, :], h[c % 2][:, f, :], up_bank[f], ALU.mult).then_inc(h_out.sem, 1)

                def add_down(c):
                    await_(dve, down, c)
                    xc = xres[:, c * CT:(c + 1) * CT, :]
                    nc.vector.tensor_tensor(xc, xc, bank_ms[:].rearrange("p (n d) -> p n d", n=CT), ALU.add).then_inc(y_out.sem, 1)

                kano.credit(dve)
                dve.sem_inc(ko_added.sem, 1)
                nc.vector.memset(xres_room[:, 0:QT], 0.0)
                project(0, 0)
                for lane in range(HL):
                    att.dve_max(dve, 0, 0, lane)
                    kan.dve_cube(dve, B + 2, lane)
                    kan.dve_mask(dve, B + 2, lane, kan_input(B + 2), 0)
                att.dve_split_max(dve, 0)
                kan.dve_silu(dve, B + 2, kan_input(B + 2), 0)
                project(1, 1)
                kano.dve_cube(dve, 0, 0)

                def body(b, p, ahead):
                    if ahead >= 1:
                        att.dve_max(dve, b + 1, 1 - p, 0)
                    for lane in range(HL):
                        if ahead >= 1 and lane + 1 < HL:
                            att.dve_max(dve, b + 1, 1 - p, lane + 1, slice(0, 2))
                        if lane == HL - 1 and ahead >= 2:
                            projected_out(b + 2)
                        kano.dve_mask(dve, b, lane, kano_input(b), 0)
                        if lane == HL - 1 and ahead >= 1:
                            att.dve_split_max(dve, b + 1)
                        if ahead >= 1 and lane + 1 < HL:
                            att.dve_max(dve, b + 1, 1 - p, lane + 1, slice(2, 4))
                        if lane < 3:
                            kano.dve_cube(dve, b, lane + 1)
                        if ahead >= 3:
                            kan.dve_cube(dve, B + b + 3, lane)
                            kan.dve_mask(dve, B + b + 3, lane, kan_input(B + b + 3), 1 - p)
                        att.dve_values(dve, b, p, lane)
                    kano.dve_silu(dve, b, kano_input(b), 0)
                    if ahead == 0:
                        norm3[0].reciprocal_root(dve)
                        normalise3(0)
                    if ahead >= 2:
                        value_out(b + 2, p, 0)
                        rope(b + 2)
                    att.dve_divide(dve, b)
                    if ahead >= 3:
                        kan.dve_silu(dve, B + b + 3, kan_input(B + b + 3), 1 - p)
                    if ahead >= 2:
                        low(b + 2)
                        value_out(b + 2, p, 1)
                        att.dve_stack(dve, b + 2, p)
                    if ahead == 0:
                        normalise3(1)
                    kano.dve_cube(dve, b + 1, 0)
                    add_output(b)
                    if ahead == 1:
                        await_(dve, ko_added, b + 1)
                        norm3[0].moments(dve)

                cross_batches(dve, body)
                def kano_steps(*ks):
                    for k in ks:
                        if k:
                            kano.dve_cube(dve, B, k)
                        kano.dve_mask(dve, B, k, kano_input(B), 0)

                normalise3(2)
                kano_steps(0, 1)
                gated(0)
                kano_steps(2, 3)
                kano.dve_silu(dve, B, kano_input(B), 0)
                add_down(0)
                gated(1)
                add_output(B)
                await_(dve, ko_added, B + 1)
                norm3[1].moments(dve)
                gated(2)
                add_down(1)
                norm3[1].reciprocal_root(dve)
                normalise3(3)
                add_down(2)
                gated(3)
                add_down(3)

        with nc.Block() as block:
            self_attention(block)
            cross_attention_and_swiglu(block)


def kernel(**inputs):
    import concourse.bacc as bacc
    from concourse.bass_utils import run_bass_kernel_spmd

    nc = bacc.Bacc("TRN2", target_bir_lowering=False, num_devices=1)
    arrays = {n: np.ascontiguousarray(a) for n, a in inputs.items()}
    arrays |= {"const": CONST, "const_staged": CONST_STAGED}
    aps = {n: nc.dram_tensor(f"in_{n}_dram", a.shape, mybir.dt.from_np(a.dtype), kind="ExternalInput").ap()
           for n, a in arrays.items()}
    out = nc.dram_tensor("out_dram", (B, S, D), F32, kind="ExternalOutput").ap()
    build(nc, aps, out)
    r = run_bass_kernel_spmd(nc, [{f"in_{n}_dram": a for n, a in arrays.items()}], core_ids=[0])
    return r.results[0]["out_dram"]
```
